# Optimizing a Trainium2 kernel written in Bass

```python
import numpy as np
import jax
import jax.numpy as jnp

def _softmax(x, axis=-1):
    return jax.nn.softmax(x, axis=axis)

def _gelu(x):
    return jax.nn.gelu(x, approximate=True)

def _silu(x):
    return jax.nn.silu(x)

def _sigmoid(x):
    return jax.nn.sigmoid(x)

def _layernorm(x, axis=-1, eps=1e-05):
    m = jnp.mean(x, axis=axis, keepdims=True)
    v = jnp.var(x, axis=axis, keepdims=True)
    return (x - m) / jnp.sqrt(v + eps)

def _scatter_add(tgt, idx, src, axis=0):
    return tgt.at[idx].add(src)

def _segment_sum(src, seg, n):
    return jax.ops.segment_sum(src, seg, n)
kernel_name = 'mk_flamingo_gated_d2_seqx_r8_ec441f'

def setup_inputs(seed: int=0):
    np.random.seed(seed)
    _w = jnp.asarray

    def _rec_inputs():
        import jax
        import jax.numpy as jnp
        _rk = jax.random.key(seed)
        x = -0.0002928 + 1 * jax.random.normal(jax.random.fold_in(_rk, 1), (128, 64, 128), jnp.float32)
        _lenS = 64 - jax.random.randint(jax.random.fold_in(_rk, 7), (128,), 0, max(1, 64 // 4) + 1, jnp.int32)
        _lenS2 = 64 - jax.random.randint(jax.random.fold_in(_rk, 8), (128,), 0, max(1, 64 // 4) + 1, jnp.int32)
        _ctx_1024P = jax.random.normal(jax.random.fold_in(_rk, 11), (128, 16, 128), jnp.float32)
        _ctx_1024c = jax.random.dirichlet(jax.random.fold_in(_rk, 511), 0.3 * jnp.ones((16,), jnp.float32), (128, 64))
        _ctx_1024t = jnp.einsum('bsk,bkd->bsd', _ctx_1024c, _ctx_1024P)
        _ctx_1024t = _ctx_1024t * jax.lax.rsqrt(jnp.mean(jnp.square(_ctx_1024t)) + 1e-12) * 0.953939
        ctx_1024 = -1.39393e-06 + 0.999914 * (_ctx_1024t + 0.3 * jax.random.normal(jax.random.fold_in(_rk, 611), (128, 64, 128), jnp.float32))
        _validS = jnp.arange(64)[None, :] < _lenS[:, None]
        _validS2 = jnp.arange(64)[None, :] < _lenS2[:, None]
        _causal = jnp.tril(jnp.ones((64, 64), dtype=bool))
        mask_BxS2_bf1 = jnp.ones((128, 64), dtype=bool)
        _g = jax.random.normal(jax.random.fold_in(_rk, 9001), (2, 2), jnp.float32)
        _g = jnp.sign(_g) * jnp.maximum(jnp.abs(_g), 1.0) + (_g == 0) * 1.0
        g_xattn = _g[0]
        g_ffn = _g[1]
        return (x, ctx_1024, mask_BxS2_bf1, g_xattn, g_ffn)
    x, ctx_1024, mask_BxS2_bf1, g_xattn, g_ffn = _rec_inputs()

    def _L0_xattn_setup():
        import jax, jax.numpy as jnp
        import numpy as np
        D_MODEL = 128
        N_HEADS = 16
        HEAD_DIM = D_MODEL // N_HEADS
        key = jax.random.key(seed)
        ks = jax.random.split(key, 9)
        B, S, D = (2, 256, D_MODEL)
        scale = 1.0 / np.sqrt(D)
        return {'q': jax.random.normal(ks[0], (B, S, D), jnp.float32), 'k': jax.random.normal(ks[1], (B, S, D), jnp.float32), 'v': jax.random.normal(ks[2], (B, S, D), jnp.float32), 'Wq': jax.random.normal(ks[3], (D, D), jnp.float32) * scale, 'bq': jax.random.normal(ks[4], (D,), jnp.float32) * 0.01, 'Wk': jax.random.normal(ks[5], (D, D), jnp.float32) * scale, 'bk': jax.random.normal(ks[6], (D,), jnp.float32) * 0.01, 'Wv': jax.random.normal(ks[7], (D, D), jnp.float32) * scale, 'bv': jax.random.normal(ks[8], (D,), jnp.float32) * 0.01}
    _L0_xattn_all = _L0_xattn_setup()
    _L0_xattn_in = {k: v for k, v in _L0_xattn_all.items() if k in ('Wq', 'bq', 'Wk', 'bk', 'Wv', 'bv')}
    del _L0_xattn_all

    def _L0_ffn_setup():
        import jax, jax.numpy as jnp
        import numpy as np
        B, S, D = (4, 128, 128)
        I = 64
        E = 32
        TOP_K = 8
        N_GROUP = 8
        TOPK_GROUP = 4

        def _group_topk(scores):
            T = scores.shape[0]
            epg = E // N_GROUP
            group_scores = scores.reshape(T, N_GROUP, epg).sum(axis=-1)
            _, top_groups = jax.lax.top_k(group_scores, TOPK_GROUP)
            group_mask = jnp.zeros((T, N_GROUP), scores.dtype).at[jnp.arange(T)[:, None], top_groups].set(1.0)
            expert_mask = jnp.repeat(group_mask, epg, axis=1)
            masked_scores = scores * expert_mask
            topk_w, topk_i = jax.lax.top_k(masked_scores, TOP_K)
            return (topk_w, topk_i)

        def _reference_tuple_inner(hidden_states, gate_w, expert_gate, expert_up, expert_down, shared_gate_w, shared_up_w, shared_down_w):
            b, s, d = hidden_states.shape
            flat = hidden_states.reshape(-1, d)
            T = flat.shape[0]
            logits = flat @ gate_w.T
            scores = jax.nn.sigmoid(logits)
            topk_w, topk_i = _group_topk(scores)
            topk_w = topk_w / jnp.clip(topk_w.sum(axis=-1, keepdims=True), 1e-12)
            combine = jnp.zeros((T, E), flat.dtype).at[jnp.arange(T)[:, None], topk_i].add(topk_w)

            def body(acc, expert):
                wg, wu, wd, w = expert
                h = jax.nn.silu(flat @ wg.T) * (flat @ wu.T)
                return (acc + w[:, None] * (h @ wd.T), None)
            out, _ = jax.lax.scan(body, jnp.zeros_like(flat), (expert_gate, expert_up, expert_down, combine.T))
            shared = jax.nn.silu(flat @ shared_gate_w.T) * (flat @ shared_up_w.T) @ shared_down_w.T
            out = out + shared
            return (out.reshape(b, s, d), logits)
        key = jax.random.key(seed)
        ks = jax.random.split(key, 8)
        scale = 0.02
        return {'hidden_states': jax.random.normal(ks[0], (B, S, D), jnp.float32), 'gate_w': jax.random.normal(ks[1], (E, D), jnp.float32) * scale, 'expert_gate': jax.random.normal(ks[2], (E, I, D), jnp.float32) * scale, 'expert_up': jax.random.normal(ks[3], (E, I, D), jnp.float32) * scale, 'expert_down': jax.random.normal(ks[4], (E, D, I), jnp.float32) * scale, 'shared_gate_w': jax.random.normal(ks[5], (I, D), jnp.float32) * scale, 'shared_up_w': jax.random.normal(ks[6], (I, D), jnp.float32) * scale, 'shared_down_w': jax.random.normal(ks[7], (D, I), jnp.float32) * scale}
    _L0_ffn_all = _L0_ffn_setup()
    _L0_ffn_in = {k: v for k, v in _L0_ffn_all.items() if k in ('gate_w', 'expert_gate', 'expert_up', 'expert_down', 'shared_gate_w', 'shared_up_w', 'shared_down_w')}
    del _L0_ffn_all

    def _L1_xattn_setup():
        import jax, jax.numpy as jnp
        import numpy as np
        HEADS = 16
        DIM_HEAD = 64
        SCALE = DIM_HEAD ** (-0.5)
        key = jax.random.key(seed)
        ks = jax.random.split(key, 6)
        B, Nq, Nkv, D = (4, 256, 128, 128)
        inner = HEADS * DIM_HEAD
        return {'x': jax.random.normal(ks[0], (B, Nq, D), dtype=jnp.float32), 'context': jax.random.normal(ks[1], (B, Nkv, D), dtype=jnp.float32), 'mask': jnp.ones((B, Nkv), dtype=bool), 'Wq': jax.random.normal(ks[2], (inner, D), dtype=jnp.float32) * D ** (-0.5), 'Wkv': jax.random.normal(ks[3], (2 * inner, D), dtype=jnp.float32) * D ** (-0.5), 'Wout': jax.random.normal(ks[4], (D, inner), dtype=jnp.float32) * inner ** (-0.5), 'b_out': jnp.zeros((D,), dtype=jnp.float32)}
    _L1_xattn_all = _L1_xattn_setup()
    _L1_xattn_in = {k: v for k, v in _L1_xattn_all.items() if k in ('Wq', 'Wkv', 'Wout', 'b_out')}
    del _L1_xattn_all

    def _L1_ffn_setup():
        import jax, jax.numpy as jnp
        import numpy as np
        TOP_K = 2
        key = jax.random.key(seed)
        ks = jax.random.split(key, 6)
        B, T, H, E, F = (2, 256, 128, 8, 512)
        s = 0.02
        return {'hidden_states': jax.random.normal(ks[0], (B, T, H), dtype=jnp.float32), 'router_w': jax.random.normal(ks[1], (E, H), dtype=jnp.float32) * s, 'w1': jax.random.normal(ks[2], (E, F, H), dtype=jnp.float32) * s, 'b1': jax.random.normal(ks[3], (E, F), dtype=jnp.float32) * s, 'w2': jax.random.normal(ks[4], (E, H, F), dtype=jnp.float32) * s, 'b2': jax.random.normal(ks[5], (E, H), dtype=jnp.float32) * s}
    _L1_ffn_all = _L1_ffn_setup()
    _L1_ffn_in = {k: v for k, v in _L1_ffn_all.items() if k in ('router_w', 'w1', 'b1', 'w2', 'b2')}
    del _L1_ffn_all
    return {'x': x, 'ctx_1024': ctx_1024, 'mask_BxS2_bf1': mask_BxS2_bf1, 'g_xattn': g_xattn, 'g_ffn': g_ffn, 'L0_xattn_Wq': _L0_xattn_in['Wq'], 'L0_xattn_bq': _L0_xattn_in['bq'], 'L0_xattn_Wk': _L0_xattn_in['Wk'], 'L0_xattn_bk': _L0_xattn_in['bk'], 'L0_xattn_Wv': _L0_xattn_in['Wv'], 'L0_xattn_bv': _L0_xattn_in['bv'], 'L0_ffn_gate_w': _L0_ffn_in['gate_w'], 'L0_ffn_expert_gate': _L0_ffn_in['expert_gate'], 'L0_ffn_expert_up': _L0_ffn_in['expert_up'], 'L0_ffn_expert_down': _L0_ffn_in['expert_down'], 'L0_ffn_shared_gate_w': _L0_ffn_in['shared_gate_w'], 'L0_ffn_shared_up_w': _L0_ffn_in['shared_up_w'], 'L0_ffn_shared_down_w': _L0_ffn_in['shared_down_w'], 'L1_xattn_Wq': _L1_xattn_in['Wq'], 'L1_xattn_Wkv': _L1_xattn_in['Wkv'], 'L1_xattn_Wout': _L1_xattn_in['Wout'], 'L1_xattn_b_out': _L1_xattn_in['b_out'], 'L1_ffn_router_w': _L1_ffn_in['router_w'], 'L1_ffn_w1': _L1_ffn_in['w1'], 'L1_ffn_b1': _L1_ffn_in['b1'], 'L1_ffn_w2': _L1_ffn_in['w2'], 'L1_ffn_b2': _L1_ffn_in['b2']}

def reference(x, ctx_1024, mask_BxS2_bf1, g_xattn, g_ffn, L0_xattn_Wq, L0_xattn_bq, L0_xattn_Wk, L0_xattn_bk, L0_xattn_Wv, L0_xattn_bv, L0_ffn_gate_w, L0_ffn_expert_gate, L0_ffn_expert_up, L0_ffn_expert_down, L0_ffn_shared_gate_w, L0_ffn_shared_up_w, L0_ffn_shared_down_w, L1_xattn_Wq, L1_xattn_Wkv, L1_xattn_Wout, L1_xattn_b_out, L1_ffn_router_w, L1_ffn_w1, L1_ffn_b1, L1_ffn_w2, L1_ffn_b2):
    import jax
    import jax.numpy as jnp

    def _L0_xattn_ref(q, k, v, Wq, bq, Wk, bk, Wv, bv):
        import jax, jax.numpy as jnp
        import numpy as np
        D_MODEL = 128
        N_HEADS = 16
        HEAD_DIM = D_MODEL // N_HEADS
        B, S, D = q.shape
        H, Dh = (N_HEADS, D // N_HEADS)
        qp = q @ Wq.T + bq
        kp = k @ Wk.T + bk
        vp = v @ Wv.T + bv
        qh = qp.reshape(B, S, H, Dh).transpose(0, 2, 1, 3)
        kh = kp.reshape(B, S, H, Dh).transpose(0, 2, 1, 3)
        vh = vp.reshape(B, S, H, Dh).transpose(0, 2, 1, 3)
        scores = jnp.einsum('bhqd,bhkd->bhqk', qh, kh) / jnp.sqrt(jnp.asarray(Dh, qh.dtype))
        attn = jax.nn.softmax(scores, axis=-1)
        out = jnp.einsum('bhqk,bhkd->bhqd', attn, vh)
        return out.transpose(0, 2, 1, 3).reshape(B, S, D)

    def _L0_ffn_ref(hidden_states, gate_w, expert_gate, expert_up, expert_down, shared_gate_w, shared_up_w, shared_down_w):
        import jax, jax.numpy as jnp
        import numpy as np
        B, S, D = (4, 128, 128)
        I = 64
        E = 32
        TOP_K = 8
        N_GROUP = 8
        TOPK_GROUP = 4

        def _group_topk(scores):
            T = scores.shape[0]
            epg = E // N_GROUP
            group_scores = scores.reshape(T, N_GROUP, epg).sum(axis=-1)
            _, top_groups = jax.lax.top_k(group_scores, TOPK_GROUP)
            group_mask = jnp.zeros((T, N_GROUP), scores.dtype).at[jnp.arange(T)[:, None], top_groups].set(1.0)
            expert_mask = jnp.repeat(group_mask, epg, axis=1)
            masked_scores = scores * expert_mask
            topk_w, topk_i = jax.lax.top_k(masked_scores, TOP_K)
            return (topk_w, topk_i)

        def _reference_tuple_inner(hidden_states, gate_w, expert_gate, expert_up, expert_down, shared_gate_w, shared_up_w, shared_down_w):
            b, s, d = hidden_states.shape
            flat = hidden_states.reshape(-1, d)
            T = flat.shape[0]
            logits = flat @ gate_w.T
            scores = jax.nn.sigmoid(logits)
            topk_w, topk_i = _group_topk(scores)
            topk_w = topk_w / jnp.clip(topk_w.sum(axis=-1, keepdims=True), 1e-12)
            combine = jnp.zeros((T, E), flat.dtype).at[jnp.arange(T)[:, None], topk_i].add(topk_w)

            def body(acc, expert):
                wg, wu, wd, w = expert
                h = jax.nn.silu(flat @ wg.T) * (flat @ wu.T)
                return (acc + w[:, None] * (h @ wd.T), None)
            out, _ = jax.lax.scan(body, jnp.zeros_like(flat), (expert_gate, expert_up, expert_down, combine.T))
            shared = jax.nn.silu(flat @ shared_gate_w.T) * (flat @ shared_up_w.T) @ shared_down_w.T
            out = out + shared
            return (out.reshape(b, s, d), logits)
        return _reference_tuple_inner(hidden_states, gate_w, expert_gate, expert_up, expert_down, shared_gate_w, shared_up_w, shared_down_w)[0]

    def _L1_xattn_ref(x, context, mask, Wq, Wkv, Wout, b_out):
        import jax, jax.numpy as jnp
        import numpy as np
        HEADS = 16
        DIM_HEAD = 64
        SCALE = DIM_HEAD ** (-0.5)
        B, Nq, _ = x.shape
        Nkv = context.shape[1]
        q = x @ Wq.T
        kv = context @ Wkv.T
        k, v = jnp.split(kv, 2, axis=-1)
        q = q.reshape(B, Nq, HEADS, DIM_HEAD).transpose(0, 2, 1, 3)
        k = k.reshape(B, Nkv, HEADS, DIM_HEAD).transpose(0, 2, 1, 3)
        v = v.reshape(B, Nkv, HEADS, DIM_HEAD).transpose(0, 2, 1, 3)
        sim = jnp.einsum('bhid,bhjd->bhij', q, k) * SCALE
        max_neg = -jnp.finfo(sim.dtype).max
        sim = jnp.where(mask[:, None, None, :], sim, max_neg)
        attn = jax.nn.softmax(sim, axis=-1)
        out = jnp.einsum('bhij,bhjd->bhid', attn, v)
        out = out.transpose(0, 2, 1, 3).reshape(B, Nq, HEADS * DIM_HEAD)
        return out @ Wout.T + b_out

    def _L1_ffn_ref(hidden_states, router_w, w1, b1, w2, b2):
        import jax, jax.numpy as jnp
        import numpy as np
        TOP_K = 2
        x = hidden_states
        router_logits = jnp.einsum('bth,eh->bte', x, router_w)
        topk_values, topk_indices = jax.lax.top_k(router_logits, TOP_K)
        topk_weights = jax.nn.softmax(topk_values.astype(jnp.float32), axis=-1).astype(x.dtype)
        h1 = jnp.einsum('bth,efh->btef', x, w1) + b1
        h1 = jax.nn.gelu(h1, approximate=False)
        expert_outputs = jnp.einsum('btef,ehf->bteh', h1, w2) + b2
        gather_idx = topk_indices[..., None]
        topk_expert_outputs = jnp.take_along_axis(expert_outputs, gather_idx, axis=2)
        mixed_output = jnp.sum(topk_expert_outputs * topk_weights[..., None], axis=2)
        return mixed_output
    x = x + jnp.tanh(g_xattn[0]) * _L0_xattn_ref(_layernorm(x, axis=-1), ctx_1024, ctx_1024, L0_xattn_Wq, L0_xattn_bq, L0_xattn_Wk, L0_xattn_bk, L0_xattn_Wv, L0_xattn_bv)
    x = x + jnp.tanh(g_ffn[0]) * _L0_ffn_ref(_layernorm(x, axis=-1), L0_ffn_gate_w, L0_ffn_expert_gate, L0_ffn_expert_up, L0_ffn_expert_down, L0_ffn_shared_gate_w, L0_ffn_shared_up_w, L0_ffn_shared_down_w)
    x = x + jnp.tanh(g_xattn[1]) * _L1_xattn_ref(_layernorm(x, axis=-1), ctx_1024, mask_BxS2_bf1, L1_xattn_Wq, L1_xattn_Wkv, L1_xattn_Wout, L1_xattn_b_out)
    x = x + jnp.tanh(g_ffn[1]) * _L1_ffn_ref(_layernorm(x, axis=-1), L1_ffn_router_w, L1_ffn_w1, L1_ffn_b1, L1_ffn_w2, L1_ffn_b2)
    return x

_drawn_inputs = setup_inputs


def setup_inputs(seed=0):
    import zlib

    import numpy as np

    out = dict(_drawn_inputs(seed))
    spreads = {'g_ffn': (-1.0, 0.6), 'L1_xattn_b_out': (0.0, 0.1)}
    factors = {'L0_xattn_bq': 8.0,
     'L0_xattn_bk': 64.0,
     'L0_xattn_bv': 8.0,
     'L0_ffn_gate_w': 8.0,
     'L0_ffn_expert_gate': 8.0,
     'L0_ffn_expert_up': 8.0,
     'L0_ffn_expert_down': 8.0,
     'L0_ffn_shared_gate_w': 8.0,
     'L0_ffn_shared_up_w': 8.0,
     'L0_ffn_shared_down_w': 8.0,
     'L1_ffn_b1': 43.356,
     'L1_ffn_b2': 5.715,
     'L1_ffn_w1': 3.945,
     'L1_ffn_w2': 3.203}
    for name, (base, spread) in spreads.items():
        noise = np.random.default_rng([zlib.crc32(name.encode()), seed]).standard_normal(out[name].shape)
        drawn = base * np.exp(spread * noise) if base else spread * noise
        out[name] = jnp.asarray(drawn.astype(out[name].dtype))
    for name, factor in factors.items():
        out[name] = (out[name] * factor).astype(out[name].dtype)
    return out
```

```python
from contextlib import ExitStack

import numpy as np

import concourse.bass as bass
from concourse import mybir

F32 = mybir.dt.float32
F32R = mybir.dt.float32r
BF16 = mybir.dt.bfloat16
U8 = mybir.dt.uint8
ALU = mybir.AluOpType
ACT = mybir.ActivationFunctionType
X = mybir.AxisListType.X

P = 128
B, S, D = 128, 64, 128
NT = B * S // P
EPS = 1e-5


def counted(value):
    return not isinstance(value, int) or value > 0


def steps(eng, n, body):
    body(0, False, True)
    with eng.Fori(1, n - 1) as i:
        body(i, True, True)
    body(n - 1, True, False)


def layernorm_statistics(s, sem):
    sq_in, sq_out = sem("ln_variance_ready"), sem("ln_root_ready")

    def on_vector(dve):
        with dve.Fori(0, NT // 8) as k:
            for u in range(8):
                dve.bn_stats(s.stats[:, bass.ds(k * 8 + u, 1), :], s.x[:, bass.ds(k * 8 + u, 1), :])
        dve.drain()
        mean_even, mean_odd = s.stats[:, :, 1], s.stats[:, :, 4]
        dve.tensor_tensor(s.mean[:, :], mean_even, mean_odd, ALU.add)
        dve.tensor_tensor(s.rstd[:, :], mean_even, mean_odd, ALU.subtract)
        dve.tensor_tensor(s.var[:, :], s.stats[:, :, 2], s.stats[:, :, 5], ALU.add)
        dve.drain()
        dve.tensor_scalar(s.mean[:, :], s.mean[:, :], 0.5, None, ALU.mult)
        dve.tensor_tensor(s.rstd[:, :], s.rstd[:, :], s.rstd[:, :], ALU.mult)
        dve.tensor_scalar(s.var[:, :], s.var[:, :], 1.0 / D, EPS, ALU.mult, ALU.add)
        dve.drain()
        dve.scalar_tensor_tensor(out=s.var[:, :], in0=s.rstd[:, :], scalar=0.25, in1=s.var[:, :],
                                 op0=ALU.mult, op1=ALU.add).then_inc(sq_in, 1)
        dve.wait_ge(sq_out, 1)
        dve.reciprocal(s.rstd[:, :], s.root[:, :])
        dve.drain()

    def on_scalar(act):
        act.wait_ge(sq_in, 1)
        act.activation(s.root[:, :], s.var[:, :], ACT.Sqrt, bias=0.0).then_inc(sq_out, 1)

    return on_vector, on_scalar


def split_on_pool(pool, source, chunks, width, hi, lo, staging, loaded, split):
    for k in range(chunks + 1):
        if k < chunks:
            if counted(k - 1):
                pool.wait_ge(split, k - 1)
            pool.dma_start(staging[:, k % 2, 0:width], source[:, k * width:(k + 1) * width]).then_inc(loaded[k % 2], 16)
        if k:
            c = slice((k - 1) * width, k * width)
            part = staging[:, (k - 1) % 2, 0:width]
            pool.wait_ge(loaded[(k - 1) % 2], 16 * ((k - 1) // 2 + 1))
            pool.tensor_copy(hi[:, c], part)
            pool.drain()
            pool.tensor_tensor(lo[:, c], part, hi[:, c].bitcast(F32), ALU.subtract).then_inc(split, 1)


def normalized(dve, s, z, k, n):
    for t in range(n):
        last = dve.tensor_scalar(z[:, t, :], s.x[:, bass.ds(k + t, 1), :], s.mean[:, bass.ds(k + t, 1)],
                                 s.rstd[:, bass.ds(k + t, 1)], ALU.subtract, ALU.mult)
    return last


def setup(nc, s, a):
    with ExitStack() as ctx:
        loaded = ctx.enter_context(nc.semaphore("loaded"))
        gates = ctx.enter_context(nc.semaphore("gates"))
        block = ctx.enter_context(nc.Block())
        pieces = [(s.x[:, 16 * k:16 * k + 16, :], a["x"][:, 16 * k:16 * k + 16, :]) for k in range(4)]
        pieces += [(s.ident[:, :], a["ident"]), (s.gates[:, 0:2], a["g_xattn"].partition_broadcast(P)),
                   (s.gates[:, 2:4], a["g_ffn"].partition_broadcast(P)), (s.tri[:, :, :], a["tri"])]

        @block.sync
        def _(sp):
            for dst, src in pieces:
                sp.dma_start(dst, src).then_inc(loaded, 16)
            sp.wait_ge(loaded, 16 * len(pieces))

        @block.scalar
        def _(act):
            act.wait_ge(loaded, 16 * len(pieces))
            act.activation(s.gates[:, :], s.gates[:, :], ACT.Tanh, bias=0.0).then_inc(gates, 1)
            act.wait_ge(gates, 1)


def softmax_shifted(dve, out, scores, top):
    dve.tensor_reduce(top, scores, X, ALU.max)
    dve.drain()
    m = top.rearrange("p (g r) -> p g r", g=4).unsqueeze(3).broadcast_to([P, 4, 4, S])
    return dve.tensor_tensor(out.rearrange("p (g r j) -> p g r j", g=4, r=4), scores, m, ALU.subtract)


def attention_0(nc, s, a):
    N = NT // 2
    SCALE = 8.0 ** -0.5
    with ExitStack() as ctx:
        def sb(name, shape, dt=F32):
            return ctx.enter_context(nc.sbuf_tensor(name, shape, dt))

        def ps(name, shape, dt=F32):
            return ctx.enter_context(nc.psum_tensor(name, shape, dt))

        def sem(name):
            return ctx.enter_context(nc.semaphore("a0_" + name))

        wq, wk, wv = sb("wq", [P, D]), sb("wk", [P, D]), sb("wv", [P, D])
        bq, bk, bv = sb("bq", [P, 1]), sb("bk", [P, 1]), sb("bv", [P, D])
        head_mask, bq_masked = sb("head_mask", [P, 4]), sb("bq_masked", [P, 4])
        place = sb("place", [P, 2, P])
        ctxT = sb("ctxT", [P, 2 * P])
        z, zT = sb("z", [P, 2, D]), sb("zT", [P, 2 * P])
        qm, kT = sb("qm", [P, 4, 4, S]), sb("kT", [P, 2 * P])
        v1 = sb("v1", [P, 2, 8, 17])
        top = sb("top", [P, 2, 16])
        probs, probsT = sb("probs", [P, 2, 8 * P]), sb("probsT", [P, 2, 8 * P])
        rden, ob = sb("rden", [P, 2, 16]), sb("ob", [P, 2, 2, P])

        scores = ps("scores", [P, 4, 2, 2, 2, S])
        bank4, bank5 = ps("bank4", [P, 512]), ps("bank5", [P, 512])
        heads = ps("heads", [P, 2, 512])

        loaded, consts, ctx_in = sem("loaded"), sem("consts"), sem("ctx_in")
        z_ready, zT_mm, zT_ready = sem("z_ready"), sem("zT_mm"), sem("zT_ready")
        qk_mm, qk_ready, v_mm, v_ready = sem("qk_mm"), sem("qk_ready"), sem("v_mm"), sem("v_ready")
        scores_mm, shifted, exped = sem("scores_mm"), sem("shifted"), sem("exped")
        pT_mm, pT_ready = sem("pT_mm"), sem("pT_ready")
        heads_mm, heads_ready, y_mm, x_new = sem("heads_mm"), sem("heads_ready"), sem("y_mm"), sem("x_new")
        w_loaded, w_split = [sem("w_loaded_even"), sem("w_loaded_odd")], sem("w_split")
        ln_vector, ln_scalar = layernorm_statistics(s, sem)
        block = ctx.enter_context(nc.Block())
        small = [(wq[:, :], a["wq0T"]), (wk[:, :], a["wk0T"]), (wv[:, :], a["wv0T"]), (bq[:, :], a["bq0"]),
                 (bk[:, :], a["bk0"]), (bv[:, :], a["bv0"].partition_broadcast(P)),
                 (head_mask[:, :], a["head_mask"]), (place[:, :, :], a["place"])]

        @block.sync
        def _(sp):
            for dst, src in small:
                sp.dma_start(dst, src).then_inc(loaded, 16)
            sp.dma_start(ctxT[:, :], a["ctxT"][:, 0:2 * P]).then_inc(ctx_in, 16)
            with sp.Fori(1, N) as k:
                sp.wait_ge(v_mm, k)
                sp.dma_start(ctxT[:, :], a["ctxT"][:, bass.ds(k * (2 * P), 2 * P)]).then_inc(ctx_in, 16)

        @block.gpsimd
        def _(pool):
            split_on_pool(pool, a["w_moe0"], 5, 1280, s.w_hi, s.w_lo, s.staging, w_loaded, w_split)
            pool.wait_ge(w_split, 5)

        @block.vector
        def _(dve):
            dve.wait_ge(loaded, 16 * len(small))
            dve.memset(v1[:, :, :, :], 1.0)
            dve.memset(ob[:, :, :, :], 0.0)
            dve.tensor_scalar(bq_masked[:, :], head_mask[:, :], bq[:, 0:1], None, ALU.mult).then_inc(consts, 1)
            ln_vector(dve)

            def values(k):
                dve.wait_ge(v_mm, k + 1)
                for t in range(2):
                    last = dve.tensor_tensor(v1[:, t, :, 0:16], bank4[:, t * P:(t + 1) * P].rearrange("p (a c) -> p a c", c=16),
                                             bv[:, :].rearrange("p (a c) -> p a c", c=16), ALU.add)
                last.then_inc(v_ready, 1)

            normalized(dve, s, z, 0, 2).then_inc(z_ready, 1)
            values(0)

            def body(i, has_previous, has_next):
                if has_next:
                    dve.wait_ge(zT_mm, i + 1)
                    normalized(dve, s, z, 2 * i + 2, 2).then_inc(z_ready, 1)
                for t in range(2):
                    if counted(4 * i - 2 + 2 * t):
                        dve.wait_ge(pT_mm, 4 * i - 2 + 2 * t)
                    dve.wait_ge(scores_mm, i + 1)
                    softmax_shifted(dve, probs[:, t, :], scores[:, :, t, :, :, :].rearrange("p g r b j -> p g (r b) j"),
                                    top[:, t, :]).then_inc(shifted, 1)
                dve.wait_ge(heads_mm, i + 1)
                if counted(i):
                    dve.wait_ge(y_mm, i)
                for b in range(2):
                    o = heads[:, b, 0:272].rearrange("p (a c) -> p a c", c=17)
                    dve.reciprocal(rden[:, b, :], o[:, :, 16])
                dve.drain()
                for b in range(2):
                    for h in range(2):
                        rows = slice(64 * h, 64 * h + 64)
                        o = heads[rows, b, 0:272].rearrange("p (a c) -> p a c", c=17)[:, :, 8 * h:8 * h + 8]
                        dst = ob[rows, b, :, :].rearrange("p t (a h d) -> p (t a) h d", h=2, d=8)[:, :, h, :]
                        last = dve.tensor_tensor(dst, o, rden[rows, b, :].unsqueeze(2).broadcast_to([64, 16, 8]), ALU.mult)
                last.then_inc(heads_ready, 1)
                if has_next:
                    values(i + 1)
                dve.wait_ge(y_mm, i + 1)
                xt = s.x[:, bass.ds(2 * i, 2), :]
                dve.scalar_tensor_tensor(out=xt, in0=bank5[:, 0:2 * P].rearrange("p (t c) -> p t c", t=2),
                                         scalar=s.gates[:, 0:1], in1=xt, op0=ALU.mult, op1=ALU.add).then_inc(x_new, 1)

            steps(dve, N, body)

        @block.scalar
        def _(act):
            ln_scalar(act)
            act.wait_ge(consts, 1)

            def normalized_transposed(k):
                act.wait_ge(zT_mm, k + 1)
                act.activation(zT[:, :], bank5[:, 0:2 * P], ACT.Copy, bias=0.0).then_inc(zT_ready, 1)

            def queries_and_keys(k):
                act.wait_ge(qk_mm, k + 1)
                for r in range(4):
                    act.activation(qm[:, :, r, :], bank4[:, 0:2 * P].rearrange("p (b i) -> p b i", b=4), ACT.Identity, bias=bq_masked[:, r:r + 1],
                                   scale=head_mask[:, r:r + 1])
                act.activation(kT[:, :], bank4[:, 2 * P:4 * P], ACT.Identity, bias=bk[:, 0:1]).then_inc(qk_ready, 1)

            normalized_transposed(0)
            queries_and_keys(0)

            def body(i, has_previous, has_next):
                if has_next:
                    normalized_transposed(i + 1)
                for t in range(2):
                    act.wait_ge(shifted, 2 * i + t + 1)
                    act.activation(probs[:, t, :], probs[:, t, :], ACT.Exp, bias=0.0, scale=SCALE).then_inc(exped, 1)
                    if t == 0 and has_next:
                        queries_and_keys(i + 1)
                if counted(i):
                    act.wait_ge(heads_mm, i)
                for q in range(4):
                    act.wait_ge(pT_mm, 4 * i + q + 1)
                    src = (bank5, bank4)[q % 2]
                    act.activation(probsT[:, q // 2, (q % 2) * 512:(q % 2) * 512 + 512], src[:, :], ACT.Copy,
                                   bias=0.0).then_inc(pT_ready, 1)

            steps(act, N, body)

        @block.tensor
        def _(pe):
            pe.wait_ge(loaded, 16 * len(small))

            def transposed(k):
                pe.wait_ge(z_ready, k + 1)
                for t in range(2):
                    last = pe.transpose(bank5[:, t * P:(t + 1) * P], z[:, t, :], s.ident[:, :])
                last.then_inc(zT_mm, 1)

            def project_qk(k):
                pe.wait_ge(zT_ready, k + 1)
                pe.wait_ge(ctx_in, 16 * (k + 1))
                pe.matmul(bank4[:, 0:2 * P], wq[:, :], zT[:, :], start=True, stop=True)
                pe.matmul(bank4[:, 2 * P:4 * P], wk[:, :], ctxT[:, :], start=True, stop=True).then_inc(qk_mm, 1)

            def project_v():
                for t in range(2):
                    last = pe.matmul(bank4[:, t * P:(t + 1) * P], ctxT[:, t * P:(t + 1) * P], wv[:, :], start=True, stop=True)
                last.then_inc(v_mm, 1)

            transposed(0)
            project_qk(0)
            pe.wait_ge(qk_ready, 1)
            project_v()

            def body(i, has_previous, has_next):
                pe.wait_ge(qk_ready, i + 1)
                if counted(2 * i):
                    pe.wait_ge(shifted, 2 * i)
                for t in range(2):
                    for rp in range(2):
                        for b in range(2):
                            at = t * P + b * S
                            for g in range(4):
                                rows = slice(32 * g, 32 * g + 32)
                                last = pe.matmul(scores[:, g, t, rp, b, :], qm[rows, 2 * t + b, 2 * rp:2 * rp + 2, :],
                                                 kT[rows, at:at + S], start=True, stop=True)
                last.then_inc(scores_mm, 1)
                if counted(i):
                    pe.wait_ge(x_new, i)
                if has_next:
                    transposed(i + 1)
                pe.wait_ge(v_ready, i + 1)
                if has_next:
                    project_qk(i + 1)
                for t in range(2):
                    pe.wait_ge(exped, 2 * i + t + 1)
                    for half in range(2):
                        if t:
                            pe.wait_ge(pT_ready, 4 * i + half + 1)
                        elif has_next:
                            pe.wait_ge((zT_ready, qk_ready)[half], i + 2)
                        dst = (bank5, bank4)[half]
                        for q in range(4):
                            pr = 4 * half + q
                            last = pe.transpose(dst[:, q * P:(q + 1) * P], probs[:, t, pr * P:(pr + 1) * P], s.ident[:, :])
                        last.then_inc(pT_mm, 1)
                if counted(i):
                    pe.wait_ge(heads_ready, i)
                for t in range(2):
                    pe.wait_ge(pT_ready, 4 * i + 2 * t + 2)
                    for pr in range(8):
                        for b in range(2):
                            rows = slice(64 * b, 64 * b + 64)
                            c = 17 * (8 * t + pr)
                            last = pe.matmul(heads[:, b, c:c + 17], probsT[rows, t, pr * P:(pr + 1) * P], v1[rows, t, pr, :],
                                             start=True, stop=True)
                last.then_inc(heads_mm, 1)
                if has_next:
                    project_v()
                pe.wait_ge(heads_ready, i + 1)
                for b in range(2):
                    last = pe.matmul(bank5[:, 0:2 * P], place[:, b, :], ob[:, b, :, :], start=(b == 0), stop=(b == 1))
                last.then_inc(y_mm, 1)

            steps(pe, N, body)


def chosen(dve, s, tmp, values, k):
    other = values.unsqueeze(2).broadcast_to([P, 4, 8, 8])
    own = values.unsqueeze(3).broadcast_to([P, 4, 8, 8])
    dve.tensor_tensor(tmp.larger[:, :, :, :], other, own, ALU.is_gt)
    dve.tensor_tensor(tmp.equal[:, :, :, :], other, own, ALU.is_equal)
    dve.drain()
    dve.tensor_tensor(tmp.equal[:, :, :, :], tmp.equal[:, :, :, :], s.tri[:, :, :].unsqueeze(1).broadcast_to([P, 4, 8, 8]), ALU.mult)
    dve.drain()
    dve.tensor_tensor(tmp.larger[:, :, :, :], tmp.larger[:, :, :, :], tmp.equal[:, :, :, :], ALU.add)
    dve.drain()
    dve.tensor_reduce(tmp.rank[:, :, :], tmp.larger[:, :, :, :], X, ALU.add)
    dve.drain()
    dve.tensor_scalar(tmp.sel[:, :, :], tmp.rank[:, :, :], float(k), None, ALU.is_lt)
    dve.drain()


def experts_0(nc, s, a):
    N, C = NT // 4, 17
    G, U, DN = 0, 2112, 4224

    with ExitStack() as ctx:
        def sb(name, shape, dt=F32):
            return ctx.enter_context(nc.sbuf_tensor("e0_" + name, shape, dt))

        def ps(name, shape, dt=F32):
            return ctx.enter_context(nc.psum_tensor("e0_" + name, shape, dt))

        def sem(name):
            return ctx.enter_context(nc.semaphore("e0_" + name))

        pick = sb("pick", [96, 16, P], BF16)
        identb = sb("identb", [P, P], BF16)
        router = sb("router", [P, 32])
        z = sb("z", [P, 4, D])
        zT = sb("zT", [P, 2, 512])
        zT_hi, zT_lo = sb("zT_hi", [P, 2, 512], F32R), sb("zT_lo", [P, 2, 512], F32R)
        gated, raised, hidden = sb("gated", [P, 2, 512]), sb("raised", [P, 2, 512]), sb("hidden", [P, 3, 512])
        down = sb("down", [P, C, D])
        yT = sb("yT", [P, 512])
        weightsT = sb("weightsT", [96, 2, 512], BF16)
        tmp = Shared()
        tmp.larger, tmp.equal = sb("larger", [P, 4, 8, 8]), sb("equal", [P, 4, 8, 8])
        tmp.rank, tmp.sel = sb("rank", [P, 4, 8]), sb("sel", [P, 4, 8])
        scored, groups = sb("scored", [P, 4, 32]), sb("groups", [P, 4, 8])
        masked, left, top8 = sb("masked", [P, 4, 32]), sb("left", [P, 4, 32]), sb("top8", [P, 4, 8])
        total = sb("total", [P, 4])
        parts = sb("parts", [P, 4, 3, 32], BF16)

        gate, up, spread = ps("gate", [P, 2, 512]), ps("up", [P, 2, 512]), ps("spread", [P, 2, 512])
        out_sum, turned = ps("out_sum", [P, 512]), ps("turned", [P, 512])
        turned_bf = turned[0:96, 0:256].bitcast(BF16)

        loaded, consts = sem("loaded"), sem("consts")
        gate_mm, up_mm, spread_mm, down_mm = sem("gate_mm"), sem("up_mm"), sem("spread_mm"), sem("down_mm")
        gated_ready, raised_ready, hidden_ready = sem("gated_ready"), sem("raised_ready"), sem("hidden_ready")
        yT_ready, y_mm, x_new = sem("yT_ready"), sem("y_mm"), sem("x_new")
        z_ready, zT_mm, zT_hi_ready, zT_ready = sem("z_ready"), sem("zT_mm"), sem("zT_hi_ready"), sem("zT_ready")
        logits_mm, scored_ready, parts_ready = sem("logits_mm"), sem("scored_ready"), sem("parts_ready")
        weights_mm, weights_ready = sem("weights_mm"), sem("weights_ready")
        ln_vector, ln_scalar = layernorm_statistics(s, sem)
        block = ctx.enter_context(nc.Block())

        def rows(j):
            return 128 if j < 16 else 64

        def before(n, j, ring):
            if j >= ring:
                return C * n + j - ring + 1
            return C * (n - 1) + max(m for m in range(C) if m % ring == j) + 1

        picks_in = s.staging[0:96, :, 0:1024]
        small = [(picks_in, a["pick"].rearrange("k (u j) m -> k u (j m)", u=2)), (router[:, :], a["router0"]),
                 (down[:, :, :], a["w_moe0"][:, DN:DN + C * D].rearrange("p (c d) -> p c d", d=D))]

        @block.sync
        def _(sp):
            for dst, src in small:
                sp.dma_start(dst, src).then_inc(loaded, 16)
            sp.wait_ge(loaded, 16 * len(small))

        @block.tensor
        def _(pe):
            pe.wait_ge(loaded, 16 * len(small))
            pe.wait_ge(consts, 1)

            def turn_z(n):
                pe.wait_ge(z_ready, n + 1)
                if counted(n):
                    pe.wait_ge(weights_ready, n)
                for t in range(4):
                    last = pe.transpose(turned[:, t * P:(t + 1) * P], z[:, t, :], s.ident[:, :])
                last.then_inc(zT_mm, 1)

            def logits(n, u):
                pe.wait_ge(zT_ready, n + 1)
                for t in range(4):
                    last = pe.matmul(turned[:, 32 * t:32 * t + 32], zT[:, u, t * P:(t + 1) * P], router[:, :], start=True, stop=True)
                last.then_inc(logits_mm, 1)

            def turn_weights(n):
                pe.wait_ge(parts_ready, n + 1)
                for t in range(4):
                    last = pe.transpose(turned_bf[:, t * P:(t + 1) * P], parts[:, t, :, :].rearrange("p c e -> p (c e)"), identb[:, :])
                last.then_inc(weights_mm, 1)

            def turn_y(n):
                pe.wait_ge(yT_ready, n + 1)
                for t in range(4):
                    last = pe.transpose(turned[:, t * P:(t + 1) * P], yT[:, t * P:(t + 1) * P], s.ident[:, :])
                last.then_inc(y_mm, 1)

            def product(dst, w, hi, lo, col, m, first=True):
                w_h, w_l = s.w_hi[:, col:col + m], s.w_lo[:, col:col + m]
                pe.matmul(dst, w_h, hi, start=True, stop=False)
                pe.matmul(dst, w_h, lo, start=False, stop=False)
                return pe.matmul(dst, w_l, hi, start=False, stop=True)

            def down_product(n, j):
                m = rows(j)
                pe.wait_ge(hidden_ready, C * n + j + 1)
                if j == 0:
                    if counted(n):
                        pe.wait_ge(yT_ready, n)
                pe.matmul(out_sum[:, :], down[0:m, j, :], hidden[0:m, j % 3, :], start=(j == 0), stop=(j == C - 1)).then_inc(down_mm, 1)

            turn_z(0)
            logits(0, 0)
            turn_weights(0)
            LAG = 2

            def body(i, has_previous, has_next):
                for u in range(2):
                    n = 2 * i + u
                    hi, lo = zT_hi[:, u, :], zT_lo[:, u, :]
                    prev, nxt = has_previous or u == 1, has_next or u == 0
                    for j in range(C):
                        m = rows(j)
                        if counted(before(n, j, 2)):
                            pe.wait_ge(gated_ready, before(n, j, 2))
                        product(gate[0:m, j % 2, :], None, hi, lo, G + j * P, m).then_inc(gate_mm, 1)
                        if counted(before(n, j, 2)):
                            pe.wait_ge(raised_ready, before(n, j, 2))
                        product(up[0:m, j % 2, :], None, hi, lo, U + j * P, m).then_inc(up_mm, 1)
                        if j < 16:
                            if j == 0:
                                pe.wait_ge(weights_ready, n + 1)
                            if counted(C * n + j - 1):
                                pe.wait_ge(hidden_ready, C * n + j - 1)
                            pe.matmul(spread[:, j % 2, :], pick[:, j, :], weightsT[:, u, :], start=True, stop=True).then_inc(spread_mm, 1)
                        if j >= LAG:
                            down_product(n, j - LAG)
                        elif prev:
                            down_product(n - 1, C - LAG + j)
                        if j == 3 and prev:
                            turn_y(n - 1)
                        if j == 5 and nxt:
                            if counted(n):
                                pe.wait_ge(x_new, n)
                            turn_z(n + 1)
                        if j == 8 and nxt:
                            logits(n + 1, 1 - u)
                        if j == 14 and nxt:
                            turn_weights(n + 1)

            steps(pe, N // 2, body)
            for j in range(C - LAG, C):
                down_product(N - 1, j)
            turn_y(N - 1)

        @block.scalar
        def _(act):
            ln_scalar(act)

            def high_part(n, u):
                act.wait_ge(zT_mm, n + 1)
                act.activation(zT_hi[:, u, :], turned[:, :], ACT.Copy, bias=0.0)
                act.activation(zT[:, u, :], turned[:, :], ACT.Copy, bias=0.0).then_inc(zT_hi_ready, 1)

            def score(n):
                act.wait_ge(logits_mm, n + 1)
                act.activation(scored[:, :, :], turned[:, 0:P].rearrange("p (t e) -> p t e", t=4), ACT.Sigmoid,
                               bias=0.0).then_inc(scored_ready, 1)

            def keep_weights(n, u):
                act.wait_ge(weights_mm, n + 1)
                act.activation(weightsT[:, u, :], turned_bf, ACT.Copy, bias=0.0).then_inc(weights_ready, 1)

            def keep_y(n):
                act.wait_ge(down_mm, C * (n + 1))
                act.activation(yT[:, :], out_sum[:, :], ACT.Copy, bias=0.0).then_inc(yT_ready, 1)

            high_part(0, 0)
            score(0)
            keep_weights(0, 0)

            def body(i, has_previous, has_next):
                for u in range(2):
                    n = 2 * i + u
                    prev, nxt = has_previous or u == 1, has_next or u == 0
                    for j in range(C):
                        m = rows(j)
                        act.wait_ge(gate_mm, C * n + j + 1)
                        if counted(before(n, j, 2)):
                            act.wait_ge(raised_ready, before(n, j, 2))
                        act.activation(gated[0:m, j % 2, :], gate[0:m, j % 2, :], ACT.Silu, bias=0.0).then_inc(gated_ready, 1)
                        if j == 2 and prev:
                            keep_y(n - 1)
                        if j == 6 and nxt:
                            high_part(n + 1, 1 - u)
                        if j == 9 and nxt:
                            score(n + 1)
                        if j == 15 and nxt:
                            keep_weights(n + 1, 1 - u)

            steps(act, N // 2, body)
            keep_y(N - 1)

        @block.vector
        def _(dve):
            dve.wait_ge(loaded, 16 * len(small))
            dve.tensor_copy(pick[:, :, :].rearrange("k (u j) m -> k u (j m)", u=2), picks_in)
            dve.tensor_copy(identb[:, :], s.ident[:, :]).then_inc(consts, 1)
            ln_vector(dve)

            def low_part(n, u):
                dve.wait_ge(zT_hi_ready, n + 1)
                dve.tensor_tensor(zT_lo[:, u, :], turned[:, :], zT_hi[:, u, :].bitcast(F32), ALU.subtract).then_inc(zT_ready, 1)

            def route(n):
                dve.wait_ge(scored_ready, n + 1)
                dve.tensor_reduce(groups[:, :, :], scored[:, :, :].rearrange("p t (g e) -> p t g e", e=4), X, ALU.add)
                dve.drain()
                chosen(dve, s, tmp, groups[:, :, :], 4)
                dve.tensor_tensor(masked[:, :, :].rearrange("p t (g e) -> p (t g) e", e=4),
                                  scored[:, :, :].rearrange("p t (g e) -> p (t g) e", e=4),
                                  tmp.sel[:, :, :].rearrange("p t g -> p (t g)").unsqueeze(2).broadcast_to([P, 32, 4]), ALU.mult)
                dve.drain()
                for t in range(4):
                    dve.max(top8[:, t, :], masked[:, t, :])
                dve.drain()
                for t in range(4):
                    dve.match_replace(left[:, t, :], top8[:, t, :], masked[:, t, :], 0.0)
                dve.tensor_reduce(total[:, :], top8[:, :, :], X, ALU.add)
                dve.drain()
                dve.tensor_tensor(masked[:, :, :], masked[:, :, :], left[:, :, :], ALU.subtract)
                dve.tensor_scalar(total[:, :], total[:, :], 1e-12, None, ALU.max)
                dve.drain()
                dve.reciprocal(total[:, :], total[:, :])
                dve.drain()
                dve.tensor_tensor(masked[:, :, :], masked[:, :, :], total[:, :].unsqueeze(2).broadcast_to([P, 4, 32]), ALU.mult)
                dve.drain()
                if counted(n):
                    dve.wait_ge(weights_mm, n)
                dve.tensor_copy(parts[:, :, 0, :], masked[:, :, :])
                dve.drain()
                dve.tensor_tensor(masked[:, :, :], masked[:, :, :], parts[:, :, 0, :], ALU.subtract)
                dve.drain()
                dve.tensor_copy(parts[:, :, 1, :], masked[:, :, :])
                dve.drain()
                dve.tensor_tensor(parts[:, :, 2, :], masked[:, :, :], parts[:, :, 1, :], ALU.subtract).then_inc(parts_ready, 1)

            def update(n):
                dve.wait_ge(y_mm, n + 1)
                xt = s.x[:, bass.ds(4 * n, 4), :]
                dve.scalar_tensor_tensor(out=xt, in0=turned[:, :].rearrange("p (t c) -> p t c", t=4),
                                         scalar=s.gates[:, 2:3], in1=xt, op0=ALU.mult, op1=ALU.add).then_inc(x_new, 1)

            def finish_hidden(n, j):
                m = rows(j)
                dve.wait_ge(raised_ready, C * n + j + 1)
                if counted(before(n, j, 3)):
                    dve.wait_ge(down_mm, before(n, j, 3))
                if j < 16:
                    dve.wait_ge(spread_mm, 16 * n + j + 1)
                    dve.tensor_tensor(hidden[:, j % 3, :], spread[:, j % 2, :], raised[:, j % 2, :], ALU.mult).then_inc(hidden_ready, 1)
                else:
                    dve.tensor_copy(hidden[0:m, j % 3, :], raised[0:m, j % 2, :]).then_inc(hidden_ready, 1)

            normalized(dve, s, z, 0, 4).then_inc(z_ready, 1)
            low_part(0, 0)
            route(0)

            def body(i, has_previous, has_next):
                for u in range(2):
                    n = 2 * i + u
                    prev, nxt = has_previous or u == 1, has_next or u == 0
                    for j in range(C):
                        m = rows(j)
                        dve.wait_ge(gated_ready, C * n + j + 1)
                        dve.wait_ge(up_mm, C * n + j + 1)
                        if j < 2:
                            if counted(before(n, j, 2)):
                                dve.wait_ge(hidden_ready, before(n, j, 2))
                        else:
                            if counted(C * n + j - 1):
                                dve.wait_ge(hidden_ready, C * n + j - 1)
                        dve.tensor_tensor(raised[0:m, j % 2, :], up[0:m, j % 2, :], gated[0:m, j % 2, :], ALU.mult).then_inc(raised_ready, 1)
                        if j >= 1:
                            finish_hidden(n, j - 1)
                        if j == 1 and nxt:
                            dve.wait_ge(zT_mm, n + 1)
                            normalized(dve, s, z, 4 * n + 4, 4).then_inc(z_ready, 1)
                        if j == 4 and prev:
                            update(n - 1)
                        if j == 7 and nxt:
                            low_part(n + 1, 1 - u)
                        if j == 10 and nxt:
                            route(n + 1)
                    finish_hidden(n, C - 1)

            steps(dve, N // 2, body)
            update(N - 1)


MASKED = 2.0 ** 100


def attention_1(nc, s, a):
    N = NT // 2
    SCALE = 64.0 ** -0.5
    with ExitStack() as ctx:
        def sb(name, shape, dt=F32):
            return ctx.enter_context(nc.sbuf_tensor("a1_" + name, shape, dt))

        def ps(name, shape, dt=F32):
            return ctx.enter_context(nc.psum_tensor("a1_" + name, shape, dt))

        def sem(name):
            return ctx.enter_context(nc.semaphore("a1_" + name))

        m_hi, m_lo = sb("m_hi", [P, 16, D], F32R), sb("m_lo", [P, 16, D], F32R)
        n_w = sb("n_w", [P, 16, D])
        b_out = sb("b_out", [P, 1])
        mask_row = sb("mask_row", [1, B * S], U8)
        mask_add = sb("mask_add", [1, 2, P], BF16)
        ones = sb("ones", [1, P], BF16)
        z = sb("z", [P, 2, D])
        zT_hi, zT_lo = sb("zT_hi", [P, 2 * P], F32R), sb("zT_lo", [P, 2 * P], F32R)
        ctxT, ctx_in = sb("ctxT", [P, 2 * P]), sb("ctx", [P, 2, D])
        c_hi, c_lo = sb("c_hi", [P, 2, 2, D], F32R), sb("c_lo", [P, 2, 2, D], F32R)
        g = sb("g", [P, 16, 2 * P])
        top, den, rden = sb("top", [P, 2, 16]), sb("den", [P, 2, 16]), sb("rden", [P, 2, 16])
        probs = sb("probs", [P, 2, 8 * P])
        pT_hi, pT_lo = sb("pT_hi", [P, 8 * P], F32R), sb("pT_lo", [P, 8 * P], F32R)
        u = sb("u", [P, 16, 2 * P])
        yT = sb("yT", [P, 2 * P])
        heads_in = u[0:64, 0:8, :].rearrange("p a (h d) -> p (a h) d", h=2)
        heads_in2 = u[0:64, 8:16, :].rearrange("p a (h d) -> p (a h) d", h=2)

        scores = ps("scores", [P, 2, 8, 2, S])
        work = ps("work", [P, 2, 512])
        out_sum = ps("out_sum", [P, 512])
        turned = ps("turned", [P, 512])

        loaded, prepared = sem("loaded"), sem("prepared")
        w_mm, w_ready = sem("w_mm"), sem("w_ready")
        ctxT_in, ctx_loaded, c_hi_ready, c_ready = sem("ctxT_in"), sem("ctx_loaded"), sem("c_hi_ready"), sem("c_ready")
        z_ready, zT_mm, zT_hi_ready, zT_ready = sem("z_ready"), sem("zT_mm"), sem("zT_hi_ready"), sem("zT_ready")
        g_mm, g_ready, mask_ready = sem("g_mm"), sem("g_ready"), sem("mask_ready")
        scores_mm, shifted, exped, den_ready, normed = (sem("scores_mm"), sem("shifted"), sem("exped"),
                                                        sem("den_ready"), sem("normed"))
        pT_mm, pT_hi_ready, pT_ready = sem("pT_mm"), sem("pT_hi_ready"), sem("pT_ready")
        u_mm, u_ready, out_mm, yT_ready, y_mm, x_new = (sem("u_mm"), sem("u_ready"), sem("out_mm"), sem("yT_ready"),
                                                        sem("y_mm"), sem("x_new"))
        w_loaded, w_split = [sem("w_loaded_even"), sem("w_loaded_odd")], sem("w_split")
        ln_vector, ln_scalar = layernorm_statistics(s, sem)

        with nc.Block() as block:
            gh = g[0:64, 0:8, :].rearrange("p a (h d) -> p (a h) d", h=2)
            gh2 = g[0:64, 8:16, :].rearrange("p a (h d) -> p (a h) d", h=2)
            small = [(heads_in, a["wq1"]), (heads_in2, a["wk1"]), (gh, a["wv1"]), (gh2, a["wo1"]),
                     (b_out[:, :], a["bo1"]), (mask_row[:, :], a["mask"])]

            @block.sync
            def _(sp):
                for dst, src in small:
                    sp.dma_start(dst, src).then_inc(loaded, 16)
                sp.wait_ge(loaded, 16 * len(small))

            @block.tensor
            def _(pe):
                pe.wait_ge(loaded, 16 * len(small))
                for k in range(8):
                    if counted(k - 1):
                        pe.wait_ge(w_ready, k - 1)
                    left, right = (heads_in, heads_in2) if k < 4 else (gh, gh2)
                    for q in range(4):
                        h = 4 * (k % 4) + q
                        last = pe.matmul(work[:, k % 2, q * D:(q + 1) * D], left[:, h, :], right[:, h, :], start=True, stop=True)
                    last.then_inc(w_mm, 1)

            @block.vector
            def _(dve):
                dve.memset(ones[:, :], 1.0)
                dve.memset(c_hi[:, :, :, :].bitcast(F32), 0.0)
                dve.memset(c_lo[:, :, :, :].bitcast(F32), 0.0)
                for k in range(8):
                    c = slice(4 * (k % 4), 4 * (k % 4) + 4)
                    src = work[:, k % 2, :].rearrange("p (h d) -> p h d", d=D)
                    dve.wait_ge(w_mm, k + 1)
                    if k < 4:
                        dve.tensor_copy(m_hi[:, c, :], src)
                        dve.drain()
                        dve.tensor_tensor(m_lo[:, c, :], src, m_hi[:, c, :].bitcast(F32), ALU.subtract).then_inc(w_ready, 1)
                    else:
                        dve.tensor_copy(n_w[:, c, :], src).then_inc(w_ready, 1)
                ln_vector(dve)

            @block.scalar
            def _(act):
                ln_scalar(act)

        block = ctx.enter_context(nc.Block())

        @block.sync
        def _(sp):
            def load(k):
                if counted(2 * k):
                    sp.wait_ge(scores_mm, 2 * k)
                sp.dma_start(ctxT[:, :], a["ctxT"][:, bass.ds(k * (2 * P), 2 * P)]).then_inc(ctxT_in, 16)
                if counted(k):
                    sp.wait_ge(c_ready, k)
                sp.dma_start(ctx_in[:, :, :], a["ctx"][:, bass.ds(2 * k, 2), :]).then_inc(ctx_loaded, 16)

            load(0)
            with sp.Fori(1, N) as k:
                load(k)

        @block.gpsimd
        def _(pool):
            def body(i, has_previous, has_next):
                for t in range(2):
                    pool.wait_ge(den_ready, 2 * i + t + 1)
                    p = probs[:, t, :].rearrange("p (g j) -> p g j", j=S)
                    pool.tensor_tensor(p, p, rden[:, t, :].unsqueeze(2).broadcast_to([P, 16, S]), ALU.mult).then_inc(normed, 1)

            split_on_pool(pool, a["w_moe1"], 8, 1024, s.w_hi, s.w_lo, s.staging, w_loaded, w_split)
            steps(pool, N, body)

        @block.vector
        def _(dve):
            def mask(k):
                m = mask_row[:, bass.ds(k * 256, 256)].rearrange("p (t c) -> p t c", t=2)
                return dve.tensor_scalar(mask_add[:, :, :], m, -1.0, MASKED, ALU.add, ALU.mult).then_inc(mask_ready, 1)

            def low_part(k):
                dve.wait_ge(zT_hi_ready, k + 1)
                dve.tensor_tensor(zT_lo[:, :], turned[:, 0:2 * P], zT_hi[:, :].bitcast(F32), ALU.subtract).then_inc(zT_ready, 1)

            def context_low(k):
                dve.wait_ge(c_hi_ready, k + 1)
                for b in range(2):
                    rows = slice(64 * b, 64 * b + 64)
                    last = dve.tensor_tensor(c_lo[rows, :, b, :], ctx_in[rows, :, :], c_hi[rows, :, b, :].bitcast(F32), ALU.subtract)
                last.then_inc(c_ready, 1)

            def update(k):
                dve.wait_ge(y_mm, k + 1)
                xt = s.x[:, bass.ds(2 * k, 2), :]
                dve.scalar_tensor_tensor(out=xt, in0=turned[:, 0:2 * P].rearrange("p (t c) -> p t c", t=2),
                                         scalar=s.gates[:, 1:2], in1=xt, op0=ALU.mult, op1=ALU.add).then_inc(x_new, 1)

            mask(0)
            normalized(dve, s, z, 0, 2).then_inc(z_ready, 1)
            low_part(0)

            def body(i, has_previous, has_next):
                if has_next:
                    dve.wait_ge(zT_mm, i + 1)
                    normalized(dve, s, z, 2 * i + 2, 2).then_inc(z_ready, 1)
                for t in range(2):
                    if counted(4 * i - 2 + 2 * t):
                        dve.wait_ge(pT_mm, 4 * i - 2 + 2 * t)
                    dve.wait_ge(scores_mm, 2 * i + t + 1)
                    softmax_shifted(dve, probs[:, t, :], scores[:, t, :, :, :].rearrange("p (g r) b j -> p g (r b) j", g=4),
                                    top[:, t, :]).then_inc(shifted, 1)
                    if t == 0:
                        if has_previous:
                            update(i - 1)
                    elif has_next:
                        mask(i + 1)
                        low_part(i + 1)
                context_low(i)
                for t in range(2):
                    dve.wait_ge(exped, 2 * i + t + 1)
                    dve.tensor_reduce(den[:, t, :], probs[:, t, :].rearrange("p (g j) -> p g j", j=S), X, ALU.add)
                    dve.drain()
                    dve.reciprocal(rden[:, t, :], den[:, t, :]).then_inc(den_ready, 1)
                for t in range(2):
                    for half in range(2):
                        c = slice(half * 512, half * 512 + 512)
                        dve.wait_ge(pT_hi_ready, 4 * i + 2 * t + half + 1)
                        dve.tensor_tensor(pT_lo[:, c], scores[:, t, 4 * half:4 * half + 4, :, :].rearrange("p r b j -> p (r b j)"),
                                          pT_hi[:, c].bitcast(F32), ALU.subtract).then_inc(pT_ready, 1)
                    for half in range(2):
                        for b in range(2):
                            n = 8 * i + 4 * t + 2 * half + b
                            dve.wait_ge(u_mm, n + 1)
                            if counted(i):
                                dve.wait_ge(out_mm, i)
                            at = t * P + b * S
                            dve.tensor_copy(u[:, 8 * half:8 * half + 8, at:at + S],
                                            work[:, b, :].rearrange("p (h i) -> p h i", i=S)).then_inc(u_ready, 1)

            steps(dve, N, body)
            update(N - 1)

        @block.scalar
        def _(act):
            def high_part(k):
                act.wait_ge(zT_mm, k + 1)
                if counted(8 * k):
                    act.wait_ge(g_mm, 8 * k)
                act.activation(zT_hi[:, :], turned[:, 0:2 * P], ACT.Copy, bias=0.0).then_inc(zT_hi_ready, 1)

            def keep_g(k, chunks):
                for c in chunks:
                    act.wait_ge(g_mm, 8 * k + c + 1)
                    act.activation(g[:, 2 * c:2 * c + 2, :], work[:, c % 2, :].rearrange("p (h i) -> p h i", h=2), ACT.Copy,
                                   bias=0.0).then_inc(g_ready, 1)

            def output_turned(k):
                act.wait_ge(out_mm, k + 1)
                act.activation(yT[:, :], out_sum[:, 0:2 * P], ACT.Identity, bias=b_out[:, 0:1]).then_inc(yT_ready, 1)

            def context_high(k):
                act.wait_ge(ctx_loaded, 16 * (k + 1))
                if counted(8 * k):
                    act.wait_ge(u_mm, 8 * k)
                for b in range(2):
                    rows = slice(64 * b, 64 * b + 64)
                    last = act.activation(c_hi[rows, :, b, :], ctx_in[rows, :, :], ACT.Copy, bias=0.0)
                last.then_inc(c_hi_ready, 1)

            high_part(0)
            keep_g(0, range(8))

            def body(i, has_previous, has_next):
                context_high(i)
                if has_previous:
                    output_turned(i - 1)
                if has_next:
                    high_part(i + 1)
                for t in range(2):
                    act.wait_ge(shifted, 2 * i + t + 1)
                    act.activation(probs[:, t, :], probs[:, t, :], ACT.Exp, bias=0.0, scale=SCALE).then_inc(exped, 1)
                    if has_next:
                        keep_g(i + 1, range(4 * t, 4 * t + 4))
                for t in range(2):
                    for half in range(2):
                        act.wait_ge(pT_mm, 4 * i + 2 * t + half + 1)
                        if counted(8 * i + 4 * t):
                            act.wait_ge(u_mm, 8 * i + 4 * t)
                        act.activation(pT_hi[:, half * 512:half * 512 + 512],
                                       scores[:, t, 4 * half:4 * half + 4, :, :].rearrange("p r b j -> p (r b j)"), ACT.Copy,
                                       bias=0.0).then_inc(pT_hi_ready, 1)

            steps(act, N, body)
            output_turned(N - 1)

        @block.tensor
        def _(pe):
            def turn_z(k):
                pe.wait_ge(z_ready, k + 1)
                for t in range(2):
                    last = pe.transpose(turned[:, t * P:(t + 1) * P], z[:, t, :], s.ident[:, :])
                last.then_inc(zT_mm, 1)

            def make_g(k):
                pe.wait_ge(zT_ready, k + 1)
                for c in range(8):
                    if counted(8 * k + c - 1):
                        pe.wait_ge(g_ready, 8 * k + c - 1)
                    for q in range(2):
                        h = 2 * c + q
                        dst = work[:, c % 2, q * 256:q * 256 + 256]
                        pe.matmul(dst, m_hi[:, h, :], zT_hi[:, :], start=True, stop=False)
                        pe.matmul(dst, m_hi[:, h, :], zT_lo[:, :], start=False, stop=False)
                        last = pe.matmul(dst, m_lo[:, h, :], zT_hi[:, :], start=False, stop=True)
                    last.then_inc(g_mm, 1)

            def turn_y(k):
                pe.wait_ge(yT_ready, k + 1)
                for t in range(2):
                    last = pe.transpose(turned[:, t * P:(t + 1) * P], yT[:, t * P:(t + 1) * P], s.ident[:, :])
                last.then_inc(y_mm, 1)

            turn_z(0)
            make_g(0)

            def body(i, has_previous, has_next):
                pe.wait_ge(ctxT_in, 16 * (i + 1))
                pe.wait_ge(mask_ready, i + 1)
                pe.wait_ge(g_ready, 8 * i + 8)
                for t in range(2):
                    if counted(4 * i - 2 + 2 * t):
                        pe.wait_ge(pT_ready, 4 * i - 2 + 2 * t)
                    for half in range(2):
                        pe.matmul(scores[:, t, 4 * half:4 * half + 4, :, :].rearrange("p r b j -> p r (b j)"), ones[:, :],
                                  mask_add[:, t, :].unsqueeze(1).broadcast_to([1, 4, P]), start=True, stop=False,
                                  skip_group_check=True)
                        for h in range(8 * half, 8 * half + 8):
                            for b in range(2):
                                at = t * P + b * S
                                rows = slice(64 * (h % 2), 64 * (h % 2) + 64)
                                last = pe.matmul(scores[rows, t, h // 2, b, :], g[:, h, at:at + S], ctxT[:, at:at + S],
                                                 start=False, stop=True, skip_group_check=True)
                    last.then_inc(scores_mm, 1)
                if has_previous:
                    turn_y(i - 1)
                    if counted(i):
                        pe.wait_ge(x_new, i)
                if has_next:
                    turn_z(i + 1)
                    if counted(8 * i):
                        pe.wait_ge(u_ready, 8 * i)
                    make_g(i + 1)
                for t in range(2):
                    pe.wait_ge(normed, 2 * i + t + 1)
                    for half in range(2):
                        for pr in range(4 * half, 4 * half + 4):
                            last = pe.transpose(scores[:, t, pr, :, :].rearrange("p b j -> p (b j)"), probs[:, t, pr * P:(pr + 1) * P],
                                                s.ident[:, :])
                        last.then_inc(pT_mm, 1)
                    pe.wait_ge(c_ready, i + 1)
                    if t == 0 and has_next:
                        pe.wait_ge(g_ready, 8 * i + 16)
                    for half in range(2):
                        pe.wait_ge(pT_ready, 4 * i + 2 * t + half + 1)
                        c = slice(half * 512, half * 512 + 512)
                        for b in range(2):
                            n = 8 * i + 4 * t + 2 * half + b
                            if counted(n - 1):
                                pe.wait_ge(u_ready, n - 1)
                            pe.matmul(work[:, b, :], c_hi[:, t, b, :], pT_hi[:, c], start=True, stop=False)
                            pe.matmul(work[:, b, :], c_hi[:, t, b, :], pT_lo[:, c], start=False, stop=False)
                            pe.matmul(work[:, b, :], c_lo[:, t, b, :], pT_hi[:, c], start=False, stop=True).then_inc(u_mm, 1)
                if counted(i):
                    pe.wait_ge(yT_ready, i)
                pe.wait_ge(u_ready, 8 * i + 8)
                for h in range(16):
                    last = pe.matmul(out_sum[:, 0:2 * P], n_w[:, h, :], u[:, h, :], start=(h == 0), stop=(h == 15))
                last.then_inc(out_mm, 1)

            steps(pe, N, body)
            turn_y(N - 1)


def experts_1(nc, s, a):
    N, C = NT // 4, 32
    LAG = 3
    DOWN = 4096

    with ExitStack() as ctx:
        def sb(name, shape, dt=F32):
            return ctx.enter_context(nc.sbuf_tensor("e1_" + name, shape, dt))

        def ps(name, shape, dt=F32):
            return ctx.enter_context(nc.psum_tensor("e1_" + name, shape, dt))

        def sem(name):
            return ctx.enter_context(nc.semaphore("e1_" + name))

        router = sb("router", [P, 8])
        b1 = sb("b1", [P, C])
        b2, b2_rest, b2_parts = sb("b2", [3, 8 * D]), sb("b2_rest", [3, 8 * D]), sb("b2_parts", [3, 8 * D], BF16)
        b2_part, part_mask = sb("b2_part", [3, 8 * D], BF16), sb("part_mask", [3, 3])
        ones = sb("ones", [3, P], BF16)
        z = sb("z", [P, 4, D])
        zT = sb("zT", [P, 2, 512])
        zT_hi, zT_lo = sb("zT_hi", [P, 2, 512], F32R), sb("zT_lo", [P, 2, 512], F32R)
        hidden = sb("hidden", [P, 4, 512])
        w2 = sb("w2", [P, C, D])
        scaled, acc = sb("scaled", [P, 2, 4, D]), sb("acc", [P, 2, 4, D])
        tmp = Shared()
        tmp.larger, tmp.equal = sb("larger", [P, 4, 8, 8]), sb("equal", [P, 4, 8, 8])
        tmp.rank, tmp.sel = sb("rank", [P, 4, 8]), sb("sel", [P, 4, 8])
        logit, shifted = sb("logit", [P, 4, 8]), sb("shifted", [P, 4, 8])
        total, weights = sb("total", [P, 4]), sb("weights", [P, 2, 4, 8])

        up, sums = ps("up", [P, 4, 512]), ps("sums", [P, 2, 4, D])
        logits_ps, turned = ps("logits", [P, 512]), ps("turned", [P, 512])

        loaded, consts = sem("loaded"), sem("consts")
        up_mm, hidden_ready, down_mm = sem("up_mm"), sem("hidden_ready"), sem("down_mm")
        sums_mm, scaled_ready, added = sem("sums_mm"), sem("scaled_ready"), sem("added")
        x_new, stored = sem("x_new"), sem("stored")
        z_ready, zT_mm, zT_hi_ready, zT_ready = sem("z_ready"), sem("zT_mm"), sem("zT_hi_ready"), sem("zT_ready")
        logits_mm, logits_read, exp_in, exp_out = sem("logits_mm"), sem("logits_read"), sem("exp_in"), sem("exp_out")
        ln_vector, ln_scalar = layernorm_statistics(s, sem)
        block = ctx.enter_context(nc.Block())

        small = [(router[:, :], a["router1"]), (b1[:, :], a["b1"]), (b2[:, :], a["b2"].broadcast_to([3, 8 * D])),
                 (part_mask[:, :], a["part_mask"]),
                 (w2[:, :, :], a["w_moe1"][:, DOWN:DOWN + C * D].rearrange("p (c d) -> p c d", d=D))]

        @block.sync
        def _(sp):
            for dst, src in small:
                sp.dma_start(dst, src).then_inc(loaded, 16)
            with sp.Fori(0, N) as n:
                sp.wait_ge(x_new, n + 1)
                sp.dma_start(s.out[:, bass.ds(4 * n, 4), :], s.x[:, bass.ds(4 * n, 4), :]).then_inc(stored, 16)
            sp.wait_ge(stored, 16 * N)

        @block.gpsimd
        def _(pool):
            def body(i, has_previous, has_next):
                for u in range(2):
                    n = 2 * i + u
                    for e in range(1, 8):
                        if counted(7 * n + e - 1):
                            pool.wait_ge(added, 7 * n + e - 1)
                        pool.wait_ge(scaled_ready, 8 * n + e + 1)
                        pool.tensor_tensor(acc[:, u, :, :], acc[:, u, :, :], scaled[:, e % 2, :, :], ALU.add).then_inc(added, 1)

            steps(pool, N // 2, body)

        @block.tensor
        def _(pe):
            pe.wait_ge(loaded, 16 * len(small))
            pe.wait_ge(consts, 1)

            def turn_z(n):
                pe.wait_ge(z_ready, n + 1)
                if counted(n):
                    pe.wait_ge(zT_ready, n)
                for t in range(4):
                    last = pe.transpose(turned[:, t * P:(t + 1) * P], z[:, t, :], s.ident[:, :])
                last.then_inc(zT_mm, 1)

            def logits(n, u):
                pe.wait_ge(zT_ready, n + 1)
                if counted(n):
                    pe.wait_ge(logits_read, n)
                for t in range(4):
                    last = pe.matmul(logits_ps[:, 8 * t:8 * t + 8], zT[:, u, t * P:(t + 1) * P], router[:, :], start=True, stop=True)
                last.then_inc(logits_mm, 1)

            def down_product(n, q):
                e, c = q // 4, q % 4
                if c == 0:
                    if counted(8 * n + e - 1):
                        pe.wait_ge(scaled_ready, 8 * n + e - 1)
                    pe.matmul(sums[:, e % 2, :, :].rearrange("p t d -> p (t d)"), ones[:, :],
                              b2_parts[:, e * D:(e + 1) * D].unsqueeze(1).broadcast_to([3, 4, D]), start=True, stop=False,
                              skip_group_check=True)
                pe.wait_ge(hidden_ready, C * n + q + 1)
                for t in range(4):
                    last = pe.matmul(sums[:, e % 2, t, :], hidden[:, q % 4, t * P:(t + 1) * P], w2[:, q, :], start=False,
                                     stop=(c == 3), skip_group_check=True)
                last.then_inc(down_mm, 1)

            turn_z(0)
            logits(0, 0)

            def body(i, has_previous, has_next):
                for u in range(2):
                    n = 2 * i + u
                    prev, nxt = has_previous or u == 1, has_next or u == 0
                    for q in range(C):
                        w = slice(q * P, (q + 1) * P)
                        dst = up[:, q % 4, :]
                        if counted(C * n + q - 3):
                            pe.wait_ge(hidden_ready, C * n + q - 3)
                        pe.matmul(dst, s.w_hi[:, w], zT_hi[:, u, :], start=True, stop=False)
                        pe.matmul(dst, s.w_hi[:, w], zT_lo[:, u, :], start=False, stop=False)
                        pe.matmul(dst, s.w_lo[:, w], zT_hi[:, u, :], start=False, stop=True).then_inc(up_mm, 1)
                        if q >= LAG:
                            down_product(n, q - LAG)
                        elif prev:
                            down_product(n - 1, C - LAG + q)
                        if q == 6 and nxt:
                            turn_z(n + 1)
                        if q == 12 and nxt:
                            logits(n + 1, 1 - u)

            steps(pe, N // 2, body)
            for q in range(C - LAG, C):
                down_product(N - 1, q)

        @block.scalar
        def _(act):
            ln_scalar(act)

            def high_part(n, u):
                act.wait_ge(zT_mm, n + 1)
                act.activation(zT_hi[:, u, :], turned[:, :], ACT.Copy, bias=0.0)
                act.activation(zT[:, u, :], turned[:, :], ACT.Copy, bias=0.0).then_inc(zT_hi_ready, 1)

            def exponential(n):
                act.wait_ge(exp_in, n + 1)
                act.activation(shifted[:, :, :], shifted[:, :, :], ACT.Exp, bias=0.0).then_inc(exp_out, 1)

            high_part(0, 0)
            exponential(0)

            def body(i, has_previous, has_next):
                for u in range(2):
                    n = 2 * i + u
                    prev, nxt = has_previous or u == 1, has_next or u == 0
                    for q in range(C):
                        act.wait_ge(up_mm, C * n + q + 1)
                        if counted(C * n + q - 3):
                            act.wait_ge(down_mm, C * n + q - 3)
                        act.activation(hidden[:, q % 4, :], up[:, q % 4, :], ACT.Gelu, bias=b1[:, q:q + 1]).then_inc(hidden_ready, 1)
                        if q == 8 and nxt:
                            high_part(n + 1, 1 - u)
                        if q == 24 and nxt:
                            exponential(n + 1)

            steps(act, N // 2, body)

        @block.vector
        def _(dve):
            dve.wait_ge(loaded, 16 * len(small))
            dve.memset(ones[:, :], 1.0)
            dve.tensor_copy(b2_part[:, :], b2[:, :])
            dve.drain()
            dve.tensor_scalar(b2_parts[:, :], b2_part[:, :], part_mask[:, 0:1], None, ALU.mult)
            for k in range(1, 3):
                dve.tensor_tensor(b2[:, :], b2[:, :], b2_part[:, :], ALU.subtract)
                dve.drain()
                dve.tensor_copy(b2_part[:, :], b2[:, :])
                dve.drain()
                last = dve.scalar_tensor_tensor(out=b2_parts[:, :], in0=b2_part[:, :], scalar=part_mask[:, k:k + 1],
                                                in1=b2_parts[:, :], op0=ALU.mult, op1=ALU.add)
                if k == 2:
                    last.then_inc(consts, 1)
                dve.drain()
            ln_vector(dve)

            def low_part(n, u):
                dve.wait_ge(zT_hi_ready, n + 1)
                dve.tensor_tensor(zT_lo[:, u, :], turned[:, :], zT_hi[:, u, :].bitcast(F32), ALU.subtract).then_inc(zT_ready, 1)

            def route(n):
                dve.wait_ge(logits_mm, n + 1)
                dve.tensor_copy(logit[:, :, :], logits_ps[:, 0:32].rearrange("p (t e) -> p t e", t=4)).then_inc(logits_read, 1)
                dve.drain()
                dve.tensor_reduce(total[:, :], logit[:, :, :], X, ALU.max)
                chosen(dve, s, tmp, logit[:, :, :], 2)
                dve.tensor_tensor(shifted[:, :, :], logit[:, :, :], total[:, :].unsqueeze(2).broadcast_to([P, 4, 8]),
                                  ALU.subtract).then_inc(exp_in, 1)

            def weigh(n, u):
                dve.wait_ge(exp_out, n + 1)
                dve.tensor_tensor(shifted[:, :, :], shifted[:, :, :], tmp.sel[:, :, :], ALU.mult)
                dve.drain()
                dve.tensor_reduce(total[:, :], shifted[:, :, :], X, ALU.add)
                dve.drain()
                dve.reciprocal(total[:, :], total[:, :])
                dve.drain()
                dve.tensor_tensor(weights[:, u, :, :], shifted[:, :, :], total[:, :].unsqueeze(2).broadcast_to([P, 4, 8]), ALU.mult)
                dve.drain()

            def scale(n, e, u):
                dve.wait_ge(down_mm, C * n + 4 * e + 4)
                dst = scaled[:, e % 2, :, :]
                if e:
                    if counted(7 * n + (e - 2 if e >= 2 else 0)):
                        dve.wait_ge(added, 7 * n + (e - 2 if e >= 2 else 0))
                else:
                    dst = acc[:, u, :, :]
                dve.tensor_tensor(dst, sums[:, e % 2, :, :], weights[:, u, :, e].unsqueeze(2).broadcast_to([P, 4, D]),
                                  ALU.mult).then_inc(scaled_ready, 1)

            def update(n, u):
                dve.wait_ge(added, 7 * n + 7)
                xt = s.x[:, bass.ds(4 * n, 4), :]
                dve.scalar_tensor_tensor(out=xt, in0=acc[:, u, :, :], scalar=s.gates[:, 3:4], in1=xt, op0=ALU.mult,
                                         op1=ALU.add).then_inc(x_new, 1)

            normalized(dve, s, z, 0, 4).then_inc(z_ready, 1)
            low_part(0, 0)
            route(0)
            weigh(0, 0)

            def body(i, has_previous, has_next):
                for u in range(2):
                    n = 2 * i + u
                    prev, nxt = has_previous or u == 1, has_next or u == 0
                    if nxt:
                        dve.wait_ge(zT_mm, n + 1)
                        normalized(dve, s, z, 4 * n + 4, 4).then_inc(z_ready, 1)
                    if prev:
                        scale(n - 1, 7, 1 - u)
                    for e in range(7):
                        if e == 1 and prev:
                            update(n - 1, 1 - u)
                        if e == 2 and nxt:
                            low_part(n + 1, 1 - u)
                        if e == 4 and nxt:
                            route(n + 1)
                        if e == 6 and nxt:
                            weigh(n + 1, 1 - u)
                        scale(n, e, u)

            steps(dve, N // 2, body)
            scale(N - 1, 7, 1)
            update(N - 1, 1)


def build(nc, a, out):
    s = Shared()
    s.out = out
    with ExitStack() as ctx:
        def sb(name, shape, dt=F32):
            return ctx.enter_context(nc.sbuf_tensor(name, shape, dt))

        s.x = sb("x_sb", [P, NT, D])
        s.ident, s.gates, s.tri = sb("ident_sb", [P, P]), sb("gates_sb", [P, 4]), sb("tri_sb", [P, 8, 8])
        s.stats, s.mean, s.var = sb("ln_stats", [P, NT, 6]), sb("ln_mean", [P, NT]), sb("ln_var", [P, NT])
        s.root, s.rstd = sb("ln_root", [P, NT]), sb("ln_rstd", [P, NT])
        s.w_hi, s.w_lo = sb("w_hi", [P, 8192], F32R), sb("w_lo", [P, 8192], F32R)
        s.staging = sb("staging", [P, 2, 1280])
        setup(nc, s, a)
        for stage in STEPS:
            stage(nc, s, a)


class Shared:
    pass


STEPS = [attention_0, experts_0, attention_1, experts_1]


def laid_out(inputs):
    v = {k: np.asarray(x) for k, x in inputs.items()}
    c = np.ascontiguousarray
    E0, I0 = 32, 64
    E1, F1 = 8, 512
    tokens = lambda t: c(t.reshape(NT, P, D).transpose(1, 0, 2))
    wkv = v["L1_xattn_Wkv"]
    heads = lambda w: c(w.reshape(16, 64, D).transpose(1, 0, 2))
    down = v["L0_ffn_expert_down"].transpose(0, 2, 1).reshape(16, P, D).transpose(1, 0, 2).reshape(P, 16 * D)
    shared_down = np.zeros((P, D), np.float32)
    shared_down[0:I0] = v["L0_ffn_shared_down_w"].T
    pick = np.zeros((3, E0, 16, 2, I0), np.float32)
    for e in range(E0):
        pick[:, e, e // 2, e % 2, :] = 1
    place = np.zeros((2, 64, 2, 2, 64), np.float32)
    for b in range(2):
        for h in range(2):
            place[h, :, b, b, :] = np.eye(64)
    head_mask = np.zeros((4, 4, 8, 4), np.float32)
    for r in range(4):
        head_mask[:, r, :, r] = 1
    return {
        "x": tokens(v["x"]), "ctx": tokens(v["ctx_1024"]), "ctxT": c(v["ctx_1024"].reshape(B * S, D).T),
        "mask": c(v["mask_BxS2_bf1"]).view(np.uint8).reshape(1, B * S),
        "g_xattn": v["g_xattn"], "g_ffn": v["g_ffn"],
        "wq0T": c(v["L0_xattn_Wq"].T), "wk0T": c(v["L0_xattn_Wk"].T), "wv0T": c(v["L0_xattn_Wv"].T),
        "bq0": v["L0_xattn_bq"].reshape(D, 1), "bk0": v["L0_xattn_bk"].reshape(D, 1), "bv0": v["L0_xattn_bv"],
        "router0": c(v["L0_ffn_gate_w"].T),
        "w_moe0": c(np.concatenate([v["L0_ffn_expert_gate"].reshape(E0 * I0, D).T, v["L0_ffn_shared_gate_w"].T,
                                    v["L0_ffn_expert_up"].reshape(E0 * I0, D).T, v["L0_ffn_shared_up_w"].T,
                                    down, shared_down], 1)),
        "wq1": heads(v["L1_xattn_Wq"]), "wk1": heads(wkv[:1024]), "wv1": heads(wkv[1024:]),
        "wo1": heads(v["L1_xattn_Wout"].T), "bo1": v["L1_xattn_b_out"].reshape(D, 1),
        "router1": c(v["L1_ffn_router_w"].T),
        "w_moe1": c(np.concatenate([v["L1_ffn_w1"].reshape(E1 * F1, D).T,
                                    v["L1_ffn_w2"].transpose(0, 2, 1).reshape(32, P, D).transpose(1, 0, 2).reshape(P, 32 * D)], 1)),
        "b1": c(v["L1_ffn_b1"].reshape(32, P).T), "b2": c(v["L1_ffn_b2"].reshape(1, E1 * D)),
        "ident": np.eye(P, dtype=np.float32), "head_mask": head_mask.reshape(P, 4), "place": place.reshape(P, 2, P),
        "tri": c(np.broadcast_to(np.tril(np.ones((8, 8), np.float32), -1), (P, 8, 8))),
        "pick": c(pick.reshape(96, 16, P)), "part_mask": np.eye(3, dtype=np.float32),
    }


def kernel(**inputs):
    import concourse.bacc as bacc
    from concourse.bass_utils import run_bass_kernel_spmd

    nc = bacc.Bacc("TRN2", target_bir_lowering=False, num_devices=1)
    arrays = {f"in_{name}": v for name, v in laid_out(inputs).items()}
    a = {name[3:]: nc.dram_tensor(name, v.shape, mybir.dt.from_np(v.dtype), kind="ExternalInput").ap()
         for name, v in arrays.items()}
    out = nc.dram_tensor("out", (P, NT, D), F32, kind="ExternalOutput").ap()
    build(nc, a, out)
    got = run_bass_kernel_spmd(nc, [arrays], core_ids=[0]).results[0]["out"]
    return np.ascontiguousarray(got.reshape(P, NT, D).transpose(1, 0, 2)).reshape(B, S, D)
```

```python
from contextlib import ExitStack

import numpy as np

import concourse.bass as bass
from concourse import mybir

F32 = mybir.dt.float32
F32R = mybir.dt.float32r
BF16 = mybir.dt.bfloat16
U8 = mybir.dt.uint8
ALU = mybir.AluOpType
ACT = mybir.ActivationFunctionType
X = mybir.AxisListType.X

P = 128
B, S, D = 128, 64, 128
NT = B * S // P
EPS = 1e-5


def counted(value):
    return not isinstance(value, int) or value > 0


def steps(eng, n, body):
    body(0, False, True)
    body(1, True, True)
    with eng.Fori(2, n - 1) as i:
        body(i, True, True)
    body(n - 1, True, False)


def layernorm_statistics(s, sem):
    sq_in, sq_out = sem("ln_variance_ready"), sem("ln_root_ready")

    def on_vector(dve):
        with dve.Fori(0, NT // 8) as k:
            for u in range(8):
                dve.bn_stats(s.stats[:, bass.ds(k * 8 + u, 1), :], s.x[:, bass.ds(k * 8 + u, 1), :])
        dve.drain()
        mean_even, mean_odd = s.stats[:, :, 1], s.stats[:, :, 4]
        dve.tensor_tensor(s.mean[:, :], mean_even, mean_odd, ALU.add)
        dve.tensor_tensor(s.rstd[:, :], mean_even, mean_odd, ALU.subtract)
        dve.tensor_tensor(s.var[:, :], s.stats[:, :, 2], s.stats[:, :, 5], ALU.add)
        dve.drain()
        dve.tensor_scalar(s.mean[:, :], s.mean[:, :], 0.5, None, ALU.mult)
        dve.tensor_tensor(s.rstd[:, :], s.rstd[:, :], s.rstd[:, :], ALU.mult)
        dve.tensor_scalar(s.var[:, :], s.var[:, :], 1.0 / D, EPS, ALU.mult, ALU.add)
        dve.drain()
        dve.scalar_tensor_tensor(out=s.var[:, :], in0=s.rstd[:, :], scalar=0.25, in1=s.var[:, :],
                                 op0=ALU.mult, op1=ALU.add).then_inc(sq_in, 1)
        dve.wait_ge(sq_out, 1)
        dve.reciprocal(s.rstd[:, :], s.root[:, :])
        dve.drain()

    def on_scalar(act):
        act.wait_ge(sq_in, 1)
        act.activation(s.root[:, :], s.var[:, :], ACT.Sqrt, bias=0.0).then_inc(sq_out, 1)

    return on_vector, on_scalar


def split_on_pool(pool, source, chunks, width, hi, lo, staging, loaded, split):
    for k in range(chunks + 1):
        if k < chunks:
            if counted(k - 1):
                pool.wait_ge(split, k - 1)
            pool.dma_start(staging[:, k % 2, 0:width], source[:, k * width:(k + 1) * width]).then_inc(loaded[k % 2], 16)
        if k:
            c = slice((k - 1) * width, k * width)
            part = staging[:, (k - 1) % 2, 0:width]
            pool.wait_ge(loaded[(k - 1) % 2], 16 * ((k - 1) // 2 + 1))
            pool.tensor_copy(hi[:, c], part)
            pool.drain()
            pool.tensor_tensor(lo[:, c], part, hi[:, c].bitcast(F32), ALU.subtract).then_inc(split, 1)


def normalized(dve, s, z, k, n):
    for t in range(n):
        last = dve.tensor_scalar(z[:, t, :], s.x[:, bass.ds(k + t, 1), :], s.mean[:, bass.ds(k + t, 1)],
                                 s.rstd[:, bass.ds(k + t, 1)], ALU.subtract, ALU.mult)
    return last


def setup(nc, s, a):
    with ExitStack() as ctx:
        loaded = ctx.enter_context(nc.semaphore("loaded"))
        gates = ctx.enter_context(nc.semaphore("gates"))
        block = ctx.enter_context(nc.Block())
        pieces = [(s.x[:, 16 * k:16 * k + 16, :], a["x"][:, 16 * k:16 * k + 16, :]) for k in range(4)]
        pieces += [(s.ident[:, :], a["ident"]), (s.gates[:, 0:2], a["g_xattn"].partition_broadcast(P)),
                   (s.gates[:, 2:4], a["g_ffn"].partition_broadcast(P)), (s.tri[:, :, :], a["tri"])]

        @block.sync
        def _(sp):
            for dst, src in pieces:
                sp.dma_start(dst, src).then_inc(loaded, 16)
            sp.wait_ge(loaded, 16 * len(pieces))

        @block.scalar
        def _(act):
            act.wait_ge(loaded, 16 * len(pieces))
            act.activation(s.gates[:, :], s.gates[:, :], ACT.Tanh, bias=0.0).then_inc(gates, 1)
            act.wait_ge(gates, 1)


def score_tops(dve, top, scores):
    dve.tensor_reduce(top, scores.rearrange("p (g j) -> p g j", j=S), X, ALU.max)
    dve.drain()


def less_tops(dve, out, scores, top):
    return dve.tensor_tensor(out.rearrange("p (g j) -> p g j", j=S), scores.rearrange("p (g j) -> p g j", j=S),
                             top.unsqueeze(2).broadcast_to([P, 16, S]), ALU.subtract)


def softmax_shifted(dve, out, scores, top):
    score_tops(dve, top, scores)
    return less_tops(dve, out, scores, top)


def attention_0(nc, s, a):
    N = NT // 2
    SCALE = 8.0 ** -0.5
    with ExitStack() as ctx:
        def sb(name, shape, dt=F32):
            return ctx.enter_context(nc.sbuf_tensor("a0_" + name, shape, dt))

        def ps(name, shape, dt=F32):
            return ctx.enter_context(nc.psum_tensor("a0_" + name, shape, dt))

        def sem(name):
            return ctx.enter_context(nc.semaphore("a0_" + name))

        wq, wk, wv = sb("wq", [P, D]), sb("wk", [P, D]), sb("wv", [P, D])
        bq, bk, bv = sb("bq", [P, 1]), sb("bk", [P, 1]), sb("bv", [P, D])
        head_mask, bq_masked = sb("head_mask", [P, 4]), sb("bq_masked", [P, 4])
        par_mask, place = sb("par_mask", [P, 2]), sb("place", [P, 2, 2, D])
        ctxT_k, ctxT_v = sb("ctxT_k", [P, 2 * P]), sb("ctxT_v", [P, 2 * P])
        z, zT = sb("z", [P, 2, D]), sb("zT", [P, 2 * P])
        qm, kz = sb("qm", [P, 4, 4, S]), sb("kz", [P, 4, 4, S])
        vz = sb("vz", [P, 2, 8, 2, 16])
        top, den, rden = sb("top", [P, 2, 16]), sb("den", [P, 2, 16]), sb("rden", [P, 2, 16])
        below_top = sb("below_top", [P, 2, 8 * P])
        probs, probsT = sb("probs", [P, 2, 8 * P]), sb("probsT", [P, 2, 8 * P])
        heads = sb("heads", [P, 2, 2, S])

        scores = ps("scores", [P, 2, 2, 4, 2, S])
        turned = ps("turned", [P, 2, 512])
        late = ps("late", [P, 512])
        early = ps("early", [P, 512])

        loaded, consts = sem("loaded"), sem("consts")
        k_in, v_in = sem("k_in"), sem("v_in")
        z_ready, zT_mm, zT_ready = sem("z_ready"), sem("zT_mm"), sem("zT_ready")
        qk_mm, qk_ready, v_mm, v_ready = sem("qk_mm"), sem("qk_ready"), sem("v_mm"), sem("v_ready")
        scores_mm, shifted, exped = sem("scores_mm"), sem("shifted"), sem("exped")
        den_ready, normed = sem("den_ready"), sem("normed")
        pT_mm, pT_ready = sem("pT_mm"), sem("pT_ready")
        heads_mm, heads_ready, y_mm, x_new = sem("heads_mm"), sem("heads_ready"), sem("y_mm"), sem("x_new")
        w_loaded, w_split = [sem("w_loaded_even"), sem("w_loaded_odd")], sem("w_split")
        ln_vector, ln_scalar = layernorm_statistics(s, sem)
        block = ctx.enter_context(nc.Block())
        small = [(wq[:, :], a["wq0T"]), (wk[:, :], a["wk0T"]), (wv[:, :], a["wv0T"]), (bq[:, :], a["bq0"]),
                 (bk[:, :], a["bk0"]), (bv[:, :], a["bv0"].partition_broadcast(P)),
                 (head_mask[:, :], a["head_mask"]), (par_mask[:, :], a["par_mask"]), (place[:, :, :, :], a["place"])]

        @block.sync
        def _(sp):
            for dst, src in small:
                sp.dma_start(dst, src).then_inc(loaded, 16)
            sp.dma_start(ctxT_k[:, :], a["ctxT"][:, 0:2 * P]).then_inc(k_in, 16)
            sp.dma_start(ctxT_v[:, :], a["ctxT"][:, 0:2 * P]).then_inc(v_in, 16)
            with sp.Fori(1, N) as k:
                sp.wait_ge(qk_mm, k)
                sp.dma_start(ctxT_k[:, :], a["ctxT"][:, bass.ds(k * (2 * P), 2 * P)]).then_inc(k_in, 16)
                sp.wait_ge(v_mm, k)
                sp.dma_start(ctxT_v[:, :], a["ctxT"][:, bass.ds(k * (2 * P), 2 * P)]).then_inc(v_in, 16)

        @block.gpsimd
        def _(pool):
            def body(i, has_previous, has_next):
                for t in range(2):
                    pool.wait_ge(den_ready, 2 * i + t + 1)
                    p = probs[:, t, :].rearrange("p (g j) -> p g j", j=S)
                    pool.tensor_tensor(p, p, rden[:, t, :].unsqueeze(2).broadcast_to([P, 16, S]), ALU.mult).then_inc(normed, 1)

            split_on_pool(pool, a["w_moe0"], 5, 1280, s.w_hi, s.w_lo, s.staging, w_loaded, w_split)
            steps(pool, N, body)

        @block.vector
        def _(dve):
            dve.memset(kz[:, :, :, :], 0.0)
            dve.memset(vz[:, :, :, :, :], 0.0)
            ln_vector(dve)
            dve.wait_ge(loaded, 16 * len(small))
            dve.tensor_scalar(bq_masked[:, :], head_mask[:, :], bq[:, 0:1], None, ALU.mult).then_inc(consts, 1)

            def values(k):
                dve.wait_ge(v_mm, k + 1)
                for b in range(2):
                    rows = slice(64 * b, 64 * b + 64)
                    v = early[rows, 0:2 * P].rearrange("p (t a c) -> p t a c", t=2, c=16)
                    bias = bv[rows, :].rearrange("p (a c) -> p a c", c=16).unsqueeze(1).broadcast_to([64, 2, 8, 16])
                    last = dve.tensor_tensor(vz[rows, :, :, b, :], v, bias, ALU.add)
                last.then_inc(v_ready, 1)

            def softmax_top(i, t):
                dve.wait_ge(scores_mm, 2 * i + t + 1)
                score_tops(dve, top[:, t, :], scores[:, t, :, :, :, :].rearrange("p h g b j -> p (h g b j)"))

            def softmax_shift(t):
                less_tops(dve, below_top[:, t, :], scores[:, t, :, :, :, :].rearrange("p h g b j -> p (h g b j)"),
                          top[:, t, :]).then_inc(shifted, 1)

            def denominators(i, t):
                dve.wait_ge(exped, 2 * i + t + 1)
                dve.tensor_reduce(den[:, t, :], probs[:, t, :].rearrange("p (g j) -> p g j", j=S), X, ALU.add)
                dve.drain()
                dve.reciprocal(rden[:, t, :], den[:, t, :]).then_inc(den_ready, 1)

            def keep_heads(i, t):
                dve.wait_ge(heads_mm, 2 * i + t + 1)
                if counted(2 * i + t - 1):
                    dve.wait_ge(y_mm, 2 * i + t - 1)
                o = late[:, 0:2 * P].rearrange("p (h r i) -> p h r i", h=2, r=2)
                dve.tensor_scalar(heads[:, t, :, :], o[:, :, 0, :], par_mask[:, 0:1], None, ALU.mult)
                dve.drain()
                dve.scalar_tensor_tensor(out=heads[:, t, :, :], in0=o[:, :, 1, :], scalar=par_mask[:, 1:2],
                                         in1=heads[:, t, :, :], op0=ALU.mult, op1=ALU.add).then_inc(heads_ready, 1)

            def update(k):
                dve.wait_ge(y_mm, 2 * k + 2)
                xt = s.x[:, bass.ds(2 * k, 2), :]
                dve.scalar_tensor_tensor(out=xt, in0=late[:, 2 * P:4 * P].rearrange("p (t c) -> p t c", t=2),
                                         scalar=s.gates[:, 0:1], in1=xt, op0=ALU.mult, op1=ALU.add).then_inc(x_new, 1)

            normalized(dve, s, z, 0, 2).then_inc(z_ready, 1)

            def body(i, has_previous, has_next):
                if has_next:
                    dve.wait_ge(zT_mm, i + 1)
                    normalized(dve, s, z, 2 * i + 2, 2).then_inc(z_ready, 1)
                if has_previous:
                    values(i - 1)
                    denominators(i - 1, 1)
                softmax_top(i, 0)
                softmax_shift(0)
                softmax_top(i, 1)
                if has_previous:
                    keep_heads(i - 1, 0)
                softmax_shift(1)
                if has_previous:
                    keep_heads(i - 1, 1)
                denominators(i, 0)
                if has_previous:
                    update(i - 1)

            steps(dve, N, body)
            values(N - 1)
            denominators(N - 1, 1)
            keep_heads(N - 1, 0)
            keep_heads(N - 1, 1)
            update(N - 1)

        @block.scalar
        def _(act):
            ln_scalar(act)
            act.wait_ge(consts, 1)

            def normalized_transposed(k):
                act.wait_ge(zT_mm, k + 1)
                act.activation(zT[:, :], early[:, 0:2 * P], ACT.Copy, bias=0.0).then_inc(zT_ready, 1)

            def keys(k):
                act.wait_ge(qk_mm, k + 1)
                for g in range(4):
                    rows = slice(32 * g, 32 * g + 32)
                    act.activation(kz[rows, :, g, :], early[rows, 2 * P:4 * P].rearrange("p (b j) -> p b j", b=4),
                                   ACT.Identity, bias=bk[rows, 0:1])

            def queries(k):
                for r in range(4):
                    last = act.activation(qm[:, :, r, :], early[:, 0:2 * P].rearrange("p (b i) -> p b i", b=4), ACT.Identity,
                                          bias=bq_masked[:, r:r + 1], scale=head_mask[:, r:r + 1])
                last.then_inc(qk_ready, 1)

            def keep_turned(i, t):
                for half in range(2):
                    act.wait_ge(pT_mm, 4 * i + 2 * t + half + 1)
                    act.activation(probsT[:, t, half * 512:half * 512 + 512], turned[:, half, :], ACT.Copy,
                                   bias=0.0).then_inc(pT_ready, 1)

            def exponential(i, t):
                if counted(4 * i - 2 + 2 * t):
                    act.wait_ge(pT_mm, 4 * i - 2 + 2 * t)
                act.wait_ge(shifted, 2 * i + t + 1)
                act.activation(probs[:, t, :], below_top[:, t, :], ACT.Exp, bias=0.0, scale=SCALE).then_inc(exped, 1)

            normalized_transposed(0)
            keys(0)
            queries(0)

            def body(i, has_previous, has_next):
                if has_next:
                    normalized_transposed(i + 1)
                if has_previous:
                    keep_turned(i - 1, 0)
                exponential(i, 0)
                if has_next:
                    keys(i + 1)
                if has_previous:
                    keep_turned(i - 1, 1)
                if has_next:
                    queries(i + 1)
                exponential(i, 1)

            steps(act, N, body)
            keep_turned(N - 1, 0)
            keep_turned(N - 1, 1)

        @block.tensor
        def _(pe):
            pe.wait_ge(loaded, 16 * len(small))

            def turn_z(k):
                pe.wait_ge(z_ready, k + 1)
                if counted(k - 1):
                    pe.wait_ge(v_ready, k - 1)
                for t in range(2):
                    last = pe.transpose(early[:, t * P:(t + 1) * P], z[:, t, :], s.ident[:, :])
                last.then_inc(zT_mm, 1)

            def project_qk(k):
                pe.wait_ge(zT_ready, k + 1)
                pe.wait_ge(k_in, 16 * (k + 1))
                pe.matmul(early[:, 0:2 * P], wq[:, :], zT[:, :], start=True, stop=True)
                pe.matmul(early[:, 2 * P:4 * P], wk[:, :], ctxT_k[:, :], start=True, stop=True).then_inc(qk_mm, 1)

            def project_v(k):
                pe.wait_ge(v_in, 16 * (k + 1))
                for t in range(2):
                    last = pe.matmul(early[:, t * P:(t + 1) * P], ctxT_v[:, t * P:(t + 1) * P], wv[:, :], start=True, stop=True)
                last.then_inc(v_mm, 1)

            def score(i, t):
                if counted(2 * i + t - 1):
                    pe.wait_ge(shifted, 2 * i + t - 1)
                for b in range(2):
                    for half in range(2):
                        q = qm[:, 2 * t + b, 2 * half:2 * half + 2, :].rearrange("p r i -> p (r i)")
                        last = pe.matmul(scores[:, t, half, :, b, :], q, kz[:, 2 * t + b, :, :], start=True, stop=True)
                last.then_inc(scores_mm, 1)

            def turn(i, t):
                pe.wait_ge(normed, 2 * i + t + 1)
                if counted(4 * i + 2 * t):
                    pe.wait_ge(pT_ready, 4 * i + 2 * t)
                for half in range(2):
                    for q in range(4):
                        pr = 4 * half + q
                        last = pe.transpose(turned[:, half, q * P:(q + 1) * P], probs[:, t, pr * P:(pr + 1) * P], s.ident[:, :])
                    last.then_inc(pT_mm, 1)

            def weigh_values(i, t):
                if counted(2 * i + t):
                    pe.wait_ge(heads_ready, 2 * i + t)
                if t == 0:
                    pe.wait_ge(v_ready, i + 1)
                    if counted(i):
                        pe.wait_ge(x_new, i)
                for half in range(2):
                    pe.wait_ge(pT_ready, 4 * i + 2 * t + half + 1)
                    for q in range(4):
                        pr = 4 * half + q
                        last = pe.matmul(late[32 * q:32 * q + 32, half * P:half * P + P], vz[:, t, pr, :, :].rearrange("p b c -> p (b c)"),
                                         probsT[:, t, pr * P:(pr + 1) * P], start=True, stop=True)
                last.then_inc(heads_mm, 1)

            def output(k, t):
                pe.wait_ge(heads_ready, 2 * k + t + 1)
                for b in range(2):
                    for half in range(2):
                        last = pe.matmul(late[64 * b:64 * b + 64, 2 * P + t * P:2 * P + (t + 1) * P], heads[:, t, half, :],
                                         place[:, b, half, :], start=(half == 0), stop=(half == 1))
                last.then_inc(y_mm, 1)

            turn_z(0)
            project_qk(0)

            def body(i, has_previous, has_next):
                pe.wait_ge(qk_ready, i + 1)
                if has_previous:
                    project_v(i - 1)
                score(i, 0)
                score(i, 1)
                if has_next:
                    turn_z(i + 1)
                if has_previous:
                    turn(i - 1, 0)
                if has_next:
                    project_qk(i + 1)
                if has_previous:
                    weigh_values(i - 1, 0)
                    turn(i - 1, 1)
                    output(i - 1, 0)
                    weigh_values(i - 1, 1)
                    output(i - 1, 1)

            steps(pe, N, body)
            project_v(N - 1)
            for t in range(2):
                turn(N - 1, t)
                weigh_values(N - 1, t)
                output(N - 1, t)


def chosen(dve, s, tmp, values, k):
    other = values.unsqueeze(2).broadcast_to([P, 4, 8, 8])
    own = values.unsqueeze(3).broadcast_to([P, 4, 8, 8])
    dve.tensor_tensor(tmp.larger[:, :, :, :], other, own, ALU.is_gt)
    dve.tensor_tensor(tmp.equal[:, :, :, :], other, own, ALU.is_equal)
    dve.drain()
    dve.tensor_tensor(tmp.equal[:, :, :, :], tmp.equal[:, :, :, :], s.tri[:, :, :].unsqueeze(1).broadcast_to([P, 4, 8, 8]), ALU.mult)
    dve.drain()
    dve.tensor_tensor(tmp.larger[:, :, :, :], tmp.larger[:, :, :, :], tmp.equal[:, :, :, :], ALU.add)
    dve.drain()
    dve.tensor_reduce(tmp.rank[:, :, :], tmp.larger[:, :, :, :], X, ALU.add)
    dve.drain()
    dve.tensor_scalar(tmp.sel[:, :, :], tmp.rank[:, :, :], float(k), None, ALU.is_lt)
    dve.drain()


def experts_0(nc, s, a):
    N, C = NT // 4, 17
    G, U, DN = 0, 2112, 4224

    with ExitStack() as ctx:
        def sb(name, shape, dt=F32):
            return ctx.enter_context(nc.sbuf_tensor("e0_" + name, shape, dt))

        def ps(name, shape, dt=F32):
            return ctx.enter_context(nc.psum_tensor("e0_" + name, shape, dt))

        def sem(name):
            return ctx.enter_context(nc.semaphore("e0_" + name))

        pick = sb("pick", [96, 16, P], BF16)
        identb = sb("identb", [P, P], BF16)
        router = sb("router", [P, 32])
        z = sb("z", [P, 4, D])
        zT = sb("zT", [P, 2, 512])
        zT_hi, zT_lo = sb("zT_hi", [P, 2, 512], F32R), sb("zT_lo", [P, 2, 512], F32R)
        gated, raised, hidden = sb("gated", [P, 2, 512]), sb("raised", [P, 2, 512]), sb("hidden", [P, 3, 512])
        down = sb("down", [P, C, D])
        yT = sb("yT", [P, 512])
        weightsT = sb("weightsT", [96, 2, 512], BF16)
        tmp = Shared()
        tmp.larger, tmp.equal = sb("larger", [P, 4, 8, 8]), sb("equal", [P, 4, 8, 8])
        tmp.rank, tmp.sel = sb("rank", [P, 4, 8]), sb("sel", [P, 4, 8])
        scored, groups = sb("scored", [P, 4, 32]), sb("groups", [P, 4, 8])
        masked, left, top8 = sb("masked", [P, 4, 32]), sb("left", [P, 4, 32]), sb("top8", [P, 4, 8])
        total = sb("total", [P, 4])
        parts = sb("parts", [P, 4, 3, 32], BF16)

        gate, up, spread = ps("gate", [P, 2, 512]), ps("up", [P, 2, 512]), ps("spread", [P, 2, 512])
        out_sum, turned = ps("out_sum", [P, 512]), ps("turned", [P, 512])
        turned_bf = turned[0:96, 0:256].bitcast(BF16)

        loaded, consts = sem("loaded"), sem("consts")
        gate_mm, up_mm, spread_mm, down_mm = sem("gate_mm"), sem("up_mm"), sem("spread_mm"), sem("down_mm")
        gated_ready, raised_ready, hidden_ready = sem("gated_ready"), sem("raised_ready"), sem("hidden_ready")
        yT_ready, y_mm, x_new = sem("yT_ready"), sem("y_mm"), sem("x_new")
        z_ready, zT_mm, zT_hi_ready, zT_ready = sem("z_ready"), sem("zT_mm"), sem("zT_hi_ready"), sem("zT_ready")
        logits_mm, scored_ready, parts_ready = sem("logits_mm"), sem("scored_ready"), sem("parts_ready")
        weights_mm, weights_ready = sem("weights_mm"), sem("weights_ready")
        ln_vector, ln_scalar = layernorm_statistics(s, sem)
        block = ctx.enter_context(nc.Block())

        def rows(j):
            return 128 if j < 16 else 64

        def before(n, j, ring):
            if j >= ring:
                return C * n + j - ring + 1
            return C * (n - 1) + max(m for m in range(C) if m % ring == j) + 1

        picks_in = s.staging[0:96, :, 0:1024]
        small = [(picks_in, a["pick"].rearrange("k (u j) m -> k u (j m)", u=2)), (router[:, :], a["router0"]),
                 (down[:, :, :], a["w_moe0"][:, DN:DN + C * D].rearrange("p (c d) -> p c d", d=D))]

        @block.sync
        def _(sp):
            for dst, src in small:
                sp.dma_start(dst, src).then_inc(loaded, 16)
            sp.wait_ge(loaded, 16 * len(small))

        @block.tensor
        def _(pe):
            pe.wait_ge(loaded, 16 * len(small))
            pe.wait_ge(consts, 1)

            def turn_z(n):
                pe.wait_ge(z_ready, n + 1)
                if counted(n):
                    pe.wait_ge(weights_ready, n)
                for t in range(4):
                    last = pe.transpose(turned[:, t * P:(t + 1) * P], z[:, t, :], s.ident[:, :])
                last.then_inc(zT_mm, 1)

            def logits(n, u):
                pe.wait_ge(zT_ready, n + 1)
                for t in range(4):
                    last = pe.matmul(turned[:, 32 * t:32 * t + 32], zT[:, u, t * P:(t + 1) * P], router[:, :], start=True, stop=True)
                last.then_inc(logits_mm, 1)

            def turn_weights(n):
                pe.wait_ge(parts_ready, n + 1)
                for t in range(4):
                    last = pe.transpose(turned_bf[:, t * P:(t + 1) * P], parts[:, t, :, :].rearrange("p c e -> p (c e)"), identb[:, :])
                last.then_inc(weights_mm, 1)

            def turn_y(n):
                pe.wait_ge(yT_ready, n + 1)
                for t in range(4):
                    last = pe.transpose(turned[:, t * P:(t + 1) * P], yT[:, t * P:(t + 1) * P], s.ident[:, :])
                last.then_inc(y_mm, 1)

            def product(dst, w, hi, lo, col, m, first=True):
                w_h, w_l = s.w_hi[:, col:col + m], s.w_lo[:, col:col + m]
                pe.matmul(dst, w_h, hi, start=True, stop=False)
                pe.matmul(dst, w_h, lo, start=False, stop=False)
                return pe.matmul(dst, w_l, hi, start=False, stop=True)

            def down_product(n, j):
                m = rows(j)
                pe.wait_ge(hidden_ready, C * n + j + 1)
                if j == 0:
                    if counted(n):
                        pe.wait_ge(yT_ready, n)
                pe.matmul(out_sum[:, :], down[0:m, j, :], hidden[0:m, j % 3, :], start=(j == 0), stop=(j == C - 1)).then_inc(down_mm, 1)

            turn_z(0)
            logits(0, 0)
            turn_weights(0)
            LAG = 2

            def body(i, has_previous, has_next):
                for u in range(2):
                    n = 2 * i + u
                    hi, lo = zT_hi[:, u, :], zT_lo[:, u, :]
                    prev, nxt = has_previous or u == 1, has_next or u == 0
                    for j in range(C):
                        m = rows(j)
                        if counted(before(n, j, 2)):
                            pe.wait_ge(gated_ready, before(n, j, 2))
                        product(gate[0:m, j % 2, :], None, hi, lo, G + j * P, m).then_inc(gate_mm, 1)
                        if counted(before(n, j, 2)):
                            pe.wait_ge(raised_ready, before(n, j, 2))
                        product(up[0:m, j % 2, :], None, hi, lo, U + j * P, m).then_inc(up_mm, 1)
                        if j < 16:
                            if j == 0:
                                pe.wait_ge(weights_ready, n + 1)
                            if counted(C * n + j - 1):
                                pe.wait_ge(hidden_ready, C * n + j - 1)
                            pe.matmul(spread[:, j % 2, :], pick[:, j, :], weightsT[:, u, :], start=True, stop=True).then_inc(spread_mm, 1)
                        if j >= LAG:
                            down_product(n, j - LAG)
                        elif prev:
                            down_product(n - 1, C - LAG + j)
                        if j == 3 and prev:
                            turn_y(n - 1)
                        if j == 5 and nxt:
                            if counted(n):
                                pe.wait_ge(x_new, n)
                            turn_z(n + 1)
                        if j == 8 and nxt:
                            logits(n + 1, 1 - u)
                        if j == 14 and nxt:
                            turn_weights(n + 1)

            steps(pe, N // 2, body)
            for j in range(C - LAG, C):
                down_product(N - 1, j)
            turn_y(N - 1)

        @block.scalar
        def _(act):
            ln_scalar(act)

            def high_part(n, u):
                act.wait_ge(zT_mm, n + 1)
                act.activation(zT_hi[:, u, :], turned[:, :], ACT.Copy, bias=0.0)
                act.activation(zT[:, u, :], turned[:, :], ACT.Copy, bias=0.0).then_inc(zT_hi_ready, 1)

            def score(n):
                act.wait_ge(logits_mm, n + 1)
                act.activation(scored[:, :, :], turned[:, 0:P].rearrange("p (t e) -> p t e", t=4), ACT.Sigmoid,
                               bias=0.0).then_inc(scored_ready, 1)

            def keep_weights(n, u):
                act.wait_ge(weights_mm, n + 1)
                act.activation(weightsT[:, u, :], turned_bf, ACT.Copy, bias=0.0).then_inc(weights_ready, 1)

            def keep_y(n):
                act.wait_ge(down_mm, C * (n + 1))
                act.activation(yT[:, :], out_sum[:, :], ACT.Copy, bias=0.0).then_inc(yT_ready, 1)

            high_part(0, 0)
            score(0)
            keep_weights(0, 0)

            def body(i, has_previous, has_next):
                for u in range(2):
                    n = 2 * i + u
                    prev, nxt = has_previous or u == 1, has_next or u == 0
                    for j in range(C):
                        m = rows(j)
                        act.wait_ge(gate_mm, C * n + j + 1)
                        if counted(before(n, j, 2)):
                            act.wait_ge(raised_ready, before(n, j, 2))
                        act.activation(gated[0:m, j % 2, :], gate[0:m, j % 2, :], ACT.Silu, bias=0.0).then_inc(gated_ready, 1)
                        if j == 2 and prev:
                            keep_y(n - 1)
                        if j == 6 and nxt:
                            high_part(n + 1, 1 - u)
                        if j == 9 and nxt:
                            score(n + 1)
                        if j == 15 and nxt:
                            keep_weights(n + 1, 1 - u)

            steps(act, N // 2, body)
            keep_y(N - 1)

        @block.vector
        def _(dve):
            dve.wait_ge(loaded, 16 * len(small))
            dve.tensor_copy(pick[:, :, :].rearrange("k (u j) m -> k u (j m)", u=2), picks_in)
            dve.tensor_copy(identb[:, :], s.ident[:, :]).then_inc(consts, 1)
            ln_vector(dve)

            def low_part(n, u):
                dve.wait_ge(zT_hi_ready, n + 1)
                dve.tensor_tensor(zT_lo[:, u, :], turned[:, :], zT_hi[:, u, :].bitcast(F32), ALU.subtract).then_inc(zT_ready, 1)

            def route(n):
                dve.wait_ge(scored_ready, n + 1)
                dve.tensor_reduce(groups[:, :, :], scored[:, :, :].rearrange("p t (g e) -> p t g e", e=4), X, ALU.add)
                dve.drain()
                chosen(dve, s, tmp, groups[:, :, :], 4)
                dve.tensor_tensor(masked[:, :, :].rearrange("p t (g e) -> p (t g) e", e=4),
                                  scored[:, :, :].rearrange("p t (g e) -> p (t g) e", e=4),
                                  tmp.sel[:, :, :].rearrange("p t g -> p (t g)").unsqueeze(2).broadcast_to([P, 32, 4]), ALU.mult)
                dve.drain()
                for t in range(4):
                    dve.max(top8[:, t, :], masked[:, t, :])
                dve.drain()
                for t in range(4):
                    dve.match_replace(left[:, t, :], top8[:, t, :], masked[:, t, :], 0.0)
                dve.tensor_reduce(total[:, :], top8[:, :, :], X, ALU.add)
                dve.drain()
                dve.tensor_tensor(masked[:, :, :], masked[:, :, :], left[:, :, :], ALU.subtract)
                dve.tensor_scalar(total[:, :], total[:, :], 1e-12, None, ALU.max)
                dve.drain()
                dve.reciprocal(total[:, :], total[:, :])
                dve.drain()
                dve.tensor_tensor(masked[:, :, :], masked[:, :, :], total[:, :].unsqueeze(2).broadcast_to([P, 4, 32]), ALU.mult)
                dve.drain()
                if counted(n):
                    dve.wait_ge(weights_mm, n)
                dve.tensor_copy(parts[:, :, 0, :], masked[:, :, :])
                dve.drain()
                dve.tensor_tensor(masked[:, :, :], masked[:, :, :], parts[:, :, 0, :], ALU.subtract)
                dve.drain()
                dve.tensor_copy(parts[:, :, 1, :], masked[:, :, :])
                dve.drain()
                dve.tensor_tensor(parts[:, :, 2, :], masked[:, :, :], parts[:, :, 1, :], ALU.subtract).then_inc(parts_ready, 1)

            def update(n):
                dve.wait_ge(y_mm, n + 1)
                xt = s.x[:, bass.ds(4 * n, 4), :]
                dve.scalar_tensor_tensor(out=xt, in0=turned[:, :].rearrange("p (t c) -> p t c", t=4),
                                         scalar=s.gates[:, 2:3], in1=xt, op0=ALU.mult, op1=ALU.add).then_inc(x_new, 1)

            def finish_hidden(n, j):
                m = rows(j)
                dve.wait_ge(raised_ready, C * n + j + 1)
                if counted(before(n, j, 3)):
                    dve.wait_ge(down_mm, before(n, j, 3))
                if j < 16:
                    dve.wait_ge(spread_mm, 16 * n + j + 1)
                    dve.tensor_tensor(hidden[:, j % 3, :], spread[:, j % 2, :], raised[:, j % 2, :], ALU.mult).then_inc(hidden_ready, 1)
                else:
                    dve.tensor_copy(hidden[0:m, j % 3, :], raised[0:m, j % 2, :]).then_inc(hidden_ready, 1)

            normalized(dve, s, z, 0, 4).then_inc(z_ready, 1)
            low_part(0, 0)
            route(0)

            def body(i, has_previous, has_next):
                for u in range(2):
                    n = 2 * i + u
                    prev, nxt = has_previous or u == 1, has_next or u == 0
                    for j in range(C):
                        m = rows(j)
                        dve.wait_ge(gated_ready, C * n + j + 1)
                        dve.wait_ge(up_mm, C * n + j + 1)
                        if j < 2:
                            if counted(before(n, j, 2)):
                                dve.wait_ge(hidden_ready, before(n, j, 2))
                        else:
                            if counted(C * n + j - 1):
                                dve.wait_ge(hidden_ready, C * n + j - 1)
                        dve.tensor_tensor(raised[0:m, j % 2, :], up[0:m, j % 2, :], gated[0:m, j % 2, :], ALU.mult).then_inc(raised_ready, 1)
                        if j >= 1:
                            finish_hidden(n, j - 1)
                        if j == 1 and nxt:
                            dve.wait_ge(zT_mm, n + 1)
                            normalized(dve, s, z, 4 * n + 4, 4).then_inc(z_ready, 1)
                        if j == 4 and prev:
                            update(n - 1)
                        if j == 7 and nxt:
                            low_part(n + 1, 1 - u)
                        if j == 10 and nxt:
                            route(n + 1)
                    finish_hidden(n, C - 1)

            steps(dve, N // 2, body)
            update(N - 1)


MASKED = 2.0 ** 100


def attention_1(nc, s, a):
    N = NT // 2
    SCALE = 64.0 ** -0.5
    with ExitStack() as ctx:
        def sb(name, shape, dt=F32):
            return ctx.enter_context(nc.sbuf_tensor("a1_" + name, shape, dt))

        def ps(name, shape, dt=F32):
            return ctx.enter_context(nc.psum_tensor("a1_" + name, shape, dt))

        def sem(name):
            return ctx.enter_context(nc.semaphore("a1_" + name))

        m_hi, m_lo = sb("m_hi", [P, 16, D], F32R), sb("m_lo", [P, 16, D], F32R)
        n_w = sb("n_w", [P, 16, D])
        b_out = sb("b_out", [P, 1])
        mask_row = sb("mask_row", [1, B * S], U8)
        mask_add = sb("mask_add", [1, 2, P], BF16)
        ones = sb("ones", [1, P], BF16)
        z = sb("z", [P, 2, D])
        zT_hi, zT_lo = sb("zT_hi", [P, 2 * P], F32R), sb("zT_lo", [P, 2 * P], F32R)
        ctxT, ctx_in = sb("ctxT", [P, 2 * P]), sb("ctx", [P, 2, D])
        c_hi, c_lo = sb("c_hi", [P, 2, 2, D], F32R), sb("c_lo", [P, 2, 2, D], F32R)
        g = sb("g", [P, 16, 2 * P])
        top, den, rden = sb("top", [P, 2, 16]), sb("den", [P, 2, 16]), sb("rden", [P, 2, 16])
        probs = sb("probs", [P, 2, 8 * P])
        pT_hi, pT_lo = sb("pT_hi", [P, 8 * P], F32R), sb("pT_lo", [P, 8 * P], F32R)
        u = sb("u", [P, 16, 2 * P])
        yT = sb("yT", [P, 2 * P])
        heads_in = u[0:64, 0:8, :].rearrange("p a (h d) -> p (a h) d", h=2)
        heads_in2 = u[0:64, 8:16, :].rearrange("p a (h d) -> p (a h) d", h=2)

        scores = ps("scores", [P, 2, 8, 2, S])
        work = ps("work", [P, 2, 512])
        out_sum = ps("out_sum", [P, 512])
        turned = ps("turned", [P, 512])

        loaded, prepared = sem("loaded"), sem("prepared")
        w_mm, w_ready = sem("w_mm"), sem("w_ready")
        ctxT_in, ctx_loaded, c_hi_ready, c_ready = sem("ctxT_in"), sem("ctx_loaded"), sem("c_hi_ready"), sem("c_ready")
        z_ready, zT_mm, zT_hi_ready, zT_ready = sem("z_ready"), sem("zT_mm"), sem("zT_hi_ready"), sem("zT_ready")
        g_mm, g_ready, mask_ready = sem("g_mm"), sem("g_ready"), sem("mask_ready")
        scores_mm, shifted, exped, den_ready, normed = (sem("scores_mm"), sem("shifted"), sem("exped"),
                                                        sem("den_ready"), sem("normed"))
        pT_mm, pT_hi_ready, pT_ready = sem("pT_mm"), sem("pT_hi_ready"), sem("pT_ready")
        u_mm, u_ready, out_mm, yT_ready, y_mm, x_new = (sem("u_mm"), sem("u_ready"), sem("out_mm"), sem("yT_ready"),
                                                        sem("y_mm"), sem("x_new"))
        w_loaded, w_split = [sem("w_loaded_even"), sem("w_loaded_odd")], sem("w_split")
        ln_vector, ln_scalar = layernorm_statistics(s, sem)

        with nc.Block() as block:
            gh = g[0:64, 0:8, :].rearrange("p a (h d) -> p (a h) d", h=2)
            gh2 = g[0:64, 8:16, :].rearrange("p a (h d) -> p (a h) d", h=2)
            small = [(heads_in, a["wq1"]), (heads_in2, a["wk1"]), (gh, a["wv1"]), (gh2, a["wo1"]),
                     (b_out[:, :], a["bo1"]), (mask_row[:, :], a["mask"])]

            @block.sync
            def _(sp):
                for dst, src in small:
                    sp.dma_start(dst, src).then_inc(loaded, 16)
                sp.wait_ge(loaded, 16 * len(small))

            @block.tensor
            def _(pe):
                pe.wait_ge(loaded, 16 * len(small))
                for k in range(8):
                    if counted(k - 1):
                        pe.wait_ge(w_ready, k - 1)
                    left, right = (heads_in, heads_in2) if k < 4 else (gh, gh2)
                    for q in range(4):
                        h = 4 * (k % 4) + q
                        last = pe.matmul(work[:, k % 2, q * D:(q + 1) * D], left[:, h, :], right[:, h, :], start=True, stop=True)
                    last.then_inc(w_mm, 1)

            @block.vector
            def _(dve):
                dve.memset(ones[:, :], 1.0)
                dve.memset(c_hi[:, :, :, :].bitcast(F32), 0.0)
                dve.memset(c_lo[:, :, :, :].bitcast(F32), 0.0)
                for k in range(8):
                    c = slice(4 * (k % 4), 4 * (k % 4) + 4)
                    src = work[:, k % 2, :].rearrange("p (h d) -> p h d", d=D)
                    dve.wait_ge(w_mm, k + 1)
                    if k < 4:
                        dve.tensor_copy(m_hi[:, c, :], src)
                        dve.drain()
                        dve.tensor_tensor(m_lo[:, c, :], src, m_hi[:, c, :].bitcast(F32), ALU.subtract).then_inc(w_ready, 1)
                    else:
                        dve.tensor_copy(n_w[:, c, :], src).then_inc(w_ready, 1)
                ln_vector(dve)

            @block.scalar
            def _(act):
                ln_scalar(act)

        block = ctx.enter_context(nc.Block())

        @block.sync
        def _(sp):
            def load(k):
                if counted(2 * k):
                    sp.wait_ge(scores_mm, 2 * k)
                sp.dma_start(ctxT[:, :], a["ctxT"][:, bass.ds(k * (2 * P), 2 * P)]).then_inc(ctxT_in, 16)
                if counted(k):
                    sp.wait_ge(c_ready, k)
                sp.dma_start(ctx_in[:, :, :], a["ctx"][:, bass.ds(2 * k, 2), :]).then_inc(ctx_loaded, 16)

            load(0)
            with sp.Fori(1, N) as k:
                load(k)

        @block.gpsimd
        def _(pool):
            def body(i, has_previous, has_next):
                for t in range(2):
                    pool.wait_ge(den_ready, 2 * i + t + 1)
                    p = probs[:, t, :].rearrange("p (g j) -> p g j", j=S)
                    pool.tensor_tensor(p, p, rden[:, t, :].unsqueeze(2).broadcast_to([P, 16, S]), ALU.mult).then_inc(normed, 1)

            split_on_pool(pool, a["w_moe1"], 8, 1024, s.w_hi, s.w_lo, s.staging, w_loaded, w_split)
            steps(pool, N, body)

        @block.vector
        def _(dve):
            def mask(k):
                m = mask_row[:, bass.ds(k * 256, 256)].rearrange("p (t c) -> p t c", t=2)
                return dve.tensor_scalar(mask_add[:, :, :], m, -1.0, MASKED, ALU.add, ALU.mult).then_inc(mask_ready, 1)

            def low_part(k):
                dve.wait_ge(zT_hi_ready, k + 1)
                dve.tensor_tensor(zT_lo[:, :], turned[:, 0:2 * P], zT_hi[:, :].bitcast(F32), ALU.subtract).then_inc(zT_ready, 1)

            def context_low(k):
                dve.wait_ge(c_hi_ready, k + 1)
                for b in range(2):
                    rows = slice(64 * b, 64 * b + 64)
                    last = dve.tensor_tensor(c_lo[rows, :, b, :], ctx_in[rows, :, :], c_hi[rows, :, b, :].bitcast(F32), ALU.subtract)
                last.then_inc(c_ready, 1)

            def update(k):
                dve.wait_ge(y_mm, k + 1)
                xt = s.x[:, bass.ds(2 * k, 2), :]
                dve.scalar_tensor_tensor(out=xt, in0=turned[:, 0:2 * P].rearrange("p (t c) -> p t c", t=2),
                                         scalar=s.gates[:, 1:2], in1=xt, op0=ALU.mult, op1=ALU.add).then_inc(x_new, 1)

            mask(0)
            normalized(dve, s, z, 0, 2).then_inc(z_ready, 1)
            low_part(0)

            def body(i, has_previous, has_next):
                if has_next:
                    dve.wait_ge(zT_mm, i + 1)
                    normalized(dve, s, z, 2 * i + 2, 2).then_inc(z_ready, 1)
                for t in range(2):
                    if counted(4 * i - 2 + 2 * t):
                        dve.wait_ge(pT_mm, 4 * i - 2 + 2 * t)
                    dve.wait_ge(scores_mm, 2 * i + t + 1)
                    softmax_shifted(dve, probs[:, t, :], scores[:, t, :, :, :].rearrange("p r b j -> p (r b j)"),
                                    top[:, t, :]).then_inc(shifted, 1)
                    if t == 0:
                        if has_previous:
                            update(i - 1)
                    elif has_next:
                        mask(i + 1)
                        low_part(i + 1)
                context_low(i)
                for t in range(2):
                    dve.wait_ge(exped, 2 * i + t + 1)
                    dve.tensor_reduce(den[:, t, :], probs[:, t, :].rearrange("p (g j) -> p g j", j=S), X, ALU.add)
                    dve.drain()
                    dve.reciprocal(rden[:, t, :], den[:, t, :]).then_inc(den_ready, 1)
                for t in range(2):
                    for half in range(2):
                        c = slice(half * 512, half * 512 + 512)
                        dve.wait_ge(pT_hi_ready, 4 * i + 2 * t + half + 1)
                        dve.tensor_tensor(pT_lo[:, c], scores[:, t, 4 * half:4 * half + 4, :, :].rearrange("p r b j -> p (r b j)"),
                                          pT_hi[:, c].bitcast(F32), ALU.subtract).then_inc(pT_ready, 1)
                    for half in range(2):
                        for b in range(2):
                            n = 8 * i + 4 * t + 2 * half + b
                            dve.wait_ge(u_mm, n + 1)
                            if counted(i):
                                dve.wait_ge(out_mm, i)
                            at = t * P + b * S
                            dve.tensor_copy(u[:, 8 * half:8 * half + 8, at:at + S],
                                            work[:, b, :].rearrange("p (h i) -> p h i", i=S)).then_inc(u_ready, 1)

            steps(dve, N, body)
            update(N - 1)

        @block.scalar
        def _(act):
            def high_part(k):
                act.wait_ge(zT_mm, k + 1)
                if counted(8 * k):
                    act.wait_ge(g_mm, 8 * k)
                act.activation(zT_hi[:, :], turned[:, 0:2 * P], ACT.Copy, bias=0.0).then_inc(zT_hi_ready, 1)

            def keep_g(k, chunks):
                for c in chunks:
                    act.wait_ge(g_mm, 8 * k + c + 1)
                    act.activation(g[:, 2 * c:2 * c + 2, :], work[:, c % 2, :].rearrange("p (h i) -> p h i", h=2), ACT.Copy,
                                   bias=0.0).then_inc(g_ready, 1)

            def output_turned(k):
                act.wait_ge(out_mm, k + 1)
                act.activation(yT[:, :], out_sum[:, 0:2 * P], ACT.Identity, bias=b_out[:, 0:1]).then_inc(yT_ready, 1)

            def context_high(k):
                act.wait_ge(ctx_loaded, 16 * (k + 1))
                if counted(8 * k):
                    act.wait_ge(u_mm, 8 * k)
                for b in range(2):
                    rows = slice(64 * b, 64 * b + 64)
                    last = act.activation(c_hi[rows, :, b, :], ctx_in[rows, :, :], ACT.Copy, bias=0.0)
                last.then_inc(c_hi_ready, 1)

            high_part(0)
            keep_g(0, range(8))

            def body(i, has_previous, has_next):
                context_high(i)
                if has_previous:
                    output_turned(i - 1)
                if has_next:
                    high_part(i + 1)
                for t in range(2):
                    act.wait_ge(shifted, 2 * i + t + 1)
                    act.activation(probs[:, t, :], probs[:, t, :], ACT.Exp, bias=0.0, scale=SCALE).then_inc(exped, 1)
                    if has_next:
                        keep_g(i + 1, range(4 * t, 4 * t + 4))
                for t in range(2):
                    for half in range(2):
                        act.wait_ge(pT_mm, 4 * i + 2 * t + half + 1)
                        if counted(8 * i + 4 * t):
                            act.wait_ge(u_mm, 8 * i + 4 * t)
                        act.activation(pT_hi[:, half * 512:half * 512 + 512],
                                       scores[:, t, 4 * half:4 * half + 4, :, :].rearrange("p r b j -> p (r b j)"), ACT.Copy,
                                       bias=0.0).then_inc(pT_hi_ready, 1)

            steps(act, N, body)
            output_turned(N - 1)

        @block.tensor
        def _(pe):
            def turn_z(k):
                pe.wait_ge(z_ready, k + 1)
                for t in range(2):
                    last = pe.transpose(turned[:, t * P:(t + 1) * P], z[:, t, :], s.ident[:, :])
                last.then_inc(zT_mm, 1)

            def make_g(k):
                pe.wait_ge(zT_ready, k + 1)
                for c in range(8):
                    if counted(8 * k + c - 1):
                        pe.wait_ge(g_ready, 8 * k + c - 1)
                    for q in range(2):
                        h = 2 * c + q
                        dst = work[:, c % 2, q * 256:q * 256 + 256]
                        pe.matmul(dst, m_hi[:, h, :], zT_hi[:, :], start=True, stop=False)
                        pe.matmul(dst, m_hi[:, h, :], zT_lo[:, :], start=False, stop=False)
                        last = pe.matmul(dst, m_lo[:, h, :], zT_hi[:, :], start=False, stop=True)
                    last.then_inc(g_mm, 1)

            def turn_y(k):
                pe.wait_ge(yT_ready, k + 1)
                for t in range(2):
                    last = pe.transpose(turned[:, t * P:(t + 1) * P], yT[:, t * P:(t + 1) * P], s.ident[:, :])
                last.then_inc(y_mm, 1)

            turn_z(0)
            make_g(0)

            def body(i, has_previous, has_next):
                pe.wait_ge(ctxT_in, 16 * (i + 1))
                pe.wait_ge(mask_ready, i + 1)
                pe.wait_ge(g_ready, 8 * i + 8)
                for t in range(2):
                    if counted(4 * i - 2 + 2 * t):
                        pe.wait_ge(pT_ready, 4 * i - 2 + 2 * t)
                    for half in range(2):
                        pe.matmul(scores[:, t, 4 * half:4 * half + 4, :, :].rearrange("p r b j -> p r (b j)"), ones[:, :],
                                  mask_add[:, t, :].unsqueeze(1).broadcast_to([1, 4, P]), start=True, stop=False,
                                  skip_group_check=True)
                        for h in range(8 * half, 8 * half + 8):
                            for b in range(2):
                                at = t * P + b * S
                                rows = slice(64 * (h % 2), 64 * (h % 2) + 64)
                                last = pe.matmul(scores[rows, t, h // 2, b, :], g[:, h, at:at + S], ctxT[:, at:at + S],
                                                 start=False, stop=True, skip_group_check=True)
                    last.then_inc(scores_mm, 1)
                if has_previous:
                    turn_y(i - 1)
                    if counted(i):
                        pe.wait_ge(x_new, i)
                if has_next:
                    turn_z(i + 1)
                    if counted(8 * i):
                        pe.wait_ge(u_ready, 8 * i)
                    make_g(i + 1)
                for t in range(2):
                    pe.wait_ge(normed, 2 * i + t + 1)
                    for half in range(2):
                        for pr in range(4 * half, 4 * half + 4):
                            last = pe.transpose(scores[:, t, pr, :, :].rearrange("p b j -> p (b j)"), probs[:, t, pr * P:(pr + 1) * P],
                                                s.ident[:, :])
                        last.then_inc(pT_mm, 1)
                    pe.wait_ge(c_ready, i + 1)
                    if t == 0 and has_next:
                        pe.wait_ge(g_ready, 8 * i + 16)
                    for half in range(2):
                        pe.wait_ge(pT_ready, 4 * i + 2 * t + half + 1)
                        c = slice(half * 512, half * 512 + 512)
                        for b in range(2):
                            n = 8 * i + 4 * t + 2 * half + b
                            if counted(n - 1):
                                pe.wait_ge(u_ready, n - 1)
                            pe.matmul(work[:, b, :], c_hi[:, t, b, :], pT_hi[:, c], start=True, stop=False)
                            pe.matmul(work[:, b, :], c_hi[:, t, b, :], pT_lo[:, c], start=False, stop=False)
                            pe.matmul(work[:, b, :], c_lo[:, t, b, :], pT_hi[:, c], start=False, stop=True).then_inc(u_mm, 1)
                if counted(i):
                    pe.wait_ge(yT_ready, i)
                pe.wait_ge(u_ready, 8 * i + 8)
                for h in range(16):
                    last = pe.matmul(out_sum[:, 0:2 * P], n_w[:, h, :], u[:, h, :], start=(h == 0), stop=(h == 15))
                last.then_inc(out_mm, 1)

            steps(pe, N, body)
            turn_y(N - 1)


def experts_1(nc, s, a):
    N, C = NT // 4, 32
    LAG = 3
    DOWN = 4096

    with ExitStack() as ctx:
        def sb(name, shape, dt=F32):
            return ctx.enter_context(nc.sbuf_tensor("e1_" + name, shape, dt))

        def ps(name, shape, dt=F32):
            return ctx.enter_context(nc.psum_tensor("e1_" + name, shape, dt))

        def sem(name):
            return ctx.enter_context(nc.semaphore("e1_" + name))

        router = sb("router", [P, 8])
        b1 = sb("b1", [P, C])
        b2, b2_rest, b2_parts = sb("b2", [3, 8 * D]), sb("b2_rest", [3, 8 * D]), sb("b2_parts", [3, 8 * D], BF16)
        b2_part, part_mask = sb("b2_part", [3, 8 * D], BF16), sb("part_mask", [3, 3])
        ones = sb("ones", [3, P], BF16)
        z = sb("z", [P, 4, D])
        zT = sb("zT", [P, 2, 512])
        zT_hi, zT_lo = sb("zT_hi", [P, 2, 512], F32R), sb("zT_lo", [P, 2, 512], F32R)
        hidden = sb("hidden", [P, 4, 512])
        w2 = sb("w2", [P, C, D])
        scaled, acc = sb("scaled", [P, 2, 4, D]), sb("acc", [P, 2, 4, D])
        tmp = Shared()
        tmp.larger, tmp.equal = sb("larger", [P, 4, 8, 8]), sb("equal", [P, 4, 8, 8])
        tmp.rank, tmp.sel = sb("rank", [P, 4, 8]), sb("sel", [P, 4, 8])
        logit, shifted = sb("logit", [P, 4, 8]), sb("shifted", [P, 4, 8])
        total, weights = sb("total", [P, 4]), sb("weights", [P, 2, 4, 8])

        up, sums = ps("up", [P, 4, 512]), ps("sums", [P, 2, 4, D])
        logits_ps, turned = ps("logits", [P, 512]), ps("turned", [P, 512])

        loaded, consts = sem("loaded"), sem("consts")
        up_mm, hidden_ready, down_mm = sem("up_mm"), sem("hidden_ready"), sem("down_mm")
        sums_mm, scaled_ready, added = sem("sums_mm"), sem("scaled_ready"), sem("added")
        x_new, stored = sem("x_new"), sem("stored")
        z_ready, zT_mm, zT_hi_ready, zT_ready = sem("z_ready"), sem("zT_mm"), sem("zT_hi_ready"), sem("zT_ready")
        logits_mm, logits_read, exp_in, exp_out = sem("logits_mm"), sem("logits_read"), sem("exp_in"), sem("exp_out")
        ln_vector, ln_scalar = layernorm_statistics(s, sem)
        block = ctx.enter_context(nc.Block())

        small = [(router[:, :], a["router1"]), (b1[:, :], a["b1"]), (b2[:, :], a["b2"].broadcast_to([3, 8 * D])),
                 (part_mask[:, :], a["part_mask"]),
                 (w2[:, :, :], a["w_moe1"][:, DOWN:DOWN + C * D].rearrange("p (c d) -> p c d", d=D))]

        @block.sync
        def _(sp):
            for dst, src in small:
                sp.dma_start(dst, src).then_inc(loaded, 16)
            with sp.Fori(0, N) as n:
                sp.wait_ge(x_new, n + 1)
                sp.dma_start(s.out[:, bass.ds(4 * n, 4), :], s.x[:, bass.ds(4 * n, 4), :]).then_inc(stored, 16)
            sp.wait_ge(stored, 16 * N)

        @block.gpsimd
        def _(pool):
            def body(i, has_previous, has_next):
                for u in range(2):
                    n = 2 * i + u
                    for e in range(1, 8):
                        if counted(7 * n + e - 1):
                            pool.wait_ge(added, 7 * n + e - 1)
                        pool.wait_ge(scaled_ready, 8 * n + e + 1)
                        pool.tensor_tensor(acc[:, u, :, :], acc[:, u, :, :], scaled[:, e % 2, :, :], ALU.add).then_inc(added, 1)

            steps(pool, N // 2, body)

        @block.tensor
        def _(pe):
            pe.wait_ge(loaded, 16 * len(small))
            pe.wait_ge(consts, 1)

            def turn_z(n):
                pe.wait_ge(z_ready, n + 1)
                if counted(n):
                    pe.wait_ge(zT_ready, n)
                for t in range(4):
                    last = pe.transpose(turned[:, t * P:(t + 1) * P], z[:, t, :], s.ident[:, :])
                last.then_inc(zT_mm, 1)

            def logits(n, u):
                pe.wait_ge(zT_ready, n + 1)
                if counted(n):
                    pe.wait_ge(logits_read, n)
                for t in range(4):
                    last = pe.matmul(logits_ps[:, 8 * t:8 * t + 8], zT[:, u, t * P:(t + 1) * P], router[:, :], start=True, stop=True)
                last.then_inc(logits_mm, 1)

            def down_product(n, q):
                e, c = q // 4, q % 4
                if c == 0:
                    if counted(8 * n + e - 1):
                        pe.wait_ge(scaled_ready, 8 * n + e - 1)
                    pe.matmul(sums[:, e % 2, :, :].rearrange("p t d -> p (t d)"), ones[:, :],
                              b2_parts[:, e * D:(e + 1) * D].unsqueeze(1).broadcast_to([3, 4, D]), start=True, stop=False,
                              skip_group_check=True)
                pe.wait_ge(hidden_ready, C * n + q + 1)
                for t in range(4):
                    last = pe.matmul(sums[:, e % 2, t, :], hidden[:, q % 4, t * P:(t + 1) * P], w2[:, q, :], start=False,
                                     stop=(c == 3), skip_group_check=True)
                last.then_inc(down_mm, 1)

            turn_z(0)
            logits(0, 0)

            def body(i, has_previous, has_next):
                for u in range(2):
                    n = 2 * i + u
                    prev, nxt = has_previous or u == 1, has_next or u == 0
                    for q in range(C):
                        w = slice(q * P, (q + 1) * P)
                        dst = up[:, q % 4, :]
                        if counted(C * n + q - 3):
                            pe.wait_ge(hidden_ready, C * n + q - 3)
                        pe.matmul(dst, s.w_hi[:, w], zT_hi[:, u, :], start=True, stop=False)
                        pe.matmul(dst, s.w_hi[:, w], zT_lo[:, u, :], start=False, stop=False)
                        pe.matmul(dst, s.w_lo[:, w], zT_hi[:, u, :], start=False, stop=True).then_inc(up_mm, 1)
                        if q >= LAG:
                            down_product(n, q - LAG)
                        elif prev:
                            down_product(n - 1, C - LAG + q)
                        if q == 6 and nxt:
                            turn_z(n + 1)
                        if q == 12 and nxt:
                            logits(n + 1, 1 - u)

            steps(pe, N // 2, body)
            for q in range(C - LAG, C):
                down_product(N - 1, q)

        @block.scalar
        def _(act):
            ln_scalar(act)

            def high_part(n, u):
                act.wait_ge(zT_mm, n + 1)
                act.activation(zT_hi[:, u, :], turned[:, :], ACT.Copy, bias=0.0)
                act.activation(zT[:, u, :], turned[:, :], ACT.Copy, bias=0.0).then_inc(zT_hi_ready, 1)

            def exponential(n):
                act.wait_ge(exp_in, n + 1)
                act.activation(shifted[:, :, :], shifted[:, :, :], ACT.Exp, bias=0.0).then_inc(exp_out, 1)

            high_part(0, 0)
            exponential(0)

            def body(i, has_previous, has_next):
                for u in range(2):
                    n = 2 * i + u
                    prev, nxt = has_previous or u == 1, has_next or u == 0
                    for q in range(C):
                        act.wait_ge(up_mm, C * n + q + 1)
                        if counted(C * n + q - 3):
                            act.wait_ge(down_mm, C * n + q - 3)
                        act.activation(hidden[:, q % 4, :], up[:, q % 4, :], ACT.Gelu, bias=b1[:, q:q + 1]).then_inc(hidden_ready, 1)
                        if q == 8 and nxt:
                            high_part(n + 1, 1 - u)
                        if q == 24 and nxt:
                            exponential(n + 1)

            steps(act, N // 2, body)

        @block.vector
        def _(dve):
            dve.wait_ge(loaded, 16 * len(small))
            dve.memset(ones[:, :], 1.0)
            dve.tensor_copy(b2_part[:, :], b2[:, :])
            dve.drain()
            dve.tensor_scalar(b2_parts[:, :], b2_part[:, :], part_mask[:, 0:1], None, ALU.mult)
            for k in range(1, 3):
                dve.tensor_tensor(b2[:, :], b2[:, :], b2_part[:, :], ALU.subtract)
                dve.drain()
                dve.tensor_copy(b2_part[:, :], b2[:, :])
                dve.drain()
                last = dve.scalar_tensor_tensor(out=b2_parts[:, :], in0=b2_part[:, :], scalar=part_mask[:, k:k + 1],
                                                in1=b2_parts[:, :], op0=ALU.mult, op1=ALU.add)
                if k == 2:
                    last.then_inc(consts, 1)
                dve.drain()
            ln_vector(dve)

            def low_part(n, u):
                dve.wait_ge(zT_hi_ready, n + 1)
                dve.tensor_tensor(zT_lo[:, u, :], turned[:, :], zT_hi[:, u, :].bitcast(F32), ALU.subtract).then_inc(zT_ready, 1)

            def route(n):
                dve.wait_ge(logits_mm, n + 1)
                dve.tensor_copy(logit[:, :, :], logits_ps[:, 0:32].rearrange("p (t e) -> p t e", t=4)).then_inc(logits_read, 1)
                dve.drain()
                dve.tensor_reduce(total[:, :], logit[:, :, :], X, ALU.max)
                chosen(dve, s, tmp, logit[:, :, :], 2)
                dve.tensor_tensor(shifted[:, :, :], logit[:, :, :], total[:, :].unsqueeze(2).broadcast_to([P, 4, 8]),
                                  ALU.subtract).then_inc(exp_in, 1)

            def weigh(n, u):
                dve.wait_ge(exp_out, n + 1)
                dve.tensor_tensor(shifted[:, :, :], shifted[:, :, :], tmp.sel[:, :, :], ALU.mult)
                dve.drain()
                dve.tensor_reduce(total[:, :], shifted[:, :, :], X, ALU.add)
                dve.drain()
                dve.reciprocal(total[:, :], total[:, :])
                dve.drain()
                dve.tensor_tensor(weights[:, u, :, :], shifted[:, :, :], total[:, :].unsqueeze(2).broadcast_to([P, 4, 8]), ALU.mult)
                dve.drain()

            def scale(n, e, u):
                dve.wait_ge(down_mm, C * n + 4 * e + 4)
                dst = scaled[:, e % 2, :, :]
                if e:
                    if counted(7 * n + (e - 2 if e >= 2 else 0)):
                        dve.wait_ge(added, 7 * n + (e - 2 if e >= 2 else 0))
                else:
                    dst = acc[:, u, :, :]
                dve.tensor_tensor(dst, sums[:, e % 2, :, :], weights[:, u, :, e].unsqueeze(2).broadcast_to([P, 4, D]),
                                  ALU.mult).then_inc(scaled_ready, 1)

            def update(n, u):
                dve.wait_ge(added, 7 * n + 7)
                xt = s.x[:, bass.ds(4 * n, 4), :]
                dve.scalar_tensor_tensor(out=xt, in0=acc[:, u, :, :], scalar=s.gates[:, 3:4], in1=xt, op0=ALU.mult,
                                         op1=ALU.add).then_inc(x_new, 1)

            normalized(dve, s, z, 0, 4).then_inc(z_ready, 1)
            low_part(0, 0)
            route(0)
            weigh(0, 0)

            def body(i, has_previous, has_next):
                for u in range(2):
                    n = 2 * i + u
                    prev, nxt = has_previous or u == 1, has_next or u == 0
                    if nxt:
                        dve.wait_ge(zT_mm, n + 1)
                        normalized(dve, s, z, 4 * n + 4, 4).then_inc(z_ready, 1)
                    if prev:
                        scale(n - 1, 7, 1 - u)
                    for e in range(7):
                        if e == 1 and prev:
                            update(n - 1, 1 - u)
                        if e == 2 and nxt:
                            low_part(n + 1, 1 - u)
                        if e == 4 and nxt:
                            route(n + 1)
                        if e == 6 and nxt:
                            weigh(n + 1, 1 - u)
                        scale(n, e, u)

            steps(dve, N // 2, body)
            scale(N - 1, 7, 1)
            update(N - 1, 1)


def build(nc, a, out):
    s = Shared()
    s.out = out
    with ExitStack() as ctx:
        def sb(name, shape, dt=F32):
            return ctx.enter_context(nc.sbuf_tensor(name, shape, dt))

        s.x = sb("x_sb", [P, NT, D])
        s.ident, s.gates, s.tri = sb("ident_sb", [P, P]), sb("gates_sb", [P, 4]), sb("tri_sb", [P, 8, 8])
        s.stats, s.mean, s.var = sb("ln_stats", [P, NT, 6]), sb("ln_mean", [P, NT]), sb("ln_var", [P, NT])
        s.root, s.rstd = sb("ln_root", [P, NT]), sb("ln_rstd", [P, NT])
        s.w_hi, s.w_lo = sb("w_hi", [P, 8192], F32R), sb("w_lo", [P, 8192], F32R)
        s.staging = sb("staging", [P, 2, 1280])
        setup(nc, s, a)
        for stage in STEPS:
            stage(nc, s, a)


class Shared:
    pass


STEPS = [attention_0, experts_0, attention_1, experts_1]


def laid_out(inputs):
    v = {k: np.asarray(x) for k, x in inputs.items()}
    c = np.ascontiguousarray
    E0, I0 = 32, 64
    E1, F1 = 8, 512
    tokens = lambda t: c(t.reshape(NT, P, D).transpose(1, 0, 2))
    wkv = v["L1_xattn_Wkv"]
    heads = lambda w: c(w.reshape(16, 64, D).transpose(1, 0, 2))
    down = v["L0_ffn_expert_down"].transpose(0, 2, 1).reshape(16, P, D).transpose(1, 0, 2).reshape(P, 16 * D)
    shared_down = np.zeros((P, D), np.float32)
    shared_down[0:I0] = v["L0_ffn_shared_down_w"].T
    pick = np.zeros((3, E0, 16, 2, I0), np.float32)
    for e in range(E0):
        pick[:, e, e // 2, e % 2, :] = 1
    place = np.zeros((4, 2, 2, 8, 2, 2, D), np.float32)
    par_mask = np.zeros((4, 2, 2, 8, 2), np.float32)
    for g in range(4):
        for r in range(4):
            for d in range(8):
                for b in range(2):
                    place[g, b, r % 2, d, b, r // 2, 32 * g + 8 * r + d] = 1
    for par in range(2):
        par_mask[:, :, par, :, par] = 1
    v_order = np.arange(D).reshape(4, 2, 16).transpose(1, 0, 2).reshape(D)
    head_mask = np.zeros((4, 4, 8, 4), np.float32)
    for r in range(4):
        head_mask[:, r, :, r] = 1
    return {
        "x": tokens(v["x"]), "ctx": tokens(v["ctx_1024"]), "ctxT": c(v["ctx_1024"].reshape(B * S, D).T),
        "mask": c(v["mask_BxS2_bf1"]).view(np.uint8).reshape(1, B * S),
        "g_xattn": v["g_xattn"], "g_ffn": v["g_ffn"],
        "wq0T": c(v["L0_xattn_Wq"].T), "wk0T": c(v["L0_xattn_Wk"].T), "wv0T": c(v["L0_xattn_Wv"].T[:, v_order]),
        "bq0": v["L0_xattn_bq"].reshape(D, 1), "bk0": v["L0_xattn_bk"].reshape(D, 1), "bv0": c(v["L0_xattn_bv"][v_order]),
        "router0": c(v["L0_ffn_gate_w"].T),
        "w_moe0": c(np.concatenate([v["L0_ffn_expert_gate"].reshape(E0 * I0, D).T, v["L0_ffn_shared_gate_w"].T,
                                    v["L0_ffn_expert_up"].reshape(E0 * I0, D).T, v["L0_ffn_shared_up_w"].T,
                                    down, shared_down], 1)),
        "wq1": heads(v["L1_xattn_Wq"]), "wk1": heads(wkv[:1024]), "wv1": heads(wkv[1024:]),
        "wo1": heads(v["L1_xattn_Wout"].T), "bo1": v["L1_xattn_b_out"].reshape(D, 1),
        "router1": c(v["L1_ffn_router_w"].T),
        "w_moe1": c(np.concatenate([v["L1_ffn_w1"].reshape(E1 * F1, D).T,
                                    v["L1_ffn_w2"].transpose(0, 2, 1).reshape(32, P, D).transpose(1, 0, 2).reshape(P, 32 * D)], 1)),
        "b1": c(v["L1_ffn_b1"].reshape(32, P).T), "b2": c(v["L1_ffn_b2"].reshape(1, E1 * D)),
        "ident": np.eye(P, dtype=np.float32), "head_mask": head_mask.reshape(P, 4), "place": place.reshape(P, 2, 2, D), "par_mask": par_mask.reshape(P, 2),
        "tri": c(np.broadcast_to(np.tril(np.ones((8, 8), np.float32), -1), (P, 8, 8))),
        "pick": c(pick.reshape(96, 16, P)), "part_mask": np.eye(3, dtype=np.float32),
    }


def kernel(**inputs):
    import concourse.bacc as bacc
    from concourse.bass_utils import run_bass_kernel_spmd

    nc = bacc.Bacc("TRN2", target_bir_lowering=False, num_devices=1)
    arrays = {f"in_{name}": v for name, v in laid_out(inputs).items()}
    a = {name[3:]: nc.dram_tensor(name, v.shape, mybir.dt.from_np(v.dtype), kind="ExternalInput").ap()
         for name, v in arrays.items()}
    out = nc.dram_tensor("out", (P, NT, D), F32, kind="ExternalOutput").ap()
    build(nc, a, out)
    got = run_bass_kernel_spmd(nc, [arrays], core_ids=[0]).results[0]["out"]
    return np.ascontiguousarray(got.reshape(P, NT, D).transpose(1, 0, 2)).reshape(B, S, D)
```

```python
from contextlib import ExitStack

import numpy as np

import concourse.bass as bass
from concourse import mybir

F32 = mybir.dt.float32
F32R = mybir.dt.float32r
BF16 = mybir.dt.bfloat16
U8 = mybir.dt.uint8
ALU = mybir.AluOpType
ACT = mybir.ActivationFunctionType
X = mybir.AxisListType.X

P = 128
B, S, D = 128, 64, 128
NT = B * S // P
EPS = 1e-5


def counted(value):
    return not isinstance(value, int) or value > 0


def steps(eng, n, body):
    body(0, False, True)
    body(1, True, True)
    with eng.Fori(2, n - 1) as i:
        body(i, True, True)
    body(n - 1, True, False)


def tile_statistics(dve, s, k, n):
    for t in range(n):
        dve.bn_stats(s.stats[:, bass.ds(k + t, 1), :], s.x[:, bass.ds(k + t, 1), :])


def layernorm_statistics(s, sem):
    sq_in, sq_out = sem("ln_variance_ready"), sem("ln_root_ready")

    def on_vector(dve):
        mean_even, mean_odd = s.stats[:, :, 1], s.stats[:, :, 4]
        dve.tensor_tensor(s.mean[:, :], mean_even, mean_odd, ALU.add)
        dve.tensor_tensor(s.rstd[:, :], mean_even, mean_odd, ALU.subtract)
        dve.tensor_tensor(s.var[:, :], s.stats[:, :, 2], s.stats[:, :, 5], ALU.add)
        dve.drain()
        dve.tensor_scalar(s.mean[:, :], s.mean[:, :], 0.5, None, ALU.mult)
        dve.tensor_tensor(s.rstd[:, :], s.rstd[:, :], s.rstd[:, :], ALU.mult)
        dve.tensor_scalar(s.var[:, :], s.var[:, :], 1.0 / D, EPS, ALU.mult, ALU.add)
        dve.drain()
        dve.scalar_tensor_tensor(out=s.var[:, :], in0=s.rstd[:, :], scalar=0.25, in1=s.var[:, :],
                                 op0=ALU.mult, op1=ALU.add).then_inc(sq_in, 1)
        dve.wait_ge(sq_out, 1)
        dve.reciprocal(s.rstd[:, :], s.root[:, :])
        dve.drain()

    def on_scalar(act):
        act.wait_ge(sq_in, 1)
        act.activation(s.root[:, :], s.var[:, :], ACT.Sqrt, bias=0.0).then_inc(sq_out, 1)

    return on_vector, on_scalar


def split_on_pool(pool, source, chunks, width, hi, lo, staging, loaded, split, before_chunk=None):
    def load(k):
        half = k % 2 * width
        pool.dma_start(staging[:, half:half + width], source[:, k * width:(k + 1) * width]).then_inc(loaded[k % 2], 16)

    load(0)
    for k in range(chunks):
        if k + 1 < chunks:
            if counted(k):
                pool.wait_ge(split, k)
            load(k + 1)
        if before_chunk:
            before_chunk(k)
        c = slice(k * width, (k + 1) * width)
        part = staging[:, k % 2 * width:k % 2 * width + width]
        pool.wait_ge(loaded[k % 2], 16 * (k // 2 + 1))
        pool.tensor_copy(hi[:, c], part)
        pool.drain()
        pool.tensor_tensor(lo[:, c], part, hi[:, c].bitcast(F32), ALU.subtract).then_inc(split, 1)


def normalized(dve, s, z, k, n):
    for t in range(n):
        last = dve.tensor_scalar(z[:, t, :], s.x[:, bass.ds(k + t, 1), :], s.mean[:, bass.ds(k + t, 1)],
                                 s.rstd[:, bass.ds(k + t, 1)], ALU.subtract, ALU.mult)
    return last


def setup(nc, s, a):
    PIECES = 4
    tiles = NT // PIECES
    with ExitStack() as ctx:
        x_in = [ctx.enter_context(nc.semaphore(f"x_in_{k}")) for k in range(PIECES)]
        loaded = ctx.enter_context(nc.semaphore("loaded"))
        gates = ctx.enter_context(nc.semaphore("gates"))
        block = ctx.enter_context(nc.Block())
        small = [(s.ident[:, :], a["ident"]), (s.gates[:, 0:2], a["g_xattn"].partition_broadcast(P)),
                   (s.gates[:, 2:4], a["g_ffn"].partition_broadcast(P)), (s.tri[:, :, :], a["tri"])]

        @block.sync
        def _(sp):
            for k in range(PIECES):
                c = slice(k * tiles, (k + 1) * tiles)
                sp.dma_start(s.x[:, c, :], a["x"][:, c, :]).then_inc(x_in[k], 16)
            for dst, src in small:
                sp.dma_start(dst, src).then_inc(loaded, 16)
            sp.wait_ge(loaded, 16 * len(small))

        @block.vector
        def _(dve):
            for k in range(PIECES):
                dve.wait_ge(x_in[k], 16)
                with dve.Fori(0, tiles // 8) as m:
                    tile_statistics(dve, s, m * 8 + k * tiles, 8)

        @block.scalar
        def _(act):
            act.wait_ge(loaded, 16 * len(small))
            act.activation(s.gates[:, :], s.gates[:, :], ACT.Tanh, bias=0.0).then_inc(gates, 1)
            act.wait_ge(gates, 1)


def score_tops(dve, top, scores):
    dve.tensor_reduce(top, scores.rearrange("p (g j) -> p g j", j=S), X, ALU.max)
    dve.drain()


def less_tops(dve, out, scores, top):
    return dve.tensor_tensor(out.rearrange("p (g j) -> p g j", j=S), scores.rearrange("p (g j) -> p g j", j=S),
                             top.unsqueeze(2).broadcast_to([P, 16, S]), ALU.subtract)


def softmax_shifted(dve, out, scores, top):
    score_tops(dve, top, scores)
    return less_tops(dve, out, scores, top)


def attention_0(nc, s, a):
    N = NT // 2
    SCALE = 8.0 ** -0.5
    with ExitStack() as ctx:
        def sb(name, shape, dt=F32):
            return ctx.enter_context(nc.sbuf_tensor("a0_" + name, shape, dt))

        def ps(name, shape, dt=F32):
            return ctx.enter_context(nc.psum_tensor("a0_" + name, shape, dt))

        def sem(name):
            return ctx.enter_context(nc.semaphore("a0_" + name))

        wq, wk, wv = sb("wq", [P, D]), sb("wk", [P, D]), sb("wv", [P, D])
        bq, bk, bv = sb("bq", [P, 1]), sb("bk", [P, 1]), sb("bv", [P, D])
        head_mask, bq_masked = sb("head_mask", [P, 4]), sb("bq_masked", [P, 4])
        par_mask, place = sb("par_mask", [P, 2]), sb("place", [P, 2, 2, D])
        ctxT_k, ctxT_v = sb("ctxT_k", [P, 2 * P]), sb("ctxT_v", [P, 2 * P])
        z, zT = sb("z", [P, 2, D]), sb("zT", [P, 2 * P])
        qm, kz = sb("qm", [P, 4, 4, S]), sb("kz", [P, 4, 4, S])
        vz = sb("vz", [P, 2, 8, 2, 16])
        top, den, rden = sb("top", [P, 2, 16]), sb("den", [P, 2, 16]), sb("rden", [P, 2, 16])
        below_top = sb("below_top", [P, 2, 8 * P])
        probs, probsT = sb("probs", [P, 2, 8 * P]), sb("probsT", [P, 2, 8 * P])
        heads = sb("heads", [P, 2, 2, S])

        scores = ps("scores", [P, 2, 2, 4, 2, S])
        turned = ps("turned", [P, 2, 512])
        late = ps("late", [P, 512])
        early = ps("early", [P, 512])

        loaded, consts = sem("loaded"), sem("consts")
        k_in, v_in = sem("k_in"), sem("v_in")
        z_ready, zT_mm, zT_ready = sem("z_ready"), sem("zT_mm"), sem("zT_ready")
        qk_mm, qk_ready, v_mm, v_ready = sem("qk_mm"), sem("qk_ready"), sem("v_mm"), sem("v_ready")
        scores_mm, shifted, exped = sem("scores_mm"), sem("shifted"), sem("exped")
        den_ready, normed = sem("den_ready"), sem("normed")
        pT_mm, pT_ready = sem("pT_mm"), sem("pT_ready")
        heads_mm, heads_ready, y_mm, x_new = sem("heads_mm"), sem("heads_ready"), sem("y_mm"), sem("x_new")
        w_loaded, w_split = [sem("w_loaded_even"), sem("w_loaded_odd")], sem("w_split")
        ln_vector, ln_scalar = layernorm_statistics(s, sem)
        block = ctx.enter_context(nc.Block())
        small = [(wq[:, :], a["wq0T"]), (wk[:, :], a["wk0T"]), (wv[:, :], a["wv0T"]), (bq[:, :], a["bq0"]),
                 (bk[:, :], a["bk0"]), (bv[:, :], a["bv0"].partition_broadcast(P)),
                 (head_mask[:, :], a["head_mask"]), (par_mask[:, :], a["par_mask"]), (place[:, :, :, :], a["place"])]

        @block.sync
        def _(sp):
            for dst, src in small:
                sp.dma_start(dst, src).then_inc(loaded, 16)
            sp.dma_start(ctxT_k[:, :], a["ctxT"][:, 0:2 * P]).then_inc(k_in, 16)
            sp.dma_start(ctxT_v[:, :], a["ctxT"][:, 0:2 * P]).then_inc(v_in, 16)
            with sp.Fori(1, N) as k:
                sp.wait_ge(qk_mm, k)
                sp.dma_start(ctxT_k[:, :], a["ctxT"][:, bass.ds(k * (2 * P), 2 * P)]).then_inc(k_in, 16)
                sp.wait_ge(v_mm, k)
                sp.dma_start(ctxT_v[:, :], a["ctxT"][:, bass.ds(k * (2 * P), 2 * P)]).then_inc(v_in, 16)

        @block.gpsimd
        def _(pool):
            def normalize(i):
                for t in range(2):
                    pool.wait_ge(den_ready, 2 * i + t + 1)
                    p = probs[:, t, :].rearrange("p (g j) -> p g j", j=S)
                    pool.tensor_tensor(p, p, rden[:, t, :].unsqueeze(2).broadcast_to([P, 16, S]), ALU.mult).then_inc(normed, 1)

            split_on_pool(pool, a["w_moe0"], 5, 1280, s.w_hi, s.w_lo, s.staging, w_loaded, w_split, normalize)
            with pool.Fori(5, N) as i:
                normalize(i)

        @block.vector
        def _(dve):
            dve.memset(kz[:, :, :, :], 0.0)
            dve.memset(vz[:, :, :, :, :], 0.0)
            ln_vector(dve)
            dve.wait_ge(loaded, 16 * len(small))
            dve.tensor_scalar(bq_masked[:, :], head_mask[:, :], bq[:, 0:1], None, ALU.mult).then_inc(consts, 1)

            def values(k):
                dve.wait_ge(v_mm, k + 1)
                for b in range(2):
                    rows = slice(64 * b, 64 * b + 64)
                    v = early[rows, 0:2 * P].rearrange("p (t a c) -> p t a c", t=2, c=16)
                    bias = bv[rows, :].rearrange("p (a c) -> p a c", c=16).unsqueeze(1).broadcast_to([64, 2, 8, 16])
                    last = dve.tensor_tensor(vz[rows, :, :, b, :], v, bias, ALU.add)
                last.then_inc(v_ready, 1)

            def softmax_top(i, t):
                dve.wait_ge(scores_mm, 2 * i + t + 1)
                score_tops(dve, top[:, t, :], scores[:, t, :, :, :, :].rearrange("p h g b j -> p (h g b j)"))

            def softmax_shift(t):
                less_tops(dve, below_top[:, t, :], scores[:, t, :, :, :, :].rearrange("p h g b j -> p (h g b j)"),
                          top[:, t, :]).then_inc(shifted, 1)

            def denominators(i, t):
                dve.wait_ge(exped, 2 * i + t + 1)
                dve.tensor_reduce(den[:, t, :], probs[:, t, :].rearrange("p (g j) -> p g j", j=S), X, ALU.add)
                dve.drain()
                dve.reciprocal(rden[:, t, :], den[:, t, :]).then_inc(den_ready, 1)

            def keep_heads(i, t):
                dve.wait_ge(heads_mm, 2 * i + t + 1)
                if counted(2 * i + t - 1):
                    dve.wait_ge(y_mm, 2 * i + t - 1)
                o = late[:, 0:2 * P].rearrange("p (h r i) -> p h r i", h=2, r=2)
                dve.tensor_scalar(heads[:, t, :, :], o[:, :, 0, :], par_mask[:, 0:1], None, ALU.mult)
                dve.drain()
                dve.scalar_tensor_tensor(out=heads[:, t, :, :], in0=o[:, :, 1, :], scalar=par_mask[:, 1:2],
                                         in1=heads[:, t, :, :], op0=ALU.mult, op1=ALU.add).then_inc(heads_ready, 1)

            def update(k):
                dve.wait_ge(y_mm, 2 * k + 2)
                xt = s.x[:, bass.ds(2 * k, 2), :]
                dve.scalar_tensor_tensor(out=xt, in0=late[:, 2 * P:4 * P].rearrange("p (t c) -> p t c", t=2),
                                         scalar=s.gates[:, 0:1], in1=xt, op0=ALU.mult, op1=ALU.add).then_inc(x_new, 1)
                dve.drain()
                tile_statistics(dve, s, 2 * k, 2)

            normalized(dve, s, z, 0, 2).then_inc(z_ready, 1)

            def body(i, has_previous, has_next):
                if has_next:
                    dve.wait_ge(zT_mm, i + 1)
                    normalized(dve, s, z, 2 * i + 2, 2).then_inc(z_ready, 1)
                if has_previous:
                    denominators(i - 1, 1)
                    values(i - 1)
                softmax_top(i, 0)
                softmax_shift(0)
                softmax_top(i, 1)
                if has_previous:
                    keep_heads(i - 1, 0)
                softmax_shift(1)
                if has_previous:
                    keep_heads(i - 1, 1)
                denominators(i, 0)
                if has_previous:
                    update(i - 1)

            steps(dve, N, body)
            values(N - 1)
            denominators(N - 1, 1)
            keep_heads(N - 1, 0)
            keep_heads(N - 1, 1)
            update(N - 1)

        @block.scalar
        def _(act):
            ln_scalar(act)
            act.wait_ge(consts, 1)

            def normalized_transposed(k):
                act.wait_ge(zT_mm, k + 1)
                act.activation(zT[:, :], early[:, 0:2 * P], ACT.Copy, bias=0.0).then_inc(zT_ready, 1)

            def keys(k):
                act.wait_ge(qk_mm, k + 1)
                for g in range(4):
                    rows = slice(32 * g, 32 * g + 32)
                    act.activation(kz[rows, :, g, :], early[rows, 2 * P:4 * P].rearrange("p (b j) -> p b j", b=4),
                                   ACT.Identity, bias=bk[rows, 0:1])

            def queries(k):
                for r in range(4):
                    last = act.activation(qm[:, :, r, :], early[:, 0:2 * P].rearrange("p (b i) -> p b i", b=4), ACT.Identity,
                                          bias=bq_masked[:, r:r + 1], scale=head_mask[:, r:r + 1])
                last.then_inc(qk_ready, 1)

            def keep_turned(i, t):
                for half in range(2):
                    act.wait_ge(pT_mm, 4 * i + 2 * t + half + 1)
                    act.activation(probsT[:, t, half * 512:half * 512 + 512], turned[:, half, :], ACT.Copy,
                                   bias=0.0).then_inc(pT_ready, 1)

            def exponential(i, t):
                if counted(4 * i - 2 + 2 * t):
                    act.wait_ge(pT_mm, 4 * i - 2 + 2 * t)
                act.wait_ge(shifted, 2 * i + t + 1)
                act.activation(probs[:, t, :], below_top[:, t, :], ACT.Exp, bias=0.0, scale=SCALE).then_inc(exped, 1)

            normalized_transposed(0)
            keys(0)
            queries(0)

            def body(i, has_previous, has_next):
                if has_next:
                    normalized_transposed(i + 1)
                if has_previous:
                    keep_turned(i - 1, 0)
                exponential(i, 0)
                if has_next:
                    keys(i + 1)
                if has_previous:
                    keep_turned(i - 1, 1)
                if has_next:
                    queries(i + 1)
                exponential(i, 1)

            steps(act, N, body)
            keep_turned(N - 1, 0)
            keep_turned(N - 1, 1)

        @block.tensor
        def _(pe):
            pe.wait_ge(loaded, 16 * len(small))

            def turn_z(k):
                pe.wait_ge(z_ready, k + 1)
                if counted(k - 1):
                    pe.wait_ge(v_ready, k - 1)
                for t in range(2):
                    last = pe.transpose(early[:, t * P:(t + 1) * P], z[:, t, :], s.ident[:, :])
                last.then_inc(zT_mm, 1)

            def project_qk(k):
                pe.wait_ge(zT_ready, k + 1)
                pe.wait_ge(k_in, 16 * (k + 1))
                pe.matmul(early[:, 0:2 * P], wq[:, :], zT[:, :], start=True, stop=True)
                pe.matmul(early[:, 2 * P:4 * P], wk[:, :], ctxT_k[:, :], start=True, stop=True).then_inc(qk_mm, 1)

            def project_v(k):
                pe.wait_ge(v_in, 16 * (k + 1))
                for t in range(2):
                    last = pe.matmul(early[:, t * P:(t + 1) * P], ctxT_v[:, t * P:(t + 1) * P], wv[:, :], start=True, stop=True)
                last.then_inc(v_mm, 1)

            def score(i, t):
                if counted(2 * i + t - 1):
                    pe.wait_ge(shifted, 2 * i + t - 1)
                for b in range(2):
                    for half in range(2):
                        q = qm[:, 2 * t + b, 2 * half:2 * half + 2, :].rearrange("p r i -> p (r i)")
                        last = pe.matmul(scores[:, t, half, :, b, :], q, kz[:, 2 * t + b, :, :], start=True, stop=True)
                last.then_inc(scores_mm, 1)

            def turn(i, t):
                pe.wait_ge(normed, 2 * i + t + 1)
                if counted(4 * i + 2 * t):
                    pe.wait_ge(pT_ready, 4 * i + 2 * t)
                for half in range(2):
                    for q in range(4):
                        pr = 4 * half + q
                        last = pe.transpose(turned[:, half, q * P:(q + 1) * P], probs[:, t, pr * P:(pr + 1) * P], s.ident[:, :])
                    last.then_inc(pT_mm, 1)

            def weigh_values(i, t):
                if counted(2 * i + t):
                    pe.wait_ge(heads_ready, 2 * i + t)
                if t == 0:
                    pe.wait_ge(v_ready, i + 1)
                    if counted(i):
                        pe.wait_ge(x_new, i)
                for half in range(2):
                    pe.wait_ge(pT_ready, 4 * i + 2 * t + half + 1)
                    for q in range(4):
                        pr = 4 * half + q
                        last = pe.matmul(late[32 * q:32 * q + 32, half * P:half * P + P], vz[:, t, pr, :, :].rearrange("p b c -> p (b c)"),
                                         probsT[:, t, pr * P:(pr + 1) * P], start=True, stop=True)
                last.then_inc(heads_mm, 1)

            def output(k, t):
                pe.wait_ge(heads_ready, 2 * k + t + 1)
                for b in range(2):
                    for half in range(2):
                        last = pe.matmul(late[64 * b:64 * b + 64, 2 * P + t * P:2 * P + (t + 1) * P], heads[:, t, half, :],
                                         place[:, b, half, :], start=(half == 0), stop=(half == 1))
                last.then_inc(y_mm, 1)

            turn_z(0)
            project_qk(0)

            def body(i, has_previous, has_next):
                pe.wait_ge(qk_ready, i + 1)
                score(i, 0)
                if has_previous:
                    project_v(i - 1)
                score(i, 1)
                if has_next:
                    turn_z(i + 1)
                if has_previous:
                    turn(i - 1, 0)
                if has_next:
                    project_qk(i + 1)
                if has_previous:
                    weigh_values(i - 1, 0)
                    turn(i - 1, 1)
                    output(i - 1, 0)
                    weigh_values(i - 1, 1)
                    output(i - 1, 1)

            steps(pe, N, body)
            project_v(N - 1)
            for t in range(2):
                turn(N - 1, t)
                weigh_values(N - 1, t)
                output(N - 1, t)


def compare_values(dve, s, tmp, values):
    other = values.unsqueeze(2).broadcast_to([P, 4, 8, 8])
    own = values.unsqueeze(3).broadcast_to([P, 4, 8, 8])
    dve.tensor_tensor(tmp.larger[:, :, :, :], other, own, ALU.is_gt)
    dve.tensor_tensor(tmp.equal[:, :, :, :], other, own, ALU.is_equal)
    dve.drain()


def count_before(dve, s, tmp):
    dve.tensor_tensor(tmp.equal[:, :, :, :], tmp.equal[:, :, :, :], s.tri[:, :, :].unsqueeze(1).broadcast_to([P, 4, 8, 8]), ALU.mult)
    dve.drain()
    dve.tensor_tensor(tmp.larger[:, :, :, :], tmp.larger[:, :, :, :], tmp.equal[:, :, :, :], ALU.add)
    dve.drain()


def choose(dve, tmp, k):
    dve.tensor_reduce(tmp.rank[:, :, :], tmp.larger[:, :, :, :], X, ALU.add)
    dve.drain()
    dve.tensor_scalar(tmp.sel[:, :, :], tmp.rank[:, :, :], float(k), None, ALU.is_lt)
    dve.drain()


def experts_0(nc, s, a):
    N, C = NT // 4, 17
    STEP, LAG, RING = 2 * C, 4, 5
    G, U, DN = 0, 2112, 4224

    with ExitStack() as ctx:
        def sb(name, shape, dt=F32):
            return ctx.enter_context(nc.sbuf_tensor("e0_" + name, shape, dt))

        def ps(name, shape, dt=F32):
            return ctx.enter_context(nc.psum_tensor("e0_" + name, shape, dt))

        def sem(name):
            return ctx.enter_context(nc.semaphore("e0_" + name))

        pick = sb("pick", [96, 16, P], BF16)
        identb = sb("identb", [P, P], BF16)
        router = sb("router", [P, 32])
        z = sb("z", [P, 4, D])
        zT = sb("zT", [P, 2, 512])
        zT_hi, zT_lo = sb("zT_hi", [P, 2, 512], F32R), sb("zT_lo", [P, 2, 512], F32R)
        gated, raised, hidden = sb("gated", [P, 2, 512]), sb("raised", [P, 2, 512]), sb("hidden", [P, RING, 512])
        hidden_hi, hidden_lo = sb("hidden_hi", [P, RING, 512], F32R), sb("hidden_lo", [P, RING, 512], F32R)
        yT = sb("yT", [P, 512])
        weightsT = sb("weightsT", [96, 2, 512], BF16)
        tmp = Shared()
        tmp.larger, tmp.equal = sb("larger", [P, 4, 8, 8]), sb("equal", [P, 4, 8, 8])
        tmp.rank, tmp.sel = sb("rank", [P, 4, 8]), sb("sel", [P, 4, 8])
        scored, groups = sb("scored", [P, 4, 32]), sb("groups", [P, 4, 8])
        masked, left, top8 = sb("masked", [P, 4, 32]), sb("left", [P, 4, 32]), sb("top8", [P, 4, 8])
        total = sb("total", [P, 4])
        parts = sb("parts", [P, 4, 3, 32], BF16)

        gate, up, spread = ps("gate", [P, 2, 512]), ps("up", [P, 2, 512]), ps("spread", [P, 2, 512])
        out_sum, turned = ps("out_sum", [P, 512]), ps("turned", [P, 512])
        turned_bf = turned[0:96, 0:256].bitcast(BF16)

        loaded, consts = sem("loaded"), sem("consts")
        gate_mm, up_mm, spread_mm, down_mm = sem("gate_mm"), sem("up_mm"), sem("spread_mm"), sem("down_mm")
        gated_ready, raised_ready, hidden_ready = sem("gated_ready"), sem("raised_ready"), sem("hidden_ready")
        hidden_hi_ready, hidden_lo_ready = sem("hidden_hi_ready"), sem("hidden_lo_ready")
        yT_ready, y_mm, x_new = sem("yT_ready"), sem("y_mm"), sem("x_new")
        z_ready, zT_mm, zT_hi_ready, zT_ready = sem("z_ready"), sem("zT_mm"), sem("zT_hi_ready"), sem("zT_ready")
        logits_mm, scored_ready, parts_ready = sem("logits_mm"), sem("scored_ready"), sem("parts_ready")
        weights_mm, weights_ready = sem("weights_mm"), sem("weights_ready")
        ln_vector, ln_scalar = layernorm_statistics(s, sem)
        block = ctx.enter_context(nc.Block())

        def rows(j):
            return 128 if j < 16 else 64

        def before(i, g, ring):
            if g >= ring:
                return STEP * i + g - ring + 1
            return STEP * (i - 1) + max(m for m in range(STEP) if m % ring == g) + 1

        picks_in = s.staging[0:96, 0:2048]
        small = [(picks_in, a["pick"].rearrange("k j m -> k (j m)")), (router[:, :], a["router0"])]

        @block.sync
        def _(sp):
            for dst, src in small:
                sp.dma_start(dst, src).then_inc(loaded, 16)
            sp.wait_ge(loaded, 16 * len(small))

        @block.tensor
        def _(pe):
            pe.wait_ge(loaded, 16 * len(small))
            pe.wait_ge(consts, 1)

            def turn_z(n):
                pe.wait_ge(z_ready, n + 1)
                if counted(n):
                    pe.wait_ge(weights_ready, n)
                for t in range(4):
                    last = pe.transpose(turned[:, t * P:(t + 1) * P], z[:, t, :], s.ident[:, :])
                last.then_inc(zT_mm, 1)

            def logits(n, u):
                pe.wait_ge(zT_ready, n + 1)
                for t in range(4):
                    last = pe.matmul(turned[:, 32 * t:32 * t + 32], zT[:, u, t * P:(t + 1) * P], router[:, :], start=True, stop=True)
                last.then_inc(logits_mm, 1)

            def turn_weights(n):
                pe.wait_ge(parts_ready, n + 1)
                for t in range(4):
                    last = pe.transpose(turned_bf[:, t * P:(t + 1) * P], parts[:, t, :, :].rearrange("p c e -> p (c e)"), identb[:, :])
                last.then_inc(weights_mm, 1)

            def turn_y(n):
                pe.wait_ge(yT_ready, n + 1)
                for t in range(4):
                    last = pe.transpose(turned[:, t * P:(t + 1) * P], yT[:, t * P:(t + 1) * P], s.ident[:, :])
                last.then_inc(y_mm, 1)

            def product(dst, hi, lo, col, m):
                w_h, w_l = s.w_hi[:, col:col + m], s.w_lo[:, col:col + m]
                pe.matmul(dst, w_h, hi, start=True, stop=False)
                pe.matmul(dst, w_h, lo, start=False, stop=False)
                return pe.matmul(dst, w_l, hi, start=False, stop=True)

            def down_product(i, g):
                n, j = 2 * i + g // C, g % C
                m, first, last = rows(j), j == 0, j == C - 1
                w_h, w_l = s.w_hi[0:m, DN + j * D:DN + j * D + D], s.w_lo[0:m, DN + j * D:DN + j * D + D]
                hi, lo = hidden_hi[0:m, g % RING, :], hidden_lo[0:m, g % RING, :]
                pe.wait_ge(hidden_lo_ready, STEP * i + g + 1)
                if j == 0:
                    if counted(n):
                        pe.wait_ge(yT_ready, n)
                pe.matmul(out_sum[:, :], w_h, hi, start=first, stop=False)
                pe.matmul(out_sum[:, :], w_h, lo, start=False, stop=False)
                pe.matmul(out_sum[:, :], w_l, hi, start=False, stop=last).then_inc(down_mm, 1)

            turn_z(0)
            logits(0, 0)
            turn_weights(0)

            def body(i, has_previous, has_next):
                for g in range(STEP):
                    u, j = g // C, g % C
                    n, m = 2 * i + u, rows(j)
                    hi, lo = zT_hi[:, u, :], zT_lo[:, u, :]
                    prev, nxt = has_previous or u == 1, has_next or u == 0
                    if counted(STEP * i + g - 1):
                        pe.wait_ge(gated_ready, STEP * i + g - 1)
                    product(gate[0:m, g % 2, :], hi, lo, G + j * P, m).then_inc(gate_mm, 1)
                    if counted(STEP * i + g - 1):
                        pe.wait_ge(raised_ready, STEP * i + g - 1)
                    product(up[0:m, g % 2, :], hi, lo, U + j * P, m).then_inc(up_mm, 1)
                    if j < 16:
                        if j == 0:
                            pe.wait_ge(weights_ready, n + 1)
                        if counted(STEP * i + g - 1 if j >= 2 else STEP * i + g - 2):
                            pe.wait_ge(hidden_ready, STEP * i + g - 1 if j >= 2 else STEP * i + g - 2)
                        pe.matmul(spread[:, j % 2, :], pick[:, j, :], weightsT[:, u, :], start=True, stop=True).then_inc(spread_mm, 1)
                    if g >= LAG:
                        down_product(i, g - LAG)
                    elif has_previous:
                        down_product(i - 1, STEP - LAG + g)
                    if j == 0 and nxt:
                        turn_z(n + 1)
                    if j == 3 and nxt:
                        logits(n + 1, 1 - u)
                    if j == 6 and prev:
                        if nxt:
                            pe.wait_ge(scored_ready, n + 2)
                        turn_y(n - 1)
                    if j == 15 and nxt:
                        if prev:
                            if counted(n):
                                pe.wait_ge(x_new, n)
                        turn_weights(n + 1)

            steps(pe, N // 2, body)
            for g in range(STEP - LAG, STEP):
                down_product(N // 2 - 1, g)
            turn_y(N - 1)

        @block.gpsimd
        def _(pool):
            def body(i, has_previous, has_next):
                for g in range(STEP):
                    pool.wait_ge(hidden_hi_ready, STEP * i + g + 1)
                    pool.tensor_tensor(hidden_lo[:, g % RING, :], hidden[:, g % RING, :], hidden_hi[:, g % RING, :].bitcast(F32),
                                       ALU.subtract).then_inc(hidden_lo_ready, 1)

            steps(pool, N // 2, body)

        @block.scalar
        def _(act):
            ln_scalar(act)

            def high_part(n, u):
                act.wait_ge(zT_mm, n + 1)
                act.activation(zT_hi[:, u, :], turned[:, :], ACT.Copy, bias=0.0)
                act.activation(zT[:, u, :], turned[:, :], ACT.Copy, bias=0.0).then_inc(zT_hi_ready, 1)

            def score(n):
                act.wait_ge(logits_mm, n + 1)
                act.activation(scored[:, :, :], turned[:, 0:P].rearrange("p (t e) -> p t e", t=4), ACT.Sigmoid,
                               bias=0.0).then_inc(scored_ready, 1)

            def keep_weights(n, u):
                act.wait_ge(weights_mm, n + 1)
                act.activation(weightsT[:, u, :], turned_bf, ACT.Copy, bias=0.0).then_inc(weights_ready, 1)

            def keep_y(n):
                act.wait_ge(down_mm, C * (n + 1))
                act.activation(yT[:, :], out_sum[:, :], ACT.Copy, bias=0.0).then_inc(yT_ready, 1)

            def hidden_high(i, g):
                act.wait_ge(hidden_ready, STEP * i + g + 1)
                if counted(before(i, g, RING)):
                    act.wait_ge(down_mm, before(i, g, RING))
                act.activation(hidden_hi[:, g % RING, :], hidden[:, g % RING, :], ACT.Copy, bias=0.0).then_inc(hidden_hi_ready, 1)

            high_part(0, 0)
            score(0)
            keep_weights(0, 0)

            def body(i, has_previous, has_next):
                for g in range(STEP):
                    u, j = g // C, g % C
                    n, m = 2 * i + u, rows(j)
                    prev, nxt = has_previous or u == 1, has_next or u == 0
                    if j == LAG and prev:
                        keep_y(n - 1)
                    act.wait_ge(gate_mm, STEP * i + g + 1)
                    if counted(STEP * i + g - 1):
                        act.wait_ge(raised_ready, STEP * i + g - 1)
                    act.activation(gated[0:m, g % 2, :], gate[0:m, g % 2, :], ACT.Silu, bias=0.0).then_inc(gated_ready, 1)
                    if g >= 2:
                        hidden_high(i, g - 2)
                    elif has_previous:
                        hidden_high(i - 1, STEP - 2 + g)
                    if j == 1 and nxt:
                        high_part(n + 1, 1 - u)
                    if j == 4 and nxt:
                        score(n + 1)
                    if j == 16 and nxt:
                        keep_weights(n + 1, 1 - u)

            steps(act, N // 2, body)
            hidden_high(N // 2 - 1, STEP - 2)
            hidden_high(N // 2 - 1, STEP - 1)
            keep_y(N - 1)

        @block.vector
        def _(dve):
            dve.wait_ge(loaded, 16 * len(small))
            dve.tensor_copy(pick[:, :, :].rearrange("k j m -> k (j m)"), picks_in)
            dve.tensor_copy(identb[:, :], s.ident[:, :]).then_inc(consts, 1)
            ln_vector(dve)

            def low_part(n, u):
                dve.wait_ge(zT_hi_ready, n + 1)
                dve.tensor_tensor(zT_lo[:, u, :], turned[:, :], zT_hi[:, u, :].bitcast(F32), ALU.subtract).then_inc(zT_ready, 1)

            def score_groups(n):
                dve.wait_ge(scored_ready, n + 1)
                dve.tensor_reduce(groups[:, :, :], scored[:, :, :].rearrange("p t (g e) -> p t g e", e=4), X, ALU.add)
                dve.drain()
                compare_values(dve, s, tmp, groups[:, :, :])

            def mask_scores():
                choose(dve, tmp, 4)
                dve.tensor_tensor(masked[:, :, :].rearrange("p t (g e) -> p (t g) e", e=4),
                                  scored[:, :, :].rearrange("p t (g e) -> p (t g) e", e=4),
                                  tmp.sel[:, :, :].rearrange("p t g -> p (t g)").unsqueeze(2).broadcast_to([P, 32, 4]), ALU.mult)
                dve.drain()

            def take_top8():
                for t in range(4):
                    dve.max(top8[:, t, :], masked[:, t, :])
                dve.drain()
                for t in range(4):
                    dve.match_replace(left[:, t, :], top8[:, t, :], masked[:, t, :], 0.0)
                dve.tensor_reduce(total[:, :], top8[:, :, :], X, ALU.add)
                dve.drain()

            def over_their_sum():
                dve.tensor_tensor(masked[:, :, :], masked[:, :, :], left[:, :, :], ALU.subtract)
                dve.tensor_scalar(total[:, :], total[:, :], 1e-12, None, ALU.max)
                dve.drain()
                dve.reciprocal(total[:, :], total[:, :])
                dve.drain()
                dve.tensor_tensor(masked[:, :, :], masked[:, :, :], total[:, :].unsqueeze(2).broadcast_to([P, 4, 32]), ALU.mult)
                dve.drain()

            def split_weights(n):
                if counted(n):
                    dve.wait_ge(weights_mm, n)
                dve.tensor_copy(parts[:, :, 0, :], masked[:, :, :])
                dve.drain()
                dve.tensor_tensor(masked[:, :, :], masked[:, :, :], parts[:, :, 0, :], ALU.subtract)
                dve.drain()
                dve.tensor_copy(parts[:, :, 1, :], masked[:, :, :])
                dve.drain()
                dve.tensor_tensor(parts[:, :, 2, :], masked[:, :, :], parts[:, :, 1, :], ALU.subtract).then_inc(parts_ready, 1)

            def update(n):
                dve.wait_ge(y_mm, n + 1)
                xt = s.x[:, bass.ds(4 * n, 4), :]
                dve.scalar_tensor_tensor(out=xt, in0=turned[:, :].rearrange("p (t c) -> p t c", t=4),
                                         scalar=s.gates[:, 2:3], in1=xt, op0=ALU.mult, op1=ALU.add).then_inc(x_new, 1)
                dve.drain()
                tile_statistics(dve, s, 4 * n, 4)

            def finish_hidden(i, g):
                u, j = g // C, g % C
                m = rows(j)
                dve.wait_ge(raised_ready, STEP * i + g + 1)
                if counted(before(i, g, RING)):
                    dve.wait_ge(hidden_lo_ready, before(i, g, RING))
                if j < 16:
                    dve.wait_ge(spread_mm, 32 * i + 16 * u + j + 1)
                    dve.tensor_tensor(hidden[:, g % RING, :], spread[:, j % 2, :], raised[:, g % 2, :], ALU.mult).then_inc(hidden_ready, 1)
                else:
                    dve.tensor_copy(hidden[0:m, g % RING, :], raised[0:m, g % 2, :]).then_inc(hidden_ready, 1)

            normalized(dve, s, z, 0, 4).then_inc(z_ready, 1)
            low_part(0, 0)
            score_groups(0)
            count_before(dve, s, tmp)
            mask_scores()
            take_top8()
            over_their_sum()
            split_weights(0)
            dve.wait_ge(zT_mm, 1)
            normalized(dve, s, z, 4, 4).then_inc(z_ready, 1)

            def body(i, has_previous, has_next):
                for g in range(STEP):
                    u, j = g // C, g % C
                    n, m = 2 * i + u, rows(j)
                    prev, nxt = has_previous or u == 1, has_next or u == 0
                    dve.wait_ge(gated_ready, STEP * i + g + 1)
                    dve.wait_ge(up_mm, STEP * i + g + 1)
                    if counted(STEP * i + g - 1):
                        dve.wait_ge(hidden_ready, STEP * i + g - 1)
                    dve.tensor_tensor(raised[0:m, g % 2, :], up[0:m, g % 2, :], gated[0:m, g % 2, :], ALU.mult).then_inc(raised_ready, 1)
                    if g >= 1:
                        finish_hidden(i, g - 1)
                    elif has_previous:
                        finish_hidden(i - 1, STEP - 1)
                    if j == 3 and has_next:
                        dve.wait_ge(zT_mm, n + 2)
                        normalized(dve, s, z, 4 * n + 8, 4).then_inc(z_ready, 1)
                    if j == 7 and prev:
                        update(n - 1)
                    if nxt:
                        if j == 2:
                            low_part(n + 1, 1 - u)
                        if j == 8:
                            score_groups(n + 1)
                        if j == 9:
                            count_before(dve, s, tmp)
                        if j == 10:
                            mask_scores()
                        if j == 12:
                            take_top8()
                        if j == 13:
                            over_their_sum()
                        if j == 14:
                            split_weights(n + 1)

            steps(dve, N // 2, body)
            finish_hidden(N // 2 - 1, STEP - 1)
            update(N - 1)


MASKED = 2.0 ** 100
CHUNKS = "GGGUGUGUGUGUGUUU"
BANKS = [0, 1, 2, 0, 1, 3, 2, 0, 1, 3, 2, 0, 1, 3, 2, 0]


def read_before(bank, position, kind):
    same_bank = [p for p in range(position) if BANKS[p] == bank and CHUNKS[p] == kind]
    return CHUNKS[:same_bank[-1] + 1].count(kind) if same_bank else 0


def attention_1(nc, s, a):
    N = NT // 2
    SCALE = 64.0 ** -0.5
    with ExitStack() as ctx:
        def sb(name, shape, dt=F32):
            return ctx.enter_context(nc.sbuf_tensor("a1_" + name, shape, dt))

        def ps(name, shape, dt=F32):
            return ctx.enter_context(nc.psum_tensor("a1_" + name, shape, dt))

        def sem(name):
            return ctx.enter_context(nc.semaphore("a1_" + name))

        m_hi, m_lo = sb("m_hi", [P, 16, D], F32R), sb("m_lo", [P, 16, D], F32R)
        n_hi = s.w_hi[:, 4352:6400].rearrange("p (h d) -> p h d", d=D)
        n_lo = s.w_lo[:, 4352:6400].rearrange("p (h d) -> p h d", d=D)
        b_out = sb("b_out", [P, 1])
        mask_row = sb("mask_row", [1, B * S], U8)
        mask_add = sb("mask_add", [1, 2, P], BF16)
        ones = sb("ones", [1, P], BF16)
        z = sb("z", [P, 2, D])
        zT_hi, zT_lo = sb("zT_hi", [P, 2 * P], F32R), sb("zT_lo", [P, 2 * P], F32R)
        ctxT, ctx_in = sb("ctxT", [P, 2 * P]), sb("ctx", [P, 2, D])
        c_hi, c_lo = sb("c_hi", [P, 2, 2, D], F32R), sb("c_lo", [P, 2, 2, D], F32R)
        g = sb("g", [P, 16, 2 * P])
        top, den, rden = sb("top", [P, 2, 16]), sb("den", [P, 2, 16]), sb("rden", [P, 2, 16])
        probs = sb("probs", [P, 2, 8 * P])
        pT_hi, pT_lo = sb("pT_hi", [P, 8 * P], F32R), sb("pT_lo", [P, 8 * P], F32R)
        u_hi, u_lo = sb("u_hi", [P, 16, 2 * P], F32R), sb("u_lo", [P, 16, 2 * P], F32R)
        yT = sb("yT", [P, 2 * P])

        scores = ps("scores", [P, 2, 8, 2, S])
        work = ps("work", [P, 3, 512])
        late = ps("late", [P, 512])
        out_sum, turned = late[:, 0:2 * P], late[:, 2 * P:4 * P]

        loaded, prepared = sem("loaded"), sem("prepared")
        w_mm, w_hi_ready, w_ready = sem("w_mm"), sem("w_hi_ready"), sem("w_ready")
        ctxT_in, ctx_loaded, c_hi_ready, c_ready = sem("ctxT_in"), sem("ctx_loaded"), sem("c_hi_ready"), sem("c_ready")
        z_ready, zT_mm, zT_hi_ready, zT_ready = sem("z_ready"), sem("zT_mm"), sem("zT_hi_ready"), sem("zT_ready")
        g_mm, g_ready, mask_ready = sem("g_mm"), sem("g_ready"), sem("mask_ready")
        scores_mm, shifted, exped, den_ready, normed = (sem("scores_mm"), sem("shifted"), sem("exped"),
                                                        sem("den_ready"), sem("normed"))
        pT_mm, pT_hi_ready, pT_ready = sem("pT_mm"), sem("pT_hi_ready"), sem("pT_ready")
        u_mm, u_hi_ready, u_ready = sem("u_mm"), sem("u_hi_ready"), sem("u_ready")
        out_mm, yT_ready, y_mm, x_new = sem("out_mm"), sem("yT_ready"), sem("y_mm"), sem("x_new")
        w_loaded, w_split = [sem("w_loaded_even"), sem("w_loaded_odd")], sem("w_split")
        ln_vector, ln_scalar = layernorm_statistics(s, sem)

        with nc.Block() as block:
            wq, wk = [g[0:64, 8 * k:8 * k + 8, :].rearrange("p a (h d) -> p (a h) d", h=2) for k in range(2)]
            wv = probs[0:64, :, :].rearrange("p t (h d) -> p (t h) d", h=8)
            wo = s.staging[0:64, 0:16 * D].rearrange("p (h d) -> p h d", d=D)
            small = [(wq, a["wq1"]), (wk, a["wk1"]), (wv, a["wv1"]), (wo, a["wo1"]),
                     (b_out[:, :], a["bo1"]), (mask_row[:, :], a["mask"])]

            @block.sync
            def _(sp):
                for dst, src in small:
                    sp.dma_start(dst, src).then_inc(loaded, 16)
                sp.wait_ge(loaded, 16 * len(small))

            @block.tensor
            def _(pe):
                pe.wait_ge(loaded, 16 * len(small))
                for k in range(8):
                    if counted(k - 2):
                        pe.wait_ge(w_ready, k - 2)
                    left, right = (wq, wk) if k < 4 else (wv, wo)
                    for q in range(4):
                        h = 4 * (k % 4) + q
                        last = pe.matmul(work[:, k % 3, q * D:(q + 1) * D], left[:, h, :], right[:, h, :], start=True, stop=True)
                    last.then_inc(w_mm, 1)

            def weight_chunk(k):
                heads = slice(4 * (k % 4), 4 * (k % 4) + 4)
                hi, lo = (m_hi, m_lo) if k < 4 else (n_hi, n_lo)
                return work[:, k % 3, :].rearrange("p (h d) -> p h d", d=D), hi[:, heads, :], lo[:, heads, :]

            @block.vector
            def _(dve):
                dve.memset(ones[:, :], 1.0)
                dve.memset(c_hi[:, :, :, :].bitcast(F32), 0.0)
                dve.memset(c_lo[:, :, :, :].bitcast(F32), 0.0)
                ln_vector(dve)
                for k in range(8):
                    product, hi, lo = weight_chunk(k)
                    dve.wait_ge(w_hi_ready, k + 1)
                    dve.tensor_tensor(lo, product, hi.bitcast(F32), ALU.subtract).then_inc(w_ready, 1)

            @block.scalar
            def _(act):
                ln_scalar(act)
                for k in range(8):
                    product, hi, lo = weight_chunk(k)
                    act.wait_ge(w_mm, k + 1)
                    act.activation(hi, product, ACT.Copy, bias=0.0).then_inc(w_hi_ready, 1)

        block = ctx.enter_context(nc.Block())

        def bank_of(k):
            return work[:, k, :] if k < 3 else scores[:, 0, 0:4, :, :].rearrange("p r b j -> p (r b j)")

        def u_chunk(n):
            position = [p for p in range(16) if CHUNKS[p] == "U"][n]
            t, half, b = n // 4, n // 2 % 2, n % 2
            return BANKS[position], slice(8 * half, 8 * half + 8), slice(t * P + b * S, t * P + b * S + S)

        @block.sync
        def _(sp):
            def load(k):
                if counted(2 * k):
                    sp.wait_ge(scores_mm, 2 * k)
                sp.dma_start(ctxT[:, :], a["ctxT"][:, bass.ds(k * (2 * P), 2 * P)]).then_inc(ctxT_in, 16)
                if counted(k):
                    sp.wait_ge(c_ready, k)
                sp.dma_start(ctx_in[:, :, :], a["ctx"][:, bass.ds(2 * k, 2), :]).then_inc(ctx_loaded, 16)

            load(0)
            with sp.Fori(1, N) as k:
                load(k)

        @block.gpsimd
        def _(pool):
            def normalize(i):
                for t in range(2):
                    pool.wait_ge(den_ready, 2 * i + t + 1)
                    for half in range(2):
                        p = probs[:, t, half * 512:half * 512 + 512].rearrange("p (g j) -> p g j", j=S)
                        r = rden[:, t, 8 * half:8 * half + 8].unsqueeze(2).broadcast_to([P, 8, S])
                        pool.tensor_tensor(p, p, r, ALU.mult).then_inc(normed, 1)

            split_on_pool(pool, a["w_moe1"], 4, 1024, s.w_hi, s.w_lo, s.staging, w_loaded, w_split, normalize)
            with pool.Fori(4, N) as i:
                normalize(i)

        @block.vector
        def _(dve):
            def mask(k):
                m = mask_row[:, bass.ds(k * 256, 256)].rearrange("p (t c) -> p t c", t=2)
                return dve.tensor_scalar(mask_add[:, :, :], m, -1.0, MASKED, ALU.add, ALU.mult).then_inc(mask_ready, 1)

            def low_part(k):
                dve.wait_ge(zT_hi_ready, k + 1)
                dve.tensor_tensor(zT_lo[:, :], turned, zT_hi[:, :].bitcast(F32), ALU.subtract).then_inc(zT_ready, 1)

            def context_low(k):
                dve.wait_ge(c_hi_ready, k + 1)
                for b in range(2):
                    rows = slice(64 * b, 64 * b + 64)
                    last = dve.tensor_tensor(c_lo[rows, :, b, :], ctx_in[rows, :, :], c_hi[rows, :, b, :].bitcast(F32), ALU.subtract)
                last.then_inc(c_ready, 1)

            def update(k):
                dve.wait_ge(y_mm, k + 1)
                xt = s.x[:, bass.ds(2 * k, 2), :]
                dve.scalar_tensor_tensor(out=xt, in0=out_sum.rearrange("p (t c) -> p t c", t=2),
                                         scalar=s.gates[:, 1:2], in1=xt, op0=ALU.mult, op1=ALU.add).then_inc(x_new, 1)
                dve.drain()
                tile_statistics(dve, s, 2 * k, 2)

            mask(0)
            normalized(dve, s, z, 0, 2).then_inc(z_ready, 1)
            low_part(0)

            def softmax_shift(i, t):
                if counted(4 * i - 2 + 2 * t):
                    dve.wait_ge(pT_mm, 4 * i - 2 + 2 * t)
                dve.wait_ge(scores_mm, 2 * i + t + 1)
                softmax_shifted(dve, probs[:, t, :], scores[:, t, :, :, :].rearrange("p r b j -> p (r b j)"),
                                top[:, t, :]).then_inc(shifted, 1)

            def denominators(i, t):
                dve.wait_ge(exped, 2 * i + t + 1)
                dve.tensor_reduce(den[:, t, :], probs[:, t, :].rearrange("p (g j) -> p g j", j=S), X, ALU.add)
                dve.drain()
                dve.reciprocal(rden[:, t, :], den[:, t, :]).then_inc(den_ready, 1)

            def turned_low(i, t, half):
                c = slice(half * 512, half * 512 + 512)
                dve.wait_ge(pT_hi_ready, 4 * i + 2 * t + half + 1)
                dve.tensor_tensor(pT_lo[:, c], scores[:, t, 4 * half:4 * half + 4, :, :].rearrange("p r b j -> p (r b j)"),
                                  pT_hi[:, c].bitcast(F32), ALU.subtract).then_inc(pT_ready, 1)

            def u_low(i, n):
                bank, heads, tokens = u_chunk(n)
                dve.wait_ge(u_hi_ready, 8 * i + n + 1)
                dve.tensor_tensor(u_lo[:, heads, tokens], bank_of(bank).rearrange("p (h i) -> p h i", i=S),
                                  u_hi[:, heads, tokens].bitcast(F32), ALU.subtract).then_inc(u_ready, 1)

            def body(i, has_previous, has_next):
                if has_next:
                    dve.wait_ge(zT_mm, i + 1)
                    normalized(dve, s, z, 2 * i + 2, 2).then_inc(z_ready, 1)
                softmax_shift(i, 0)
                if has_next:
                    low_part(i + 1)
                softmax_shift(i, 1)
                denominators(i, 0)
                denominators(i, 1)
                context_low(i)
                if has_next:
                    mask(i + 1)
                turned_low(i, 0, 0)
                turned_low(i, 0, 1)
                if has_previous:
                    update(i - 1)
                for n in range(8):
                    u_low(i, n)
                    if n in (1, 3):
                        turned_low(i, 1, n // 2)

            steps(dve, N, body)
            update(N - 1)

        @block.scalar
        def _(act):
            def high_part(k):
                act.wait_ge(zT_mm, k + 1)
                if counted(8 * k):
                    act.wait_ge(g_mm, 8 * k)
                act.activation(zT_hi[:, :], turned, ACT.Copy, bias=0.0).then_inc(zT_hi_ready, 1)

            def keep_g(k, c, bank):
                act.wait_ge(g_mm, 8 * k + c + 1)
                act.activation(g[:, 2 * c:2 * c + 2, :], bank_of(bank).rearrange("p (h i) -> p h i", h=2), ACT.Copy,
                               bias=0.0).then_inc(g_ready, 1)

            def u_high(i, n):
                bank, heads, tokens = u_chunk(n)
                act.wait_ge(u_mm, 8 * i + n + 1)
                act.activation(u_hi[:, heads, tokens], bank_of(bank).rearrange("p (h i) -> p h i", i=S), ACT.Copy,
                               bias=0.0).then_inc(u_hi_ready, 1)

            def turned_high(i, t, half):
                act.wait_ge(pT_mm, 4 * i + 2 * t + half + 1)
                if counted(8 * i + 2 * half + 4 * t - 2):
                    act.wait_ge(u_mm, 8 * i + 2 * half + 4 * t - 2)
                act.activation(pT_hi[:, half * 512:half * 512 + 512],
                               scores[:, t, 4 * half:4 * half + 4, :, :].rearrange("p r b j -> p (r b j)"), ACT.Copy,
                               bias=0.0).then_inc(pT_hi_ready, 1)

            def output_turned(k):
                act.wait_ge(out_mm, k + 1)
                act.activation(yT[:, :], out_sum, ACT.Identity, bias=b_out[:, 0:1]).then_inc(yT_ready, 1)

            def context_high(k):
                act.wait_ge(ctx_loaded, 16 * (k + 1))
                if counted(8 * k):
                    act.wait_ge(u_mm, 8 * k)
                for b in range(2):
                    rows = slice(64 * b, 64 * b + 64)
                    last = act.activation(c_hi[rows, :, b, :], ctx_in[rows, :, :], ACT.Copy, bias=0.0)
                last.then_inc(c_hi_ready, 1)

            high_part(0)
            for c in range(8):
                keep_g(0, c, c % 3)

            def body(i, has_previous, has_next):
                context_high(i)
                if has_next:
                    high_part(i + 1)
                for t in range(2):
                    act.wait_ge(shifted, 2 * i + t + 1)
                    act.activation(probs[:, t, :], probs[:, t, :], ACT.Exp, bias=0.0, scale=SCALE).then_inc(exped, 1)
                if has_previous:
                    output_turned(i - 1)
                turned_high(i, 0, 0)
                turned_high(i, 0, 1)
                for position, kind in enumerate(CHUNKS):
                    c = CHUNKS[:position].count(kind)
                    if kind == "U":
                        u_high(i, c)
                        if c in (1, 3):
                            turned_high(i, 1, c // 2)
                    elif has_next:
                        keep_g(i + 1, c, BANKS[position])

            steps(act, N, body)
            output_turned(N - 1)

        @block.tensor
        def _(pe):
            def turn_z(k):
                pe.wait_ge(z_ready, k + 1)
                for t in range(2):
                    last = pe.transpose(turned[:, t * P:(t + 1) * P], z[:, t, :], s.ident[:, :])
                last.then_inc(zT_mm, 1)

            def make_g(c, bank):
                for q in range(2):
                    h = 2 * c + q
                    dst = bank_of(bank)[:, q * 256:q * 256 + 256]
                    pe.matmul(dst, m_hi[:, h, :], zT_hi[:, :], start=True, stop=False)
                    pe.matmul(dst, m_hi[:, h, :], zT_lo[:, :], start=False, stop=False)
                    last = pe.matmul(dst, m_lo[:, h, :], zT_hi[:, :], start=False, stop=True)
                last.then_inc(g_mm, 1)

            def make_u(n, bank):
                t, half, b = n // 4, n // 2 % 2, n % 2
                c = slice(half * 512, half * 512 + 512)
                pe.matmul(bank_of(bank), c_hi[:, t, b, :], pT_hi[:, c], start=True, stop=False)
                pe.matmul(bank_of(bank), c_hi[:, t, b, :], pT_lo[:, c], start=False, stop=False)
                pe.matmul(bank_of(bank), c_lo[:, t, b, :], pT_hi[:, c], start=False, stop=True).then_inc(u_mm, 1)

            def score(i, t):
                if counted(4 * i - 2 + 2 * t):
                    pe.wait_ge(pT_ready, 4 * i - 2 + 2 * t)
                if t == 0:
                    if counted(8 * i - 8 + read_before(3, len(CHUNKS), "U")):
                        pe.wait_ge(u_ready, 8 * i - 8 + read_before(3, len(CHUNKS), "U"))
                for half in range(2):
                    pe.matmul(scores[:, t, 4 * half:4 * half + 4, :, :].rearrange("p r b j -> p r (b j)"), ones[:, :],
                              mask_add[:, t, :].unsqueeze(1).broadcast_to([1, 4, P]), start=True, stop=False,
                              skip_group_check=True)
                    for h in range(8 * half, 8 * half + 8):
                        for b in range(2):
                            at = t * P + b * S
                            rows = slice(64 * (h % 2), 64 * (h % 2) + 64)
                            last = pe.matmul(scores[rows, t, h // 2, b, :], g[:, h, at:at + S], ctxT[:, at:at + S],
                                             start=False, stop=True, skip_group_check=True)
                last.then_inc(scores_mm, 1)

            def turn_probs(i, t):
                for half in range(2):
                    pe.wait_ge(normed, 4 * i + 2 * t + half + 1)
                    for pr in range(4 * half, 4 * half + 4):
                        last = pe.transpose(scores[:, t, pr, :, :].rearrange("p b j -> p (b j)"), probs[:, t, pr * P:(pr + 1) * P],
                                            s.ident[:, :])
                    last.then_inc(pT_mm, 1)

            def output(k):
                pe.wait_ge(u_ready, 8 * k + 8)
                for h in range(16):
                    pe.matmul(out_sum, n_hi[:, h, :], u_hi[:, h, :], start=(h == 0), stop=False)
                    pe.matmul(out_sum, n_hi[:, h, :], u_lo[:, h, :], start=False, stop=False)
                    last = pe.matmul(out_sum, n_lo[:, h, :], u_hi[:, h, :], start=False, stop=(h == 15))
                last.then_inc(out_mm, 1)

            def turn_y(k):
                pe.wait_ge(yT_ready, k + 1)
                for t in range(2):
                    last = pe.transpose(out_sum[:, t * P:(t + 1) * P], yT[:, t * P:(t + 1) * P], s.ident[:, :])
                last.then_inc(y_mm, 1)

            turn_z(0)
            pe.wait_ge(zT_ready, 1)
            for c in range(8):
                if counted(c - 2):
                    pe.wait_ge(g_ready, c - 2)
                make_g(c, c % 3)

            def body(i, has_previous, has_next):
                pe.wait_ge(ctxT_in, 16 * (i + 1))
                pe.wait_ge(mask_ready, i + 1)
                pe.wait_ge(g_ready, 8 * i + 8)
                score(i, 0)
                if has_next:
                    if counted(i - 1):
                        pe.wait_ge(x_new, i - 1)
                    turn_z(i + 1)
                score(i, 1)
                if has_next:
                    pe.wait_ge(zT_ready, i + 2)
                if has_previous:
                    output(i - 1)
                turn_probs(i, 0)
                for position, kind in enumerate(CHUNKS):
                    c = CHUNKS[:position].count(kind)
                    bank = BANKS[position]
                    g_read, u_read = read_before(bank, position, "G"), read_before(bank, position, "U")
                    if position == 2:
                        if has_previous:
                            turn_y(i - 1)
                        turn_probs(i, 1)
                    if has_next and g_read:
                        pe.wait_ge(g_ready, 8 * i + 8 + g_read)
                    if u_read:
                        pe.wait_ge(u_ready, 8 * i + u_read)
                    if kind == "U":
                        if c == 0:
                            pe.wait_ge(c_ready, i + 1)
                        pe.wait_ge(pT_ready, 4 * i + c // 2 + 1)
                        make_u(c, bank)
                    elif has_next:
                        make_g(c, bank)

            steps(pe, N, body)
            pe.wait_ge(x_new, N - 1)
            output(N - 1)
            turn_y(N - 1)


def experts_1(nc, s, a):
    N, C = NT // 4, 32
    LAG, RING = 6, 8

    with ExitStack() as ctx:
        def sb(name, shape, dt=F32):
            return ctx.enter_context(nc.sbuf_tensor("e1_" + name, shape, dt))

        def ps(name, shape, dt=F32):
            return ctx.enter_context(nc.psum_tensor("e1_" + name, shape, dt))

        def sem(name):
            return ctx.enter_context(nc.semaphore("e1_" + name))

        router, b1 = sb("router", [P, 8]), sb("b1", [P, C])
        b2, b2_parts = sb("b2", [24, D]), sb("b2_parts", [24, 3, D], BF16)
        pick, identb = sb("pick", [24, 8, P], BF16), sb("identb", [P, P], BF16)
        z = sb("z", [P, 4, D])
        zT = sb("zT", [P, 2, 512])
        zT_hi, zT_lo = sb("zT_hi", [P, 2, 512], F32R), sb("zT_lo", [P, 2, 512], F32R)
        w2_hi, w2_lo = sb("w2_hi", [P, C * D], F32R), sb("w2_lo", [P, C * D], F32R)
        active, hidden = sb("active", [P, 4, 512]), sb("hidden", [P, 4, 512])
        hidden_hi, hidden_lo = sb("hidden_hi", [P, RING, 512], F32R), sb("hidden_lo", [P, RING, 512], F32R)
        yT = sb("yT", [P, 512])
        weightsT = sb("weightsT", [24, 2, 512], BF16)
        tmp = Shared()
        tmp.larger, tmp.equal = sb("larger", [P, 4, 8, 8]), sb("equal", [P, 4, 8, 8])
        tmp.rank, tmp.sel = sb("rank", [P, 4, 8]), sb("sel", [P, 4, 8])
        logit, shifted = sb("logit", [P, 4, 8]), sb("shifted", [P, 4, 8])
        total, parts = sb("total", [P, 4]), sb("parts", [P, 4, 3, 8], BF16)

        up, spread = ps("up", [P, 4, 512]), ps("spread", [P, 2, 512])
        out_sum, turned = ps("out_sum", [P, 512]), ps("turned", [P, 512])
        turned_bf = turned[0:24, 0:256].bitcast(BF16)

        loaded, consts = sem("loaded"), sem("consts")
        up_mm, active_ready, spread_mm, hidden_ready = sem("up_mm"), sem("active_ready"), sem("spread_mm"), sem("hidden_ready")
        hi_ready, lo_by_pool, lo_by_vector, down_mm = sem("hi_ready"), sem("lo_by_pool"), sem("lo_by_vector"), sem("down_mm")
        yT_ready, y_mm, x_new, stored = sem("yT_ready"), sem("y_mm"), sem("x_new"), sem("stored")
        z_ready, zT_mm, zT_hi_ready, zT_ready = sem("z_ready"), sem("zT_mm"), sem("zT_hi_ready"), sem("zT_ready")
        logits_mm, logits_read, exp_in, exp_out = sem("logits_mm"), sem("logits_read"), sem("exp_in"), sem("exp_out")
        parts_ready, weights_mm, weights_ready = sem("parts_ready"), sem("weights_mm"), sem("weights_ready")
        w_loaded, w_split = [sem("w_loaded_even"), sem("w_loaded_odd")], sem("w_split")
        ln_vector, ln_scalar = layernorm_statistics(s, sem)
        block = ctx.enter_context(nc.Block())

        pick_in = zT[0:24, :, :].rearrange("p u t -> p (u t)")
        small = [(router[:, :], a["router1"]), (b1[:, :], a["b1"]), (b2[:, :], a["b2"]), (pick_in, a["pick1"])]

        @block.sync
        def _(sp):
            for dst, src in small:
                sp.dma_start(dst, src).then_inc(loaded, 16)
            with sp.Fori(0, N) as n:
                sp.wait_ge(x_new, n + 1)
                sp.dma_start(s.out[:, bass.ds(4 * n, 4), :], s.x[:, bass.ds(4 * n, 4), :]).then_inc(stored, 16)
            sp.wait_ge(stored, 16 * N)

        @block.gpsimd
        def _(pool):
            def body(i, has_previous, has_next):
                for u in range(2):
                    n = 2 * i + u
                    for q in range(C):
                        e, r = q // 4, q % 4
                        if r < 3:
                            pool.wait_ge(hi_ready, 24 * n + 3 * e + r + 1)
                            pool.tensor_tensor(hidden_lo[:, q % RING, :], hidden[:, r, :], hidden_hi[:, q % RING, :].bitcast(F32),
                                               ALU.subtract).then_inc(lo_by_pool, 1)

            split_on_pool(pool, a["w_moe1"][:, C * P:2 * C * P], 4, 1024, w2_hi, w2_lo, s.staging, w_loaded, w_split)
            steps(pool, N // 2, body)

        @block.tensor
        def _(pe):
            pe.wait_ge(loaded, 16 * len(small))
            pe.wait_ge(consts, 1)

            def turn_z(n):
                pe.wait_ge(z_ready, n + 1)
                if counted(n):
                    pe.wait_ge(weights_ready, n)
                for t in range(4):
                    last = pe.transpose(turned[:, t * P:(t + 1) * P], z[:, t, :], s.ident[:, :])
                last.then_inc(zT_mm, 1)

            def logits(n, u):
                pe.wait_ge(zT_ready, n + 1)
                for t in range(4):
                    last = pe.matmul(turned[:, 8 * t:8 * t + 8], zT[:, u, t * P:(t + 1) * P], router[:, :], start=True, stop=True)
                last.then_inc(logits_mm, 1)

            def turn_weights(n):
                pe.wait_ge(parts_ready, n + 1)
                for t in range(4):
                    last = pe.transpose(turned_bf[:, t * P:(t + 1) * P], parts[:, t, :, :].rearrange("p c e -> p (c e)"), identb[:, :])
                last.then_inc(weights_mm, 1)

            def turn_y(n):
                pe.wait_ge(yT_ready, n + 1)
                for t in range(4):
                    last = pe.transpose(turned[:, t * P:(t + 1) * P], yT[:, t * P:(t + 1) * P], s.ident[:, :])
                last.then_inc(y_mm, 1)

            def down_product(n, u, q):
                e, r = q // 4, q % 4
                w = slice(q * D, (q + 1) * D)
                hi, lo = hidden_hi[:, q % RING, :], hidden_lo[:, q % RING, :]
                if q == 0:
                    if counted(n):
                        pe.wait_ge(yT_ready, n)
                    for k in range(3):
                        pe.matmul(out_sum[:, :], b2_parts[:, k, :], weightsT[:, u, :], start=(k == 0), stop=False)
                if r < 3:
                    pe.wait_ge(lo_by_pool, 24 * n + 3 * e + r + 1)
                else:
                    pe.wait_ge(lo_by_vector, 8 * n + e + 1)
                pe.matmul(out_sum[:, :], w2_hi[:, w], hi, start=False, stop=False)
                pe.matmul(out_sum[:, :], w2_hi[:, w], lo, start=False, stop=False)
                pe.matmul(out_sum[:, :], w2_lo[:, w], hi, start=False, stop=(q == C - 1)).then_inc(down_mm, 1)

            turn_z(0)
            logits(0, 0)
            turn_weights(0)

            def body(i, has_previous, has_next):
                for u in range(2):
                    n = 2 * i + u
                    prev, nxt = has_previous or u == 1, has_next or u == 0
                    for q in range(C):
                        w = slice(q * P, (q + 1) * P)
                        if q % 4 == 0:
                            if q == 0:
                                pe.wait_ge(weights_ready, n + 1)
                            if counted(C * n + q - 4):
                                pe.wait_ge(hidden_ready, C * n + q - 4)
                            pe.matmul(spread[:, q // 4 % 2, :], pick[:, q // 4, :], weightsT[:, u, :], start=True,
                                      stop=True).then_inc(spread_mm, 1)
                        if counted(C * n + q - 3):
                            pe.wait_ge(active_ready, C * n + q - 3)
                        pe.matmul(up[:, q % 4, :], s.w_hi[:, w], zT_hi[:, u, :], start=True, stop=False)
                        pe.matmul(up[:, q % 4, :], s.w_hi[:, w], zT_lo[:, u, :], start=False, stop=False)
                        pe.matmul(up[:, q % 4, :], s.w_lo[:, w], zT_hi[:, u, :], start=False, stop=True).then_inc(up_mm, 1)
                        if q == LAG and not prev:
                            pe.wait_ge(w_split, 4)
                        if q >= LAG:
                            down_product(n, u, q - LAG)
                        elif prev:
                            down_product(n - 1, 1 - u, C - LAG + q)
                        if q == 0 and nxt:
                            turn_z(n + 1)
                        if q == 5 and nxt:
                            logits(n + 1, 1 - u)
                        if q == 10 and prev:
                            if nxt:
                                pe.wait_ge(logits_read, n + 2)
                            turn_y(n - 1)
                        if q == 23 and nxt:
                            if prev:
                                if counted(n):
                                    pe.wait_ge(x_new, n)
                            turn_weights(n + 1)

            steps(pe, N // 2, body)
            for q in range(C - LAG, C):
                down_product(N - 1, 1, q)
            turn_y(N - 1)

        @block.scalar
        def _(act):
            ln_scalar(act)

            def high_part(n, u):
                act.wait_ge(zT_mm, n + 1)
                act.activation(zT_hi[:, u, :], turned[:, :], ACT.Copy, bias=0.0)
                act.activation(zT[:, u, :], turned[:, :], ACT.Copy, bias=0.0).then_inc(zT_hi_ready, 1)

            def exponential(n):
                act.wait_ge(exp_in, n + 1)
                act.activation(shifted[:, :, :], shifted[:, :, :], ACT.Exp, bias=0.0).then_inc(exp_out, 1)

            def keep_weights(n, u):
                act.wait_ge(weights_mm, n + 1)
                act.activation(weightsT[:, u, :], turned_bf, ACT.Copy, bias=0.0).then_inc(weights_ready, 1)

            def keep_y(n):
                act.wait_ge(down_mm, C * (n + 1))
                act.activation(yT[:, :], out_sum[:, :], ACT.Copy, bias=0.0).then_inc(yT_ready, 1)

            def hidden_high(n, q):
                if q % 4 < 3:
                    act.wait_ge(hidden_ready, C * n + q + 1)
                    if counted(C * n + q - 7):
                        act.wait_ge(down_mm, C * n + q - 7)
                    act.activation(hidden_hi[:, q % RING, :], hidden[:, q % 4, :], ACT.Copy, bias=0.0).then_inc(hi_ready, 1)

            act.wait_ge(consts, 1)
            high_part(0, 0)
            exponential(0)
            keep_weights(0, 0)

            def body(i, has_previous, has_next):
                for u in range(2):
                    n = 2 * i + u
                    prev, nxt = has_previous or u == 1, has_next or u == 0
                    for q in range(C):
                        if q == LAG and prev:
                            keep_y(n - 1)
                        act.wait_ge(up_mm, C * n + q + 1)
                        if counted(C * n + q - 3):
                            act.wait_ge(hidden_ready, C * n + q - 3)
                        act.activation(active[:, q % 4, :], up[:, q % 4, :], ACT.Gelu, bias=b1[:, q:q + 1]).then_inc(active_ready, 1)
                        if q >= 2:
                            hidden_high(n, q - 2)
                        elif prev:
                            hidden_high(n - 1, C - 2 + q)
                        if q == 2 and nxt:
                            high_part(n + 1, 1 - u)
                        if q == 13 and nxt:
                            exponential(n + 1)
                        if q == 25 and nxt:
                            keep_weights(n + 1, 1 - u)

            steps(act, N // 2, body)
            hidden_high(N - 1, C - 2)
            keep_y(N - 1)

        @block.vector
        def _(dve):
            dve.wait_ge(loaded, 16 * len(small))
            dve.tensor_copy(pick[:, :, :].rearrange("k e m -> k (e m)"), pick_in)
            dve.tensor_copy(identb[:, :], s.ident[:, :])
            for k in range(3):
                last = dve.tensor_copy(b2_parts[:, k, :], b2[:, :])
                if k == 2:
                    last.then_inc(consts, 1)
                dve.drain()
                if k < 2:
                    dve.tensor_tensor(b2[:, :], b2[:, :], b2_parts[:, k, :], ALU.subtract)
                    dve.drain()
            ln_vector(dve)

            def low_part(n, u):
                dve.wait_ge(zT_hi_ready, n + 1)
                dve.tensor_tensor(zT_lo[:, u, :], turned[:, :], zT_hi[:, u, :].bitcast(F32), ALU.subtract).then_inc(zT_ready, 1)

            def compare_logits(n):
                dve.wait_ge(logits_mm, n + 1)
                dve.tensor_copy(logit[:, :, :], turned[:, 0:32].rearrange("p (t e) -> p t e", t=4)).then_inc(logits_read, 1)
                dve.drain()
                compare_values(dve, s, tmp, logit[:, :, :])

            def choose_two(n):
                dve.tensor_reduce(total[:, :], logit[:, :, :], X, ALU.max)
                choose(dve, tmp, 2)
                dve.tensor_tensor(shifted[:, :, :], logit[:, :, :], total[:, :].unsqueeze(2).broadcast_to([P, 4, 8]),
                                  ALU.subtract).then_inc(exp_in, 1)

            def over_their_sum(n):
                dve.wait_ge(exp_out, n + 1)
                dve.tensor_tensor(shifted[:, :, :], shifted[:, :, :], tmp.sel[:, :, :], ALU.mult)
                dve.drain()
                dve.tensor_reduce(total[:, :], shifted[:, :, :], X, ALU.add)
                dve.drain()
                dve.reciprocal(total[:, :], total[:, :])
                dve.drain()
                dve.tensor_tensor(shifted[:, :, :], shifted[:, :, :], total[:, :].unsqueeze(2).broadcast_to([P, 4, 8]), ALU.mult)
                dve.drain()

            def split_weights(n):
                if counted(n):
                    dve.wait_ge(weights_mm, n)
                dve.tensor_copy(parts[:, :, 0, :], shifted[:, :, :])
                dve.drain()
                dve.tensor_tensor(shifted[:, :, :], shifted[:, :, :], parts[:, :, 0, :], ALU.subtract)
                dve.drain()
                dve.tensor_copy(parts[:, :, 1, :], shifted[:, :, :])
                dve.drain()
                dve.tensor_tensor(parts[:, :, 2, :], shifted[:, :, :], parts[:, :, 1, :], ALU.subtract).then_inc(parts_ready, 1)

            def update(n):
                dve.wait_ge(y_mm, n + 1)
                xt = s.x[:, bass.ds(4 * n, 4), :]
                dve.scalar_tensor_tensor(out=xt, in0=turned[:, :].rearrange("p (t c) -> p t c", t=4),
                                         scalar=s.gates[:, 3:4], in1=xt, op0=ALU.mult, op1=ALU.add).then_inc(x_new, 1)

            def finish_hidden(n, q):
                e, r = q // 4, q % 4
                dve.wait_ge(active_ready, C * n + q + 1)
                dve.wait_ge(spread_mm, 8 * n + e + 1)
                if r < 3:
                    if counted(24 * n + 3 * e + r - 2):
                        dve.wait_ge(lo_by_pool, 24 * n + 3 * e + r - 2)
                else:
                    if counted(C * n + q - 7):
                        dve.wait_ge(down_mm, C * n + q - 7)
                dve.tensor_tensor(hidden[:, r, :], spread[:, e % 2, :], active[:, r, :], ALU.mult).then_inc(hidden_ready, 1)
                if r == 3:
                    dve.drain()
                    dve.tensor_copy(hidden_hi[:, q % RING, :], hidden[:, r, :])
                    dve.drain()
                    dve.tensor_tensor(hidden_lo[:, q % RING, :], hidden[:, r, :], hidden_hi[:, q % RING, :].bitcast(F32),
                                      ALU.subtract).then_inc(lo_by_vector, 1)
                    dve.drain()

            normalized(dve, s, z, 0, 4).then_inc(z_ready, 1)
            low_part(0, 0)
            compare_logits(0)
            count_before(dve, s, tmp)
            choose_two(0)
            over_their_sum(0)
            split_weights(0)
            dve.wait_ge(zT_mm, 1)
            normalized(dve, s, z, 4, 4).then_inc(z_ready, 1)

            def body(i, has_previous, has_next):
                for u in range(2):
                    n = 2 * i + u
                    prev, nxt = has_previous or u == 1, has_next or u == 0
                    for q in range(C):
                        finish_hidden(n, q)
                        if q == 5 and has_next:
                            dve.wait_ge(zT_mm, n + 2)
                            normalized(dve, s, z, 4 * n + 8, 4).then_inc(z_ready, 1)
                        if q == 12 and prev:
                            update(n - 1)
                        if nxt:
                            if q == 2:
                                low_part(n + 1, 1 - u)
                            if q == 6:
                                compare_logits(n + 1)
                            if q == 8:
                                count_before(dve, s, tmp)
                            if q == 9:
                                choose_two(n + 1)
                            if q == 17:
                                over_their_sum(n + 1)
                            if q == 20:
                                split_weights(n + 1)

            steps(dve, N // 2, body)
            update(N - 1)


def build(nc, a, out):
    s = Shared()
    s.out = out
    with ExitStack() as ctx:
        def sb(name, shape, dt=F32):
            return ctx.enter_context(nc.sbuf_tensor(name, shape, dt))

        s.x = sb("x_sb", [P, NT, D])
        s.ident, s.gates, s.tri = sb("ident_sb", [P, P]), sb("gates_sb", [P, 4]), sb("tri_sb", [P, 8, 8])
        s.stats, s.mean, s.var = sb("ln_stats", [P, NT, 6]), sb("ln_mean", [P, NT]), sb("ln_var", [P, NT])
        s.root, s.rstd = sb("ln_root", [P, NT]), sb("ln_rstd", [P, NT])
        s.w_hi, s.w_lo = sb("w_hi", [P, 6400], F32R), sb("w_lo", [P, 6400], F32R)
        s.staging = sb("staging", [P, 2 * 1280])
        setup(nc, s, a)
        for stage in STEPS:
            stage(nc, s, a)


class Shared:
    pass


STEPS = [attention_0, experts_0, attention_1, experts_1]


def laid_out(inputs):
    v = {k: np.asarray(x) for k, x in inputs.items()}
    c = np.ascontiguousarray
    E0, I0 = 32, 64
    E1, F1 = 8, 512
    tokens = lambda t: c(t.reshape(NT, P, D).transpose(1, 0, 2))
    wkv = v["L1_xattn_Wkv"]
    heads = lambda w: c(w.reshape(16, 64, D).transpose(1, 0, 2))
    down = v["L0_ffn_expert_down"].transpose(0, 2, 1).reshape(16, P, D).transpose(1, 0, 2).reshape(P, 16 * D)
    shared_down = np.zeros((P, D), np.float32)
    shared_down[0:I0] = v["L0_ffn_shared_down_w"].T
    pick = np.zeros((3, E0, 16, 2, I0), np.float32)
    for e in range(E0):
        pick[:, e, e // 2, e % 2, :] = 1
    place = np.zeros((4, 2, 2, 8, 2, 2, D), np.float32)
    par_mask = np.zeros((4, 2, 2, 8, 2), np.float32)
    for g in range(4):
        for r in range(4):
            for d in range(8):
                for b in range(2):
                    place[g, b, r % 2, d, b, r // 2, 32 * g + 8 * r + d] = 1
    for par in range(2):
        par_mask[:, :, par, :, par] = 1
    v_order = np.arange(D).reshape(4, 2, 16).transpose(1, 0, 2).reshape(D)
    head_mask = np.zeros((4, 4, 8, 4), np.float32)
    for r in range(4):
        head_mask[:, r, :, r] = 1
    return {
        "x": tokens(v["x"]), "ctx": tokens(v["ctx_1024"]), "ctxT": c(v["ctx_1024"].reshape(B * S, D).T),
        "mask": c(v["mask_BxS2_bf1"]).view(np.uint8).reshape(1, B * S),
        "g_xattn": v["g_xattn"], "g_ffn": v["g_ffn"],
        "wq0T": c(v["L0_xattn_Wq"].T), "wk0T": c(v["L0_xattn_Wk"].T), "wv0T": c(v["L0_xattn_Wv"].T[:, v_order]),
        "bq0": v["L0_xattn_bq"].reshape(D, 1), "bk0": v["L0_xattn_bk"].reshape(D, 1), "bv0": c(v["L0_xattn_bv"][v_order]),
        "router0": c(v["L0_ffn_gate_w"].T),
        "w_moe0": c(np.concatenate([v["L0_ffn_expert_gate"].reshape(E0 * I0, D).T, v["L0_ffn_shared_gate_w"].T,
                                    v["L0_ffn_expert_up"].reshape(E0 * I0, D).T, v["L0_ffn_shared_up_w"].T,
                                    down, shared_down], 1)),
        "wq1": heads(v["L1_xattn_Wq"]), "wk1": heads(wkv[:1024]), "wv1": heads(wkv[1024:]),
        "wo1": heads(v["L1_xattn_Wout"].T), "bo1": v["L1_xattn_b_out"].reshape(D, 1),
        "router1": c(v["L1_ffn_router_w"].T),
        "w_moe1": c(np.concatenate([v["L1_ffn_w1"].reshape(E1 * F1, D).T,
                                    v["L1_ffn_w2"].transpose(0, 2, 1).reshape(32, P, D).transpose(1, 0, 2).reshape(P, 32 * D)], 1)),
        "b1": c(v["L1_ffn_b1"].reshape(32, P).T), "b2": c(np.tile(v["L1_ffn_b2"], (3, 1))),
        "ident": np.eye(P, dtype=np.float32), "head_mask": head_mask.reshape(P, 4), "place": place.reshape(P, 2, 2, D), "par_mask": par_mask.reshape(P, 2),
        "tri": c(np.broadcast_to(np.tril(np.ones((8, 8), np.float32), -1), (P, 8, 8))),
        "pick": c(pick.reshape(96, 16, P)), "pick1": c(np.tile(np.repeat(np.eye(E1, dtype=np.float32), P, 1), (3, 1))),
    }


def kernel(**inputs):
    import concourse.bacc as bacc
    from concourse.bass_utils import run_bass_kernel_spmd

    nc = bacc.Bacc("TRN2", target_bir_lowering=False, num_devices=1)
    arrays = {f"in_{name}": v for name, v in laid_out(inputs).items()}
    a = {name[3:]: nc.dram_tensor(name, v.shape, mybir.dt.from_np(v.dtype), kind="ExternalInput").ap()
         for name, v in arrays.items()}
    out = nc.dram_tensor("out", (P, NT, D), F32, kind="ExternalOutput").ap()
    build(nc, a, out)
    got = run_bass_kernel_spmd(nc, [arrays], core_ids=[0]).results[0]["out"]
    return np.ascontiguousarray(got.reshape(P, NT, D).transpose(1, 0, 2)).reshape(B, S, D)
```
